# Optimizing a Trainium2 kernel written in Bass

```python
import numpy as np
import jax
import jax.numpy as jnp

def _softmax(x, axis=-1):
    return jax.nn.softmax(x, axis=axis)

def _gelu(x):
    return jax.nn.gelu(x, approximate=True)

def _silu(x):
    return jax.nn.silu(x)

def _sigmoid(x):
    return jax.nn.sigmoid(x)

def _layernorm(x, axis=-1, eps=1e-05):
    m = jnp.mean(x, axis=axis, keepdims=True)
    v = jnp.var(x, axis=axis, keepdims=True)
    return (x - m) / jnp.sqrt(v + eps)

def _scatter_add(tgt, idx, src, axis=0):
    return tgt.at[idx].add(src)

def _segment_sum(src, seg, n):
    return jax.ops.segment_sum(src, seg, n)
kernel_name = 'mk_flamingo_gated_d4_seqx_r4_1de105'

def setup_inputs(seed: int=0):
    np.random.seed(seed)
    _w = jnp.asarray

    def _rec_inputs():
        import jax
        import jax.numpy as jnp
        _rk = jax.random.key(seed)
        x = -0.0002928 + 1 * jax.random.normal(jax.random.fold_in(_rk, 1), (16, 128, 256), jnp.float32)
        _lenS = 128 - jax.random.randint(jax.random.fold_in(_rk, 7), (16,), 0, max(1, 128 // 4) + 1, jnp.int32)
        _lenS2 = 128 - jax.random.randint(jax.random.fold_in(_rk, 8), (16,), 0, max(1, 128 // 4) + 1, jnp.int32)
        _ctx_1024P = jax.random.normal(jax.random.fold_in(_rk, 11), (16, 16, 256), jnp.float32)
        _ctx_1024c = jax.random.dirichlet(jax.random.fold_in(_rk, 511), 0.3 * jnp.ones((16,), jnp.float32), (16, 128))
        _ctx_1024t = jnp.einsum('bsk,bkd->bsd', _ctx_1024c, _ctx_1024P)
        _ctx_1024t = _ctx_1024t * jax.lax.rsqrt(jnp.mean(jnp.square(_ctx_1024t)) + 1e-12) * 0.953939
        ctx_1024 = -1.39393e-06 + 0.999914 * (_ctx_1024t + 0.3 * jax.random.normal(jax.random.fold_in(_rk, 611), (16, 128, 256), jnp.float32))
        _validS = jnp.arange(128)[None, :] < _lenS[:, None]
        _validS2 = jnp.arange(128)[None, :] < _lenS2[:, None]
        _causal = jnp.tril(jnp.ones((128, 128), dtype=bool))
        mask_Bx1xSxS2_ff1 = jnp.where(jnp.ones((16, 1, 128, 128), dtype=bool), 1.0, 0.0).astype(jnp.float32)
        _g = jax.random.normal(jax.random.fold_in(_rk, 9001), (2, 4), jnp.float32)
        _g = jnp.sign(_g) * jnp.maximum(jnp.abs(_g), 1.0) + (_g == 0) * 1.0
        g_xattn = _g[0]
        g_ffn = _g[1]
        return (x, ctx_1024, mask_Bx1xSxS2_ff1, g_xattn, g_ffn)
    x, ctx_1024, mask_Bx1xSxS2_ff1, g_xattn, g_ffn = _rec_inputs()

    def _L0_xattn_setup():
        import jax, jax.numpy as jnp
        import numpy as np
        import math
        HIDDEN = 256
        HEADS = 16
        HEAD = HIDDEN // HEADS
        SCALE_BASE = 512.0

        def _gammas(heads):
            return 1.0 - jnp.exp(jnp.linspace(math.log(1.0 / 32.0), math.log(1.0 / 512.0), heads))

        def _xpos(x, downscale):
            S, d = (x.shape[2], x.shape[3])
            half = d // 2
            base_scale = (jnp.arange(0, d, 2, dtype=jnp.float32) + 0.4 * d) / (1.4 * d)
            pos = jnp.arange(S, dtype=jnp.float32)
            scale = base_scale[None, :] ** (pos / SCALE_BASE)[:, None]
            if downscale:
                scale = 1.0 / scale
            inv_freq = 1.0 / 10000.0 ** (jnp.arange(half, dtype=jnp.float32) / half)
            sinusoid = pos[:, None] * inv_freq[None, :]
            sin = jnp.repeat(jnp.sin(sinusoid) * scale, 2, axis=-1)
            cos = jnp.repeat(jnp.cos(sinusoid) * scale, 2, axis=-1)
            x1 = x[..., ::2]
            x2 = x[..., 1::2]
            rot = jnp.stack([-x2, x1], axis=-1).reshape(x.shape)
            return x * cos + rot * sin

        def _decay_mask(S, gammas):
            n = jnp.arange(S)[:, None]
            m = jnp.arange(S)[None, :]
            diff = (n - m).astype(jnp.float32)
            mask = n >= m
            pw = jnp.maximum(diff, 0.0)[None, :, :]
            return jnp.where(mask[None, :, :], gammas[:, None, None] ** pw, 0.0)

        def retention_forward(Q, K, V):
            B, S, _ = Q.shape

            def split(x, hd):
                return x.reshape(B, S, HEADS, hd).transpose(0, 2, 1, 3)
            q = _xpos(split(Q, HEAD), downscale=False)
            k = _xpos(split(K, HEAD), downscale=True)
            v = split(V, HEAD)
            D = _decay_mask(S, _gammas(HEADS).astype(Q.dtype))
            scores = jnp.einsum('bhsd,bhtd->bhst', q, k) * D[None]
            out = jnp.einsum('bhst,bhtd->bhsd', scores, v)
            return out.transpose(0, 2, 1, 3).reshape(B, S, HEADS * HEAD)
        key = jax.random.key(seed)
        kq, kk, kv = jax.random.split(key, 3)
        B, S = (2, 512)
        return {'Q': jax.random.normal(kq, (B, S, HIDDEN), dtype=jnp.float32), 'K': jax.random.normal(kk, (B, S, HIDDEN), dtype=jnp.float32), 'V': jax.random.normal(kv, (B, S, HIDDEN), dtype=jnp.float32)}
    _L0_xattn_all = _L0_xattn_setup()
    _L0_xattn_in = {k: v for k, v in _L0_xattn_all.items() if k in ()}
    del _L0_xattn_all

    def _L0_ffn_setup():
        import jax, jax.numpy as jnp
        import numpy as np
        B, N, DIM = (2, 512, 256)
        HEADS, DIM_HEAD, EXPERTS = (8, 64, 8)
        SCALE = DIM_HEAD ** (-0.5)
        key = jax.random.key(seed)
        ks = jax.random.split(key, 6)
        dim_inner = HEADS * DIM_HEAD
        return {'x': jax.random.normal(ks[0], (B, N, DIM), jnp.float32), 'w_q': jax.random.normal(ks[1], (DIM, dim_inner), jnp.float32) * 0.02, 'w_k': jax.random.normal(ks[2], (DIM, dim_inner), jnp.float32) * 0.02, 'w_gate': jax.random.normal(ks[3], (DIM, HEADS * EXPERTS), jnp.float32) * 0.02, 'value_experts': jax.random.normal(ks[4], (EXPERTS, HEADS, DIM, DIM_HEAD), jnp.float32) * 0.02, 'output_experts': jax.random.normal(ks[5], (EXPERTS, HEADS, DIM_HEAD, DIM), jnp.float32) * 0.02}
    _L0_ffn_all = _L0_ffn_setup()
    _L0_ffn_in = {k: v for k, v in _L0_ffn_all.items() if k in ('w_q', 'w_k', 'w_gate', 'value_experts', 'output_experts')}
    del _L0_ffn_all

    def _L1_xattn_setup():
        import jax, jax.numpy as jnp
        import numpy as np
        from jax import lax
        BIG = jnp.float32(1e+30)

        def _pairwise_euclidean(a, b):
            aa = jnp.sum(a * a, axis=-1)[:, None]
            bb = jnp.sum(b * b, axis=-1)[None, :]
            ab = a @ b.T
            return jnp.sqrt(jnp.maximum(aa + bb - 2.0 * ab, 0.0))

        def _dtw_cost(D):
            row0 = jnp.cumsum(D[0])

            def row_step(prev_row, d_row):
                first = d_row[0] + prev_row[0]

                def col_step(left, inp):
                    d_ij, up, diag = inp
                    r = d_ij + jnp.minimum(jnp.minimum(up, left), diag)
                    return (r, r)
                _, rest = lax.scan(col_step, first, (d_row[1:], prev_row[1:], prev_row[:-1]))
                row = jnp.concatenate([first[None], rest])
                return (row, row)
            _, rows = lax.scan(row_step, row0, D[1:])
            return jnp.concatenate([row0[None], rows], axis=0)

        def _backtrack(R, T1, T2):
            L = T1 + T2 - 1

            def step(carry, _):
                i, j, done = carry
                valid = jnp.logical_not(done)
                cd = jnp.where((i > 0) & (j > 0), R[jnp.maximum(i - 1, 0), jnp.maximum(j - 1, 0)], BIG)
                cu = jnp.where(i > 0, R[jnp.maximum(i - 1, 0), j], BIG)
                cl = jnp.where(j > 0, R[i, jnp.maximum(j - 1, 0)], BIG)
                choice = jnp.argmin(jnp.stack([cd, cu, cl]))
                ni = jnp.where(choice <= 1, i - 1, i)
                nj = jnp.where((choice == 0) | (choice == 2), j - 1, j)
                at_origin = (i == 0) & (j == 0)
                ni = jnp.where(at_origin, 0, ni)
                nj = jnp.where(at_origin, 0, nj)
                return ((ni, nj, done | at_origin), (i, j, valid))
            init = (jnp.int32(T1 - 1), jnp.int32(T2 - 1), jnp.bool_(False))
            _, (i_idx, j_idx, valid) = lax.scan(step, init, None, length=L)
            return (i_idx, j_idx, valid)

        def _align_one(small, large):
            T_small, d = small.shape
            T_large = large.shape[0]
            D = _pairwise_euclidean(small, large)
            R = _dtw_cost(D)
            i_idx, j_idx, valid = _backtrack(R, T_small, T_large)
            contrib = small[i_idx] * valid[:, None].astype(small.dtype)
            expanded = jnp.zeros((T_large, d), dtype=small.dtype).at[j_idx].add(contrib)
            return expanded
        key = jax.random.key(seed)
        k1, k2 = jax.random.split(key)
        teacher = jax.random.normal(k1, (16, 100, 256), dtype=jnp.float32)
        student = jax.random.normal(k2, (16, 150, 256), dtype=jnp.float32)
        return {'teacher_features': teacher, 'student_features': student}
    _L1_xattn_all = _L1_xattn_setup()
    _L1_xattn_in = {k: v for k, v in _L1_xattn_all.items() if k in ()}
    del _L1_xattn_all

    def _L1_ffn_setup():
        import jax, jax.numpy as jnp
        import numpy as np
        B, S, IN, OUT = (4, 2048, 256, 256)
        EPS = 1e-06

        def _xla_quantized_matmul(x2d, weight_q, weight_scale):
            amax = jnp.max(jnp.abs(x2d), axis=-1, keepdims=True)
            x_scale = jnp.maximum(amax, EPS) / 127.0
            x_q = jnp.clip(jnp.round(x2d / x_scale), -128, 127).astype(jnp.int8)
            acc = jax.lax.dot_general(x_q, weight_q, (((1,), (1,)), ((), ())), preferred_element_type=jnp.int32)
            return acc.astype(jnp.float32) * x_scale * weight_scale[None, :]
        key = jax.random.key(seed)
        k1, k2, k3, k4 = jax.random.split(key, 4)
        x = jax.random.normal(k1, (B, S, IN), dtype=jnp.float32)
        weight_q = jax.random.randint(k2, (OUT, IN), -128, 128, dtype=jnp.int32).astype(jnp.int8)
        weight_scale = jax.random.uniform(k3, (OUT,), dtype=jnp.float32, minval=0.001, maxval=0.01)
        bias = jax.random.normal(k4, (OUT,), dtype=jnp.float32) * 0.01
        return {'x': x, 'weight_q': weight_q, 'weight_scale': weight_scale, 'bias': bias}
    _L1_ffn_all = _L1_ffn_setup()
    _L1_ffn_in = {k: v for k, v in _L1_ffn_all.items() if k in ('weight_q', 'weight_scale', 'bias')}
    del _L1_ffn_all

    def _L2_xattn_setup():
        import math
        import jax, jax.numpy as jnp
        import numpy as np
        B, T, DMODEL, NUM_HEADS = (2, 512, 256, 16)
        HEAD_DIM = DMODEL // NUM_HEADS
        MAX_TIMESCALE = 10000.0

        def _sinusoid_reversed(batch, length, dim):
            pos = jnp.arange(length - 1, -1, -1, dtype=jnp.float32)
            n = dim // 2
            inv = jnp.exp(jnp.arange(n, dtype=jnp.float32) * (-math.log(MAX_TIMESCALE) / (n - 1)))
            st = pos[:, None] * inv[None, :]
            emb = jnp.concatenate([jnp.sin(st), jnp.cos(st)], axis=-1)
            return jnp.broadcast_to(emb[None], (batch, length, dim))

        def _relative_shift(x):
            b, h, t, TT = x.shape
            x = jnp.pad(x, ((0, 0), (0, 0), (0, 0), (1, 0)))
            x = jnp.reshape(x, (b, h, TT + 1, t))[:, :, 1:, :]
            return jnp.reshape(x, (b, h, t, TT))
        key = jax.random.key(seed)
        ks = jax.random.split(key, 16)
        s = 1.0 / math.sqrt(DMODEL)
        d = {'x': jax.random.normal(ks[0], (B, T, DMODEL), jnp.float32), 'y': jax.random.normal(ks[1], (B, T, DMODEL), jnp.float32), 'mask': jnp.ones((B, 1, T, T), jnp.float32), 'Wq': jax.random.normal(ks[2], (DMODEL, DMODEL), jnp.float32) * s, 'bq': jnp.zeros((DMODEL,), jnp.float32), 'Wk': jax.random.normal(ks[3], (DMODEL, DMODEL), jnp.float32) * s, 'bk': jnp.zeros((DMODEL,), jnp.float32), 'Wv': jax.random.normal(ks[4], (DMODEL, DMODEL), jnp.float32) * s, 'bv': jnp.zeros((DMODEL,), jnp.float32), 'Wp': jax.random.normal(ks[5], (DMODEL, DMODEL), jnp.float32) * s, 'bp': jnp.zeros((DMODEL,), jnp.float32), 'r_w_bias': jax.random.normal(ks[6], (1, 1, NUM_HEADS, HEAD_DIM), jnp.float32) * 0.02, 'r_r_bias': jax.random.normal(ks[7], (1, 1, NUM_HEADS, HEAD_DIM), jnp.float32) * 0.02, 'Wo': jax.random.normal(ks[8], (DMODEL, DMODEL), jnp.float32) * s, 'bo': jnp.zeros((DMODEL,), jnp.float32)}
        return d
    _L2_xattn_all = _L2_xattn_setup()
    _L2_xattn_in = {k: v for k, v in _L2_xattn_all.items() if k in ('Wq', 'bq', 'Wk', 'bk', 'Wv', 'bv', 'Wp', 'bp', 'r_w_bias', 'r_r_bias', 'Wo', 'bo')}
    del _L2_xattn_all

    def _L2_ffn_setup():
        import jax, jax.numpy as jnp
        import numpy as np
        D_MODEL, D_FF, RANK = (256, 1024, 64)
        B, S = (4, 1024)
        key = jax.random.key(seed)
        ks = jax.random.split(key, 7)
        return {'x': jax.random.normal(ks[0], (B, S, D_MODEL), dtype=jnp.float32), 'U1': jax.random.normal(ks[1], (D_MODEL, RANK), dtype=jnp.float32) * 0.02, 'V1': jax.random.normal(ks[2], (RANK, D_FF), dtype=jnp.float32) * 0.02, 'b1': jnp.zeros((D_FF,), dtype=jnp.float32), 'U2': jax.random.normal(ks[3], (D_FF, RANK), dtype=jnp.float32) * 0.02, 'V2': jax.random.normal(ks[4], (RANK, D_MODEL), dtype=jnp.float32) * 0.02, 'b2': jnp.zeros((D_MODEL,), dtype=jnp.float32)}
    _L2_ffn_all = _L2_ffn_setup()
    _L2_ffn_in = {k: v for k, v in _L2_ffn_all.items() if k in ('U1', 'V1', 'b1', 'U2', 'V2', 'b2')}
    del _L2_ffn_all

    def _L3_xattn_setup():
        import jax, jax.numpy as jnp
        import numpy as np
        D_MODEL = 256
        NUM_HEADS = 16
        HEAD_DIM = D_MODEL // NUM_HEADS
        B, S = (4, 512)

        def _split_heads(x):
            b, s, _ = x.shape
            return x.reshape(b, s, NUM_HEADS, HEAD_DIM).transpose(0, 2, 1, 3)
        key = jax.random.key(seed)
        ks = jax.random.split(key, 11)
        sc = 1.0 / np.sqrt(D_MODEL)
        return {'query': jax.random.normal(ks[0], (B, S, D_MODEL), jnp.float32), 'key': jax.random.normal(ks[1], (B, S, D_MODEL), jnp.float32), 'value': jax.random.normal(ks[2], (B, S, D_MODEL), jnp.float32), 'Wq': jax.random.normal(ks[3], (D_MODEL, D_MODEL), jnp.float32) * sc, 'bq': jnp.zeros((D_MODEL,), jnp.float32), 'Wk': jax.random.normal(ks[4], (D_MODEL, D_MODEL), jnp.float32) * sc, 'bk': jnp.zeros((D_MODEL,), jnp.float32), 'Wv': jax.random.normal(ks[5], (D_MODEL, D_MODEL), jnp.float32) * sc, 'bv': jnp.zeros((D_MODEL,), jnp.float32), 'Wo': jax.random.normal(ks[6], (D_MODEL, D_MODEL), jnp.float32) * sc, 'bo': jnp.zeros((D_MODEL,), jnp.float32)}
    _L3_xattn_all = _L3_xattn_setup()
    _L3_xattn_in = {k: v for k, v in _L3_xattn_all.items() if k in ('Wq', 'bq', 'Wk', 'bk', 'Wv', 'bv', 'Wo', 'bo')}
    del _L3_xattn_all

    def _L3_ffn_setup():
        import jax, jax.numpy as jnp
        import numpy as np
        TOP_K = 2
        NUM_EXPERTS = 8
        key = jax.random.key(seed)
        ks = jax.random.split(key, 8)
        h, d, ds, E = (256, 128, 256, NUM_EXPERTS)
        s = 1.0 / np.sqrt(h)
        return {'x': jax.random.normal(ks[0], (2, 512, h), jnp.float32), 'router': jax.random.normal(ks[1], (h, E), jnp.float32) * s, 'experts_gate': jax.random.normal(ks[2], (E, h, d), jnp.float32) * s, 'experts_up': jax.random.normal(ks[3], (E, h, d), jnp.float32) * s, 'experts_down': jax.random.normal(ks[4], (E, d, h), jnp.float32) * (1.0 / np.sqrt(d)), 'shared_gate': jax.random.normal(ks[5], (h, ds), jnp.float32) * s, 'shared_up': jax.random.normal(ks[6], (h, ds), jnp.float32) * s, 'shared_down': jax.random.normal(ks[7], (ds, h), jnp.float32) * (1.0 / np.sqrt(ds))}
    _L3_ffn_all = _L3_ffn_setup()
    _L3_ffn_in = {k: v for k, v in _L3_ffn_all.items() if k in ('router', 'experts_gate', 'experts_up', 'experts_down', 'shared_gate', 'shared_up', 'shared_down')}
    del _L3_ffn_all
    return {'x': x, 'ctx_1024': ctx_1024, 'mask_Bx1xSxS2_ff1': mask_Bx1xSxS2_ff1, 'g_xattn': g_xattn, 'g_ffn': g_ffn, 'L0_ffn_w_q': _L0_ffn_in['w_q'], 'L0_ffn_w_k': _L0_ffn_in['w_k'], 'L0_ffn_w_gate': _L0_ffn_in['w_gate'], 'L0_ffn_value_experts': _L0_ffn_in['value_experts'], 'L0_ffn_output_experts': _L0_ffn_in['output_experts'], 'L1_ffn_weight_q': _L1_ffn_in['weight_q'], 'L1_ffn_weight_scale': _L1_ffn_in['weight_scale'], 'L1_ffn_bias': _L1_ffn_in['bias'], 'L2_xattn_Wq': _L2_xattn_in['Wq'], 'L2_xattn_bq': _L2_xattn_in['bq'], 'L2_xattn_Wk': _L2_xattn_in['Wk'], 'L2_xattn_bk': _L2_xattn_in['bk'], 'L2_xattn_Wv': _L2_xattn_in['Wv'], 'L2_xattn_bv': _L2_xattn_in['bv'], 'L2_xattn_Wp': _L2_xattn_in['Wp'], 'L2_xattn_bp': _L2_xattn_in['bp'], 'L2_xattn_r_w_bias': _L2_xattn_in['r_w_bias'], 'L2_xattn_r_r_bias': _L2_xattn_in['r_r_bias'], 'L2_xattn_Wo': _L2_xattn_in['Wo'], 'L2_xattn_bo': _L2_xattn_in['bo'], 'L2_ffn_U1': _L2_ffn_in['U1'], 'L2_ffn_V1': _L2_ffn_in['V1'], 'L2_ffn_b1': _L2_ffn_in['b1'], 'L2_ffn_U2': _L2_ffn_in['U2'], 'L2_ffn_V2': _L2_ffn_in['V2'], 'L2_ffn_b2': _L2_ffn_in['b2'], 'L3_xattn_Wq': _L3_xattn_in['Wq'], 'L3_xattn_bq': _L3_xattn_in['bq'], 'L3_xattn_Wk': _L3_xattn_in['Wk'], 'L3_xattn_bk': _L3_xattn_in['bk'], 'L3_xattn_Wv': _L3_xattn_in['Wv'], 'L3_xattn_bv': _L3_xattn_in['bv'], 'L3_xattn_Wo': _L3_xattn_in['Wo'], 'L3_xattn_bo': _L3_xattn_in['bo'], 'L3_ffn_router': _L3_ffn_in['router'], 'L3_ffn_experts_gate': _L3_ffn_in['experts_gate'], 'L3_ffn_experts_up': _L3_ffn_in['experts_up'], 'L3_ffn_experts_down': _L3_ffn_in['experts_down'], 'L3_ffn_shared_gate': _L3_ffn_in['shared_gate'], 'L3_ffn_shared_up': _L3_ffn_in['shared_up'], 'L3_ffn_shared_down': _L3_ffn_in['shared_down']}

def reference(x, ctx_1024, mask_Bx1xSxS2_ff1, g_xattn, g_ffn, L0_ffn_w_q, L0_ffn_w_k, L0_ffn_w_gate, L0_ffn_value_experts, L0_ffn_output_experts, L1_ffn_weight_q, L1_ffn_weight_scale, L1_ffn_bias, L2_xattn_Wq, L2_xattn_bq, L2_xattn_Wk, L2_xattn_bk, L2_xattn_Wv, L2_xattn_bv, L2_xattn_Wp, L2_xattn_bp, L2_xattn_r_w_bias, L2_xattn_r_r_bias, L2_xattn_Wo, L2_xattn_bo, L2_ffn_U1, L2_ffn_V1, L2_ffn_b1, L2_ffn_U2, L2_ffn_V2, L2_ffn_b2, L3_xattn_Wq, L3_xattn_bq, L3_xattn_Wk, L3_xattn_bk, L3_xattn_Wv, L3_xattn_bv, L3_xattn_Wo, L3_xattn_bo, L3_ffn_router, L3_ffn_experts_gate, L3_ffn_experts_up, L3_ffn_experts_down, L3_ffn_shared_gate, L3_ffn_shared_up, L3_ffn_shared_down):
    import jax
    import jax.numpy as jnp

    def _L0_xattn_ref(Q, K, V):
        import jax, jax.numpy as jnp
        import numpy as np
        import math
        HIDDEN = 256
        HEADS = 16
        HEAD = HIDDEN // HEADS
        SCALE_BASE = 512.0

        def _gammas(heads):
            return 1.0 - jnp.exp(jnp.linspace(math.log(1.0 / 32.0), math.log(1.0 / 512.0), heads))

        def _xpos(x, downscale):
            S, d = (x.shape[2], x.shape[3])
            half = d // 2
            base_scale = (jnp.arange(0, d, 2, dtype=jnp.float32) + 0.4 * d) / (1.4 * d)
            pos = jnp.arange(S, dtype=jnp.float32)
            scale = base_scale[None, :] ** (pos / SCALE_BASE)[:, None]
            if downscale:
                scale = 1.0 / scale
            inv_freq = 1.0 / 10000.0 ** (jnp.arange(half, dtype=jnp.float32) / half)
            sinusoid = pos[:, None] * inv_freq[None, :]
            sin = jnp.repeat(jnp.sin(sinusoid) * scale, 2, axis=-1)
            cos = jnp.repeat(jnp.cos(sinusoid) * scale, 2, axis=-1)
            x1 = x[..., ::2]
            x2 = x[..., 1::2]
            rot = jnp.stack([-x2, x1], axis=-1).reshape(x.shape)
            return x * cos + rot * sin

        def _decay_mask(S, gammas):
            n = jnp.arange(S)[:, None]
            m = jnp.arange(S)[None, :]
            diff = (n - m).astype(jnp.float32)
            mask = n >= m
            pw = jnp.maximum(diff, 0.0)[None, :, :]
            return jnp.where(mask[None, :, :], gammas[:, None, None] ** pw, 0.0)

        def retention_forward(Q, K, V):
            B, S, _ = Q.shape

            def split(x, hd):
                return x.reshape(B, S, HEADS, hd).transpose(0, 2, 1, 3)
            q = _xpos(split(Q, HEAD), downscale=False)
            k = _xpos(split(K, HEAD), downscale=True)
            v = split(V, HEAD)
            D = _decay_mask(S, _gammas(HEADS).astype(Q.dtype))
            scores = jnp.einsum('bhsd,bhtd->bhst', q, k) * D[None]
            out = jnp.einsum('bhst,bhtd->bhsd', scores, v)
            return out.transpose(0, 2, 1, 3).reshape(B, S, HEADS * HEAD)
        return retention_forward(Q, K, V)

    def _L0_ffn_ref(x, w_q, w_k, w_gate, value_experts, output_experts):
        import jax, jax.numpy as jnp
        import numpy as np
        B, N, DIM = (2, 512, 256)
        HEADS, DIM_HEAD, EXPERTS = (8, 64, 8)
        SCALE = DIM_HEAD ** (-0.5)
        b, n, _ = x.shape
        q = (x @ w_q).reshape(b, n, HEADS, DIM_HEAD).transpose(0, 2, 1, 3)
        k = (x @ w_k).reshape(b, n, HEADS, DIM_HEAD).transpose(0, 2, 1, 3)
        gates = jax.nn.sigmoid((x @ w_gate).reshape(b, n, HEADS, EXPERTS).transpose(0, 2, 1, 3))
        sel = jnp.argmax(gates, axis=-1)
        gm = jax.nn.one_hot(sel, EXPERTS, dtype=x.dtype) * gates
        values = jnp.einsum('bhne,ehdk,bnd->bhnk', gm, value_experts, x)
        sim = jnp.einsum('bhid,bhjd->bhij', q * SCALE, k)
        causal_mask = jnp.triu(jnp.ones((n, n), dtype=bool), 1)
        sim = jnp.where(causal_mask, jnp.finfo(sim.dtype).min, sim)
        attn = jax.nn.softmax(sim, axis=-1)
        out = jnp.einsum('bhij,bhjk->bhik', attn, values)
        out = jnp.einsum('bhne,ehkd,bhnk->bhnd', gm, output_experts, out)
        return out.sum(axis=1)

    def _L1_xattn_ref(teacher_features, student_features):
        import jax, jax.numpy as jnp
        import numpy as np
        from jax import lax
        BIG = jnp.float32(1e+30)

        def _pairwise_euclidean(a, b):
            aa = jnp.sum(a * a, axis=-1)[:, None]
            bb = jnp.sum(b * b, axis=-1)[None, :]
            ab = a @ b.T
            return jnp.sqrt(jnp.maximum(aa + bb - 2.0 * ab, 0.0))

        def _dtw_cost(D):
            row0 = jnp.cumsum(D[0])

            def row_step(prev_row, d_row):
                first = d_row[0] + prev_row[0]

                def col_step(left, inp):
                    d_ij, up, diag = inp
                    r = d_ij + jnp.minimum(jnp.minimum(up, left), diag)
                    return (r, r)
                _, rest = lax.scan(col_step, first, (d_row[1:], prev_row[1:], prev_row[:-1]))
                row = jnp.concatenate([first[None], rest])
                return (row, row)
            _, rows = lax.scan(row_step, row0, D[1:])
            return jnp.concatenate([row0[None], rows], axis=0)

        def _backtrack(R, T1, T2):
            L = T1 + T2 - 1

            def step(carry, _):
                i, j, done = carry
                valid = jnp.logical_not(done)
                cd = jnp.where((i > 0) & (j > 0), R[jnp.maximum(i - 1, 0), jnp.maximum(j - 1, 0)], BIG)
                cu = jnp.where(i > 0, R[jnp.maximum(i - 1, 0), j], BIG)
                cl = jnp.where(j > 0, R[i, jnp.maximum(j - 1, 0)], BIG)
                choice = jnp.argmin(jnp.stack([cd, cu, cl]))
                ni = jnp.where(choice <= 1, i - 1, i)
                nj = jnp.where((choice == 0) | (choice == 2), j - 1, j)
                at_origin = (i == 0) & (j == 0)
                ni = jnp.where(at_origin, 0, ni)
                nj = jnp.where(at_origin, 0, nj)
                return ((ni, nj, done | at_origin), (i, j, valid))
            init = (jnp.int32(T1 - 1), jnp.int32(T2 - 1), jnp.bool_(False))
            _, (i_idx, j_idx, valid) = lax.scan(step, init, None, length=L)
            return (i_idx, j_idx, valid)

        def _align_one(small, large):
            T_small, d = small.shape
            T_large = large.shape[0]
            D = _pairwise_euclidean(small, large)
            R = _dtw_cost(D)
            i_idx, j_idx, valid = _backtrack(R, T_small, T_large)
            contrib = small[i_idx] * valid[:, None].astype(small.dtype)
            expanded = jnp.zeros((T_large, d), dtype=small.dtype).at[j_idx].add(contrib)
            return expanded
        return jax.vmap(_align_one)(teacher_features, student_features)

    def _L1_ffn_ref(x, weight_q, weight_scale, bias):
        import jax, jax.numpy as jnp
        import numpy as np
        B, S, IN, OUT = (4, 2048, 256, 256)
        EPS = 1e-06

        def _xla_quantized_matmul(x2d, weight_q, weight_scale):
            amax = jnp.max(jnp.abs(x2d), axis=-1, keepdims=True)
            x_scale = jnp.maximum(amax, EPS) / 127.0
            x_q = jnp.clip(jnp.round(x2d / x_scale), -128, 127).astype(jnp.int8)
            acc = jax.lax.dot_general(x_q, weight_q, (((1,), (1,)), ((), ())), preferred_element_type=jnp.int32)
            return acc.astype(jnp.float32) * x_scale * weight_scale[None, :]
        orig_shape = x.shape
        x2d = x.reshape(-1, orig_shape[-1])
        out = _xla_quantized_matmul(x2d, weight_q, weight_scale)
        out = out.reshape(*orig_shape[:-1], out.shape[-1])
        out = out + bias
        return out

    def _L2_xattn_ref(x, y, mask, Wq, bq, Wk, bk, Wv, bv, Wp, bp, r_w_bias, r_r_bias, Wo, bo):
        import math
        import jax, jax.numpy as jnp
        import numpy as np
        B, T, DMODEL, NUM_HEADS = (2, 512, 256, 16)
        HEAD_DIM = DMODEL // NUM_HEADS
        MAX_TIMESCALE = 10000.0

        def _sinusoid_reversed(batch, length, dim):
            pos = jnp.arange(length - 1, -1, -1, dtype=jnp.float32)
            n = dim // 2
            inv = jnp.exp(jnp.arange(n, dtype=jnp.float32) * (-math.log(MAX_TIMESCALE) / (n - 1)))
            st = pos[:, None] * inv[None, :]
            emb = jnp.concatenate([jnp.sin(st), jnp.cos(st)], axis=-1)
            return jnp.broadcast_to(emb[None], (batch, length, dim))

        def _relative_shift(x):
            b, h, t, TT = x.shape
            x = jnp.pad(x, ((0, 0), (0, 0), (0, 0), (1, 0)))
            x = jnp.reshape(x, (b, h, TT + 1, t))[:, :, 1:, :]
            return jnp.reshape(x, (b, h, t, TT))
        b, t, _ = x.shape
        kv_t = y.shape[1]
        q = (x @ Wq + bq).reshape(b, t, NUM_HEADS, HEAD_DIM)
        k = (y @ Wk + bk).reshape(b, kv_t, NUM_HEADS, HEAD_DIM)
        v = (y @ Wv + bv).reshape(b, kv_t, NUM_HEADS, HEAD_DIM)
        content = jnp.einsum('bthd,bThd->bhtT', q + r_w_bias, k)
        pe = _sinusoid_reversed(b, kv_t, DMODEL) @ Wp + bp
        pe = pe.reshape(b, kv_t, NUM_HEADS, HEAD_DIM)
        rel = jnp.einsum('bthd,bThd->bhtT', q + r_r_bias, pe)
        rel = _relative_shift(rel)
        attn = (content + rel) * (1.0 / math.sqrt(HEAD_DIM))
        attn = attn * mask - 10000000000.0 * (1.0 - mask)
        p = jax.nn.softmax(attn, axis=-1)
        out = jnp.einsum('bhtT,bThd->bthd', p, v).reshape(b, t, DMODEL)
        return out @ Wo + bo

    def _L2_ffn_ref(x, U1, V1, b1, U2, V2, b2):
        import jax, jax.numpy as jnp
        import numpy as np
        D_MODEL, D_FF, RANK = (256, 1024, 64)
        B, S = (4, 1024)
        P = jnp.einsum('bsd,dr->bsr', x, U1)
        H = jax.nn.gelu(jnp.einsum('bsr,rf->bsf', P, V1) + b1)
        Q = jnp.einsum('bsf,fr->bsr', H, U2)
        return jnp.einsum('bsr,rd->bsd', Q, V2) + b2

    def _L3_xattn_ref(query, key, value, Wq, bq, Wk, bk, Wv, bv, Wo, bo):
        import jax, jax.numpy as jnp
        import numpy as np
        D_MODEL = 256
        NUM_HEADS = 16
        HEAD_DIM = D_MODEL // NUM_HEADS
        B, S = (4, 512)

        def _split_heads(x):
            b, s, _ = x.shape
            return x.reshape(b, s, NUM_HEADS, HEAD_DIM).transpose(0, 2, 1, 3)
        q = _split_heads(query @ Wq + bq)
        k = _split_heads(key @ Wk + bk)
        v = _split_heads(value @ Wv + bv)
        scores = jnp.einsum('bhqd,bhkd->bhqk', q, k) / np.sqrt(HEAD_DIM)
        attn = jax.nn.softmax(scores, axis=-1)
        out = jnp.einsum('bhqk,bhkd->bhqd', attn, v)
        out = out.transpose(0, 2, 1, 3).reshape(query.shape[0], -1, D_MODEL)
        return out @ Wo + bo

    def _L3_ffn_ref(x, router, experts_gate, experts_up, experts_down, shared_gate, shared_up, shared_down):
        import jax, jax.numpy as jnp
        import numpy as np
        TOP_K = 2
        NUM_EXPERTS = 8
        b, s, h = x.shape
        E = router.shape[1]
        shared_act = jax.nn.silu(jnp.einsum('bsh,hd->bsd', x, shared_gate))
        shared_up_out = jnp.einsum('bsh,hd->bsd', x, shared_up)
        shared_out = jnp.einsum('bsd,dh->bsh', shared_act * shared_up_out, shared_down)
        router_probs = jax.nn.softmax(jnp.einsum('bsh,he->bse', x, router), axis=-1)
        topk_probs, topk_idx = jax.lax.top_k(router_probs, TOP_K)
        coef = jnp.sum(jax.nn.one_hot(topk_idx, E, dtype=x.dtype) * topk_probs[..., None], axis=2)
        coef = coef.reshape(b * s, E)
        x_flat = x.reshape(b * s, h)
        gate = jnp.einsum('th,ehd->etd', x_flat, experts_gate)
        up = jnp.einsum('th,ehd->etd', x_flat, experts_up)
        expert_out = jnp.einsum('etd,edh->eth', jax.nn.silu(gate) * up, experts_down)
        routed = jnp.einsum('eth,te->th', expert_out, coef)
        return routed.reshape(b, s, h) + shared_out
    x = x + jnp.tanh(g_xattn[0]) * _L0_xattn_ref(_layernorm(x, axis=-1), ctx_1024, ctx_1024)
    x = x + jnp.tanh(g_ffn[0]) * _L0_ffn_ref(_layernorm(x, axis=-1), L0_ffn_w_q, L0_ffn_w_k, L0_ffn_w_gate, L0_ffn_value_experts, L0_ffn_output_experts)
    x = x + jnp.tanh(g_xattn[1]) * _L1_xattn_ref(ctx_1024, _layernorm(x, axis=-1))
    x = x + jnp.tanh(g_ffn[1]) * _L1_ffn_ref(_layernorm(x, axis=-1), L1_ffn_weight_q, L1_ffn_weight_scale, L1_ffn_bias)
    x = x + jnp.tanh(g_xattn[2]) * _L2_xattn_ref(_layernorm(x, axis=-1), ctx_1024, mask_Bx1xSxS2_ff1, L2_xattn_Wq, L2_xattn_bq, L2_xattn_Wk, L2_xattn_bk, L2_xattn_Wv, L2_xattn_bv, L2_xattn_Wp, L2_xattn_bp, L2_xattn_r_w_bias, L2_xattn_r_r_bias, L2_xattn_Wo, L2_xattn_bo)
    x = x + jnp.tanh(g_ffn[2]) * _L2_ffn_ref(_layernorm(x, axis=-1), L2_ffn_U1, L2_ffn_V1, L2_ffn_b1, L2_ffn_U2, L2_ffn_V2, L2_ffn_b2)
    x = x + jnp.tanh(g_xattn[3]) * _L3_xattn_ref(_layernorm(x, axis=-1), ctx_1024, ctx_1024, L3_xattn_Wq, L3_xattn_bq, L3_xattn_Wk, L3_xattn_bk, L3_xattn_Wv, L3_xattn_bv, L3_xattn_Wo, L3_xattn_bo)
    x = x + jnp.tanh(g_ffn[3]) * _L3_ffn_ref(_layernorm(x, axis=-1), L3_ffn_router, L3_ffn_experts_gate, L3_ffn_experts_up, L3_ffn_experts_down, L3_ffn_shared_gate, L3_ffn_shared_up, L3_ffn_shared_down)
    return x

_drawn_inputs = setup_inputs


def setup_inputs(seed=0):
    import zlib

    import numpy as np

    out = dict(_drawn_inputs(seed))
    spreads = {'L2_xattn_bq': (0.0, 0.8),
     'L2_xattn_bk': (0.0, 2.0),
     'L2_xattn_bv': (0.0, 0.8),
     'L2_xattn_bp': (0.0, 0.8),
     'L2_xattn_bo': (0.0, 0.8),
     'L2_ffn_b1': (0.0, 0.8),
     'L2_ffn_b2': (0.0, 0.8),
     'L3_xattn_bq': (0.0, 0.8),
     'L3_xattn_bk': (0.0, 2.0),
     'L3_xattn_bv': (0.0, 0.8),
     'L3_xattn_bo': (0.0, 2.0)}
    factors = {'g_ffn': 8.0,
     'L0_ffn_w_q': 8.0,
     'L0_ffn_w_k': 8.0,
     'L0_ffn_w_gate': 8.0,
     'L0_ffn_value_experts': 8.0,
     'L0_ffn_output_experts': 8.0,
     'L1_ffn_bias': 8.0,
     'L2_xattn_Wq': 8.0,
     'L2_xattn_Wk': 8.0,
     'L2_xattn_Wv': 6.853,
     'L2_xattn_Wp': 8.0,
     'L2_xattn_r_w_bias': 8.0,
     'L2_xattn_r_r_bias': 8.0,
     'L2_xattn_Wo': 6.684,
     'L2_ffn_U1': 8.0,
     'L2_ffn_V1': 8.0,
     'L2_ffn_U2': 8.0,
     'L2_ffn_V2': 8.0,
     'L3_xattn_Wq': 8.0,
     'L3_xattn_Wk': 8.0,
     'L3_xattn_Wv': 6.935,
     'L3_xattn_Wo': 6.687,
     'L3_ffn_router': 8.0,
     'L3_ffn_experts_gate': 8.0,
     'L3_ffn_experts_up': 8.0,
     'L3_ffn_experts_down': 8.0,
     'L3_ffn_shared_gate': 6.057,
     'L3_ffn_shared_up': 5.679,
     'L3_ffn_shared_down': 5.696}
    for name, (base, spread) in spreads.items():
        noise = np.random.default_rng([zlib.crc32(name.encode()), seed]).standard_normal(out[name].shape)
        drawn = base * np.exp(spread * noise) if base else spread * noise
        out[name] = jnp.asarray(drawn.astype(out[name].dtype))
    for name, factor in factors.items():
        out[name] = (out[name] * factor).astype(out[name].dtype)
    return out
```

```python
from contextlib import ExitStack
import math

import numpy as np
import concourse.bass as bass
from concourse import mybir

ALU = mybir.AluOpType
ACT = mybir.ActivationFunctionType
AX = mybir.AxisListType
F32 = mybir.dt.float32
BF16 = mybir.dt.bfloat16
I32 = mybir.dt.int32
I8 = mybir.dt.int8


B = 16
S = 128
D = 256
DT = D // 128
H = 16
HD = D // H
LN_EPS = 1e-5
LAYERS = 8


def retention_tables():
    f = np.float32
    half = HD // 2
    base = (np.arange(0, HD, 2, dtype=f) + f(0.4 * HD)) / f(1.4 * HD)
    pos = np.arange(S, dtype=f)
    scale = (base[None, :] ** (pos / f(512.0))[:, None]).astype(f)
    inv_freq = (f(1.0) / f(10000.0) ** (np.arange(half, dtype=f) / f(half))).astype(f)
    ang = (pos[:, None] * inv_freq[None, :]).astype(f)
    sign = np.tile(np.array([-1.0, 1.0], f), half)

    def table(sc):
        cos = np.repeat(np.cos(ang).astype(f) * sc, 2, axis=-1)
        sin = np.repeat(np.sin(ang).astype(f) * sc, 2, axis=-1) * sign[None, :]
        t = np.stack([cos.T, sin.T], axis=1)
        return np.ascontiguousarray(np.tile(t, (128 // HD, 1, 1)).astype(f))

    gam = (f(1.0) - np.exp(np.linspace(math.log(1 / 32), math.log(1 / 512), H).astype(f))).astype(f)
    s, t = np.arange(S)[None, :], np.arange(S)[:, None]
    decay = np.where(s >= t, gam[:, None, None] ** np.maximum(s - t, 0).astype(f), f(0)).astype(f)
    order = [h for bank in range(4) for h in heads_of_bank(bank)]
    decay = np.ascontiguousarray(decay[order].transpose(1, 0, 2))
    return table(scale), table((f(1.0) / scale).astype(f)), decay


def heads_of_bank(bank):
    return [2 * bank, 2 * bank + 1, 2 * bank + 8, 2 * bank + 9]


def pair_masks():
    odd = (np.arange(128) // HD) % 2
    return np.stack([1 - odd, odd], axis=1).astype(np.float32)


PRIME = 16


def after(n):
    return n + PRIME


class Kernel:

    def __init__(self, nc, ins, out):
        self.nc, self.ins, self.out = nc, ins, out
        self.unprimed, self.used = [], []

    def semaphore(self, ctx, name):
        s = self.nc.alloc_semaphore(name)
        self.unprimed.append(s)
        self.used.append(s)
        return s

    def clear_semaphores(self):
        numbers = sorted(s.num for s in self.used)
        with self.nc.Block() as block:
            @block.gpsimd
            def _(pool):
                first = 0
                for n in range(1, len(numbers) + 1):
                    if n == len(numbers) or numbers[n] != numbers[n - 1] + 1:
                        pool.sem_clear(range(numbers[first], numbers[n - 1] + 1))
                        first = n
        for s in self.used:
            self.nc.release_semaphore(s)
        self.used = []

    def prime(self, pool):
        for s in self.unprimed:
            pool.sem_inc(s, PRIME)
        self.unprimed = []


class LayerNorm:

    def __init__(self, k, ctx, name):
        nc = k.nc
        self.k = k
        sb = lambda n, s: ctx.enter_context(nc.sbuf_tensor(f"{name}_{n}", s, F32))
        sem = lambda n: k.semaphore(ctx, f"{name}_{n}")
        self.stats, self.mv = sb("stats", [128, 6]), sb("mv", [128, 2])
        self.ve, self.rstd, self.xn = sb("ve", [128, 1]), sb("rstd", [128, 1]), sb("xn", [128, D])
        self.pace = sb("pace", [128, 1])
        self.stats_ready, self.mv_ready, self.ve_ready = sem("stats"), sem("mean_var"), sem("var_eps")
        self.rstd_ready, self.xn_ready = sem("rstd"), sem("xn")

    def statistics(self, dve, b, x):
        dve.bn_stats(self.stats[:, :], x).then_inc(self.stats_ready, 1)
        dve.wait_ge(self.stats_ready, after(b + 1))
        dve.memset(self.pace[:, :], 0.0)
        dve.bn_aggr(self.mv[:, :], self.stats[:, :]).then_inc(self.mv_ready, 1)

    def inverse_root(self, pool, b):
        pool.wait_ge(self.mv_ready, after(b + 1))
        pool.tensor_tensor(self.ve[:, :], self.mv[:, 1:2], self.k.eps[:, :], ALU.add).then_inc(self.ve_ready, 1)
        pool.wait_ge(self.ve_ready, after(b + 1))
        pool.tensor_tensor(self.rstd[:, :], self.ve[:, :], self.k.minus_half[:, :],
                           ALU.pow).then_inc(self.rstd_ready, 1)

    def normalize(self, dve, b, x):
        dve.wait_ge(self.rstd_ready, after(b + 1))
        return dve.tensor_scalar(self.xn[:, :], x, self.mv[:, 0:1], self.rstd[:, :],
                                 ALU.subtract, ALU.mult).then_inc(self.xn_ready, 1)


def stage_retention(k, x_in, x_out):
    nc = k.nc
    with ExitStack() as ctx:
        sb = lambda n, s, t=F32: ctx.enter_context(nc.sbuf_tensor("ret_" + n, s, t))
        ps = lambda n, s, t=F32: ctx.enter_context(nc.psum_tensor("ret_" + n, s, t))
        sem = lambda n: k.semaphore(ctx, "ret_" + n)

        x = [sb(f"x{u}", [128, D]) for u in range(2)]
        c = [sb(f"c{u}", [128, D]) for u in range(2)]
        cT = [sb(f"cT{u}", [128, 2, DT, S]) for u in range(2)]
        q_rot = sb("q_rot", [128, 2, 1, S])
        k_rot = sb("k_rot", [128, 2, 1, S])
        decay = sb("decay", [128, H, S])
        ln = LayerNorm(k, ctx, "ret_ln")
        xn = ln.xn
        xs = sb("xs", [128, D])
        q_parts = sb("q_parts", [128, 2, DT, S])
        qT = sb("qT", [128, DT, S])
        qz = sb("qz", [128, DT, 2, S])
        k_parts = sb("k_parts", [128, 2, DT, S])
        kT = [sb(f"kT{u}", [128, DT, S]) for u in range(2)]
        sc = sb("sc", [128, H, S])
        xo = [sb(f"xo{u}", [128, D]) for u in range(2)]

        q_ps = ps("q_ps", [128, 2, DT, S])
        sc_ps = [ps(f"sc_ps{r}", [128, 4, S]) for r in range(4)]
        o_ps = ps("o_ps", [128, 512])

        tables_in = sem("tables_in")
        x_in_s = [sem(f"x_loaded{u}") for u in range(2)]
        out_s = [sem(f"x_stored{u}") for u in range(2)]
        xs_r = sem("xs")
        xT_r, qp_r, qT_r, qz_r = sem("xT"), sem("qp"), sem("qT"), sem("qz")
        kp_r, kT_r = sem("kp"), sem("kT")
        scps_r, sc_r, ops_r, xo_r = sem("scps"), sem("sc"), sem("ops"), sem("xo")

        with nc.Block() as block:

            @block.sync
            def _(sp):
                sp.dma_start(q_rot[:, :, 0, :], k.ins["c_q_rot"]).then_inc(tables_in, 16)
                sp.dma_start(k_rot[:, :, 0, :], k.ins["c_k_rot"]).then_inc(tables_in, 16)
                sp.dma_start(decay[:, :, :], k.ins["c_decay"]).then_inc(tables_in, 16)

                def load(b, u):
                    sp.dma_start(x[u][:, :], x_in[b]).then_inc(x_in_s[u], 16)
                    sp.dma_start(c[u][:, :], k.ins["ctx_1024"][b]).then_inc(x_in_s[u], 16)
                    sp.dma_start(cT[u][:, :, :, :].rearrange("p a t s -> p (a t) s"),
                                 k.ins["ctxT_pairs"][b].rearrange("a (t p) s -> p (a t) s", p=128)).then_inc(x_in_s[u], 16)

                def store(b, u):
                    sp.wait_ge(xo_r, after(b + 1))
                    sp.dma_start(x_out[b], xo[u][:, :]).then_inc(out_s[u], 16)

                load(0, 0)
                load(1, 1)
                with sp.Fori(0, B // 2 - 1) as i:
                    for u in range(2):
                        b = i * 2 + u
                        store(b, u)
                        load(b + 2, u)
                for u in range(2):
                    store(B - 2 + u, u)
                for u in range(2):
                    sp.wait_ge(out_s[u], after(16 * B // 2))

            @block.gpsimd
            def _(pool):
                k.prime(pool)
                pool.wait_ge(tables_in, after(48))
                with pool.Fori(0, B // 2) as i:
                    for u in range(2):
                        b = i * 2 + u
                        pool.wait_ge(x_in_s[u], after(i * 48 + 48))
                        pool.tensor_tensor(k_parts[:, :, :, :], cT[u][:, :, :, :],
                                           k_rot[:, :, :, :].to_broadcast([128, 2, DT, S]), ALU.mult).then_inc(kp_r, 1)
                        pool.wait_ge(kp_r, after(b + 1))
                        pool.wait_ge(ops_r, after(i * 2))
                        pool.tensor_tensor(kT[u][:, :, :], k_parts[:, 0], k_parts[:, 1], ALU.add).then_inc(kT_r, 1)
                        ln.inverse_root(pool, b)

            @block.vector
            def _(dve):
                dve.wait_ge(tables_in, after(48))
                with dve.Fori(0, B // 2) as i:
                    for u in range(2):
                        b = i * 2 + u
                        dve.wait_ge(x_in_s[u], after(i * 48 + 48))
                        ln.statistics(dve, b, x[u][:, :])
                        ln.normalize(dve, b, x[u][:, :])
                        dve.tensor_scalar(xs[:, :].rearrange("p (n two) -> p n two", two=2)[:, :, ::-1],
                                          x[u][:, :].rearrange("p (n two) -> p n two", two=2), ln.mv[:, 0:1],
                                          ln.rstd[:, :], ALU.subtract, ALU.mult).then_inc(xs_r, 1)
                        dve.wait_ge(xT_r, after(b + 1))
                        dve.tensor_tensor(q_parts[:, :, :, :], q_ps[:, :, :, :],
                                          q_rot[:, :, :, :].to_broadcast([128, 2, DT, S]), ALU.mult).then_inc(qp_r, 1)
                        dve.wait_ge(qp_r, after(b + 1))
                        dve.wait_ge(qz_r, after(b))
                        dve.tensor_tensor(qT[:, :, :], q_parts[:, 0], q_parts[:, 1], ALU.add).then_inc(qT_r, 1)
                        dve.wait_ge(ops_r, after(b))
                        for r in range(4):
                            dve.wait_ge(scps_r, after(b * 4 + (r + 1)))
                            dve.tensor_tensor(sc[:, 4 * r:4 * r + 4, :], sc_ps[r][:, :, :],
                                              decay[:, 4 * r:4 * r + 4, :], ALU.mult).then_inc(sc_r, 1)
                        dve.wait_ge(ops_r, after(b + 1))
                        dve.wait_ge(out_s[u], after(i * 16))
                        dve.scalar_tensor_tensor(xo[u][:, :], o_ps[:, 0:D], k.gates[:, 0:1], x[u][:, :],
                                                 ALU.mult, ALU.add).then_inc(xo_r, 1)

            @block.scalar
            def _(act):
                with act.Fori(0, B // 2) as i:
                    for u in range(2):
                        b = i * 2 + u
                        act.wait_ge(qT_r, after(b + 1))
                        act.wait_ge(scps_r, after(b * 4))
                        for par in range(2):
                            act.activation(qz[:, :, par, :], qT[:, :, :], ACT.Copy,
                                           scale=k.pair_mask[:, par:par + 1]).then_inc(qz_r, 1) if par else \
                                act.activation(qz[:, :, par, :], qT[:, :, :], ACT.Copy,
                                               scale=k.pair_mask[:, par:par + 1])

            @block.tensor
            def _(pe):
                def transposes(b):
                    pe.wait_ge(xs_r, after(b + 1))
                    pe.wait_ge(qp_r, after(b))
                    for t in range(DT):
                        pe.transpose(q_ps[:, 0, t, :], xn[:, 128 * t:128 * t + 128], k.ident[:, :])
                    for t in range(DT):
                        last = pe.transpose(q_ps[:, 1, t, :], xs[:, 128 * t:128 * t + 128], k.ident[:, :])
                    last.then_inc(xT_r, 1)

                with pe.Fori(0, B // 2) as i:
                    for u in range(2):
                        b = i * 2 + u
                        transposes(b)
                        pe.wait_ge(qz_r, after(b + 1))
                        pe.wait_ge(kT_r, after(b + 1))
                        pe.wait_ge(sc_r, after(b * 4))
                        for half in range(2):
                            for r in range(4):
                                rows = slice(32 * r, 32 * r + 32)
                                last = pe.matmul(sc_ps[r][:, 2 * half:2 * half + 2, :], kT[u][rows, half, :],
                                                 qz[rows, half, :, :], start=True, stop=True, tile_position=(32 * r, 0))
                                if half:
                                    last.then_inc(scps_r, 1)
                        pe.wait_ge(xo_r, after(b))
                        for r in range(4):
                            pe.wait_ge(sc_r, after(b * 4 + (r + 1)))
                            for j, h in enumerate(heads_of_bank(r)):
                                last = pe.matmul(o_ps[:, h * HD:h * HD + HD], sc[:, 4 * r + j, :],
                                                 c[u][:, h * HD:h * HD + HD], start=True, stop=True)
                        last.then_inc(ops_r, 1)


MH = 8
MD = 64
E = 8
HK = MH * MD
MASKED = -1.0e30


def expert_spread():
    t = np.zeros((E, MH, E, HK), np.float32)
    for e in range(E):
        for h in range(MH):
            t[e, h, e, h * MD:(h + 1) * MD] = 1.0
    return np.ascontiguousarray(t.reshape(E * MH, E * HK))


def stage_switch_attention(k, x_in, x_out):
    nc = k.nc
    TOP = 17.33
    with ExitStack() as ctx:
        sb = lambda n, s, t=F32: ctx.enter_context(nc.sbuf_tensor("moa_" + n, s, t))
        ps = lambda n, s, t=F32: ctx.enter_context(nc.psum_tensor("moa_" + n, s, t))
        sem = lambda n: k.semaphore(ctx, "moa_" + n)

        x = [sb(f"x{u}", [128, D]) for u in range(2)]
        xo = [sb(f"xo{u}", [128, D]) for u in range(2)]
        wq, wk, wg = sb("wq", [128, DT, HK]), sb("wk", [128, DT, HK]), sb("wg", [128, DT, MH * E])
        w_value = sb("w_value", [128, DT, E, HK])
        w_out = sb("w_out", [128, E, 4, D])
        spread_f = sb("spread_f", [E * MH, E * HK])
        spread = sb("spread", [E * MH, E * HK], BF16)
        identb = sb("identb", [128, 128], BF16)
        causal = sb("causal", [128, S])
        rank = sb("rank", [128, MH, E])
        ln = LayerNorm(k, ctx, "moa_ln")
        xnT = sb("xnT", [128, DT, S])
        qT, kT = sb("qT", [128, 4, S]), sb("kT", [128, 4, S])
        z = sb("z", [128, MH, E])
        z_top, tied, key, key_top = sb("z_top", [128, MH]), sb("tied", [128, MH, E]), sb("key", [128, MH, E]), sb("key_top", [128, MH])
        onehot = sb("onehot", [128, E, MH])
        onehot_b = sb("onehot_b", [128, 2 * E, MH], BF16)
        ohT = sb("ohT", [E * MH, S], BF16)
        eneg, gden, gate = sb("eneg", [128, MH]), sb("gden", [128, MH]), sb("gate", [128, MH])
        att = sb("att", [128, 2, 4, S])
        nmax = sb("nmax", [128, 2, 4])
        prob = sb("prob", [128, 2, 4, S])
        total = sb("total", [128, 2, 4])
        rtotal, scale_o = sb("rtotal", [128, 2, 4]), sb("scale_o", [128, MH])
        probT = sb("probT", [128, 2, 4, S])
        v_sel, v = sb("v_sel", [128, MH, MD]), sb("v", [128, MH, MD])
        og = sb("og", [128, MH, MD])
        ogT = sb("ogT", [128, 4, S])
        oe = [sb(f"oe{j}", [128, 4, S]) for j in range(2)]

        t_ps = ps("t_ps", [128, 512])
        q_ps, k_ps = ps("q_ps", [128, 4, S]), ps("k_ps", [128, 512])
        s_ps = [ps(f"s_ps{j}", [128, 4, S]) for j in range(2)]
        y_ps = [ps(f"y_ps{j}", [128, 4, S]) for j in range(2)]
        o_ps = ps("o_ps", [128, MH, MD])
        oh_view = t_ps[:, 384:448].bitcast(BF16)

        weights_in = sem("weights_in")
        x_loaded = [sem(f"x_loaded{u}") for u in range(2)]
        x_stored = [sem(f"x_stored{u}") for u in range(2)]
        consts_cast = sem("consts_cast")
        xT_ps, xT_ready, logits, q_done, k_done, q_ready, k_ready = map(sem, (
            "xT_ps", "xT_ready", "logits", "q_done", "k_done", "q_ready", "k_ready"))
        s_done, att_masked, max_ready, prob_ready = map(sem, ("s_done", "att_masked", "max_ready", "prob_ready"))
        gate_step, onehot_ready, eneg_ready, gate_ready = map(sem, ("gate_step", "onehot_ready", "eneg_ready", "gate_ready"))
        y_done, y_taken, v_ready = map(sem, ("y_done", "y_taken", "v_ready"))
        ohT_ps, ohT_ready, pT_ps, pT_ready = map(sem, ("ohT_ps", "ohT_ready", "pT_ps", "pT_ready"))
        o_done, scale_step, og_ready, ogT_ps, ogT_ready = map(sem, ("o_done", "scale_step", "og_ready", "ogT_ps", "ogT_ready"))
        mask_done, oe_ready, out_done, xo_ready = map(sem, ("mask_done", "oe_ready", "out_done", "xo_ready"))

        with nc.Block() as block:

            @block.sync
            def _(sp):
                def load(b, u):
                    sp.dma_start(x[u][:, :], x_in[b]).then_inc(x_loaded[u], 16)

                def store(b, u):
                    sp.wait_ge(xo_ready, after(b + 1))
                    sp.dma_start(x_out[b], xo[u][:, :]).then_inc(x_stored[u], 16)

                load(0, 0)
                load(1, 1)
                for tile, name in ((wg, "w_gate"), (wq, "w_q"), (wk, "w_k")):
                    sp.dma_start(tile[:, :, :], k.ins["L0_ffn_" + name].rearrange("(t p) n -> p t n", p=128)).then_inc(weights_in, 16)
                sp.dma_start(causal[:, :], k.ins["c_causal"]).then_inc(weights_in, 16)
                sp.dma_start(rank[:, :, :], k.ins["c_rank"]).then_inc(weights_in, 16)
                sp.dma_start(spread_f[:, :], k.ins["c_spread"]).then_inc(weights_in, 16)
                sp.dma_start(w_value[:, :, :, :].rearrange("p t e n -> p t (e n)"), k.ins["w_value"].rearrange("(t p) n -> p t n", p=128)).then_inc(weights_in, 16)
                sp.dma_start(w_out[:, :, :, :], k.ins["w_out"]).then_inc(weights_in, 16)
                with sp.Fori(0, B // 2 - 1) as i:
                    for u in range(2):
                        b = i * 2 + u
                        store(b, u)
                        load(b + 2, u)
                for u in range(2):
                    store(B - 2 + u, u)
                for u in range(2):
                    sp.wait_ge(x_stored[u], after(16 * B // 2))

            @block.gpsimd
            def _(pool):
                k.prime(pool)
                pool.wait_ge(weights_in, after(128))
                pool.tensor_copy(spread[:, :], spread_f[:, :]).then_inc(consts_cast, 1)
                pool.tensor_copy(identb[:, :], k.ident[:, :]).then_inc(consts_cast, 1)
                pool.memset(onehot_b[:, E:2 * E, :], 0.0).then_inc(consts_cast, 1)
                with pool.Fori(0, B) as b:
                    ln.inverse_root(pool, b)

            @block.vector
            def _(dve):
                dve.wait_ge(weights_in, after(128))
                with dve.Fori(0, B // 2) as i:
                    for u in range(2):
                        b = i * 2 + u
                        dve.wait_ge(x_loaded[u], after(i * 16 + 16))
                        ln.statistics(dve, b, x[u][:, :])
                        dve.wait_ge(xT_ps, after(b))
                        ln.normalize(dve, b, x[u][:, :])
                        dve.wait_ge(logits, after(b + 1))
                        dve.tensor_scalar(z[:, :, :], t_ps[:, 256:320].rearrange("p (h e) -> p h e", e=E), TOP, None,
                                          ALU.min).then_inc(gate_step, 1)
                        dve.wait_ge(gate_step, after(b * 5 + 1))
                        dve.wait_ge(eneg_ready, after(b))
                        dve.tensor_reduce(z_top[:, :], z[:, :, :], AX.X, ALU.max).then_inc(gate_step, 1)
                        dve.wait_ge(gate_step, after(b * 5 + 2))
                        dve.tensor_tensor(tied[:, :, :], z[:, :, :], z_top[:, :].unsqueeze(2).to_broadcast([128, MH, E]),
                                          ALU.is_equal).then_inc(gate_step, 1)
                        dve.wait_ge(gate_step, after(b * 5 + 3))
                        dve.tensor_tensor(key[:, :, :], tied[:, :, :], rank[:, :, :], ALU.mult).then_inc(gate_step, 1)
                        dve.wait_ge(gate_step, after(b * 5 + 4))
                        dve.tensor_reduce(key_top[:, :], key[:, :, :], AX.X, ALU.max).then_inc(gate_step, 1)
                        dve.wait_ge(gate_step, after(b * 5 + 5))
                        dve.wait_ge(ohT_ps, after(b))
                        dve.tensor_tensor(onehot[:, :, :].rearrange("p e h -> p h e"), key[:, :, :],
                                          key_top[:, :].unsqueeze(2).to_broadcast([128, MH, E]), ALU.is_equal)
                        dve.tensor_tensor(onehot_b[:, 0:E, :].rearrange("p e h -> p h e"), key[:, :, :],
                                          key_top[:, :].unsqueeze(2).to_broadcast([128, MH, E]),
                                          ALU.is_equal).then_inc(onehot_ready, 1)
                        dve.wait_ge(eneg_ready, after(b + 1))
                        dve.tensor_scalar(gden[:, :], eneg[:, :], 1.0, None, ALU.add).then_inc(gate_ready, 1)
                        dve.wait_ge(gate_ready, after(2 * b + 1))
                        dve.reciprocal(gate[:, :], gden[:, :]).then_inc(gate_ready, 1)
                        for j in range(2):
                            dve.wait_ge(s_done, after(b * 2 + (j + 1)))
                            dve.wait_ge(prob_ready, after(b * 8))
                            dve.tensor_tensor(att[:, j], s_ps[j][:, :, :], causal[:, :].unsqueeze(1).to_broadcast([128, 4, S]),
                                              ALU.add).then_inc(att_masked, 1)
                            dve.wait_ge(att_masked, after(b * 2 + (j + 1)))
                            dve.tensor_reduce(nmax[:, j], att[:, j], AX.X, ALU.max, negate=True).then_inc(max_ready, 1)
                        dve.wait_ge(onehot_ready, after(b + 1))
                        for e in range(1, E):
                            dve.wait_ge(y_taken, after(b * 8 + e))
                            dve.wait_ge(y_done, after(b * 8 + (e + 1)))
                            dve.memset(ln.pace[:, :], 0.0)
                            dve.copy_predicated(v_sel[:, :, :], onehot[:, e, :].bitcast(I32).unsqueeze(2).to_broadcast([128, MH, MD]),
                                                y_ps[e % 2][:, :, :].rearrange("p m (h k) -> p (m h) k", k=MD)).then_inc(y_taken, 1)
                        dve.wait_ge(y_taken, after(b * 8 + 8))
                        dve.wait_ge(gate_ready, after(2 * b + 2))
                        dve.wait_ge(o_done, after(b))
                        dve.tensor_tensor(v[:, :, :], v_sel[:, :, :], gate[:, :].unsqueeze(2).to_broadcast([128, MH, MD]),
                                          ALU.mult).then_inc(v_ready, 1)
                        dve.wait_ge(pT_ps, after(b * 2 + 2))
                        dve.tensor_copy(probT[:, 1], s_ps[1][:, :, :]).then_inc(pT_ready, 1)
                        dve.wait_ge(prob_ready, after(b * 8 + 8))
                        dve.reciprocal(rtotal[:, :, :], total[:, :, :]).then_inc(scale_step, 1)
                        dve.wait_ge(scale_step, after(2 * b + 1))
                        dve.tensor_tensor(scale_o[:, :].rearrange("p (m j) -> p j m", j=2), rtotal[:, :, :],
                                          gate[:, :].rearrange("p (m j) -> p j m", j=2), ALU.mult).then_inc(scale_step, 1)
                        dve.wait_ge(scale_step, after(2 * b + 2))
                        dve.wait_ge(o_done, after(b + 1))
                        dve.wait_ge(ogT_ps, after(b))
                        dve.tensor_tensor(og[:, :, :], o_ps[:, :, :], scale_o[:, :].unsqueeze(2).to_broadcast([128, MH, MD]),
                                          ALU.mult).then_inc(og_ready, 1)
                        dve.wait_ge(ogT_ready, after(b + 1))
                        for e in range(E):
                            dve.wait_ge(mask_done, after(b * 8 + (e + 1)))
                            dve.wait_ge(out_done, after(b * 8 + (e - 1)))
                            dve.tensor_tensor(oe[e % 2][:, :, :], y_ps[e % 2][:, :, :], ogT[:, :, :],
                                              ALU.mult).then_inc(oe_ready, 1)
                        dve.wait_ge(out_done, after(b * 8 + 8))
                        dve.wait_ge(x_stored[u], after(i * 16))
                        dve.scalar_tensor_tensor(xo[u][:, :], k_ps[:, 0:D], k.gates[:, 4:5], x[u][:, :],
                                                 ALU.mult, ALU.add).then_inc(xo_ready, 1)

            @block.scalar
            def _(act):
                with act.Fori(0, B) as b:
                    act.wait_ge(xT_ps, after(b + 1))
                    act.wait_ge(y_done, after(b * 8))
                    act.activation(xnT[:, :, :], t_ps[:, 0:D].rearrange("p (t s) -> p t s", t=DT), ACT.Copy).then_inc(xT_ready, 1)
                    act.wait_ge(s_done, after(b * 2))
                    act.wait_ge(q_done, after(b + 1))
                    act.activation(qT[:, :, :], q_ps[:, :, :], ACT.Copy, scale=MD ** -0.5).then_inc(q_ready, 1)
                    act.wait_ge(k_done, after(b + 1))
                    act.activation(kT[:, :, :], k_ps[:, :].rearrange("p (m s) -> p m s", s=S), ACT.Copy).then_inc(k_ready, 1)
                    act.wait_ge(gate_step, after(b * 5 + 2))
                    act.wait_ge(gate_ready, after(b * 2))
                    act.activation(eneg[:, :], z_top[:, :], ACT.Exp, scale=-1.0).then_inc(eneg_ready, 1)
                    act.wait_ge(v_ready, after(b))
                    act.wait_ge(y_done, after(b * 8 + 1))
                    act.activation(v_sel[:, :, :], y_ps[0][:, :, :].rearrange("p m (h k) -> p (m h) k", k=MD),
                                   ACT.Copy).then_inc(y_taken, 1)
                    act.wait_ge(pT_ps, after(b * 2))
                    act.wait_ge(scale_step, after(b * 2))
                    for j in range(2):
                        act.wait_ge(max_ready, after(b * 2 + (j + 1)))
                        for m in range(4):
                            act.activation(prob[:, j, m], att[:, j, m], ACT.Exp, bias=nmax[:, j, m:m + 1],
                                           accum_out=total[:, j, m:m + 1]).then_inc(prob_ready, 1)
                    act.wait_ge(ohT_ps, after(b + 1))
                    act.wait_ge(mask_done, after(b * 8))
                    act.activation(ohT[:, :], oh_view[0:E * MH, :], ACT.Copy).then_inc(ohT_ready, 1)
                    act.wait_ge(pT_ps, after(b * 2 + 1))
                    act.wait_ge(o_done, after(b))
                    act.activation(probT[:, 0], s_ps[0][:, :, :], ACT.Copy).then_inc(pT_ready, 1)
                    act.wait_ge(ogT_ps, after(b + 1))
                    act.wait_ge(oe_ready, after(b * 8))
                    act.activation(ogT[:, :, :], q_ps[:, :, :], ACT.Copy).then_inc(ogT_ready, 1)

            @block.tensor
            def _(pe):
                pe.wait_ge(weights_in, after(128))
                pe.wait_ge(consts_cast, after(3))
                with pe.Fori(0, B) as b:
                    pe.wait_ge(ln.xn_ready, after(b + 1))
                    pe.wait_ge(ohT_ready, after(b))
                    for t in range(DT):
                        last = pe.transpose(t_ps[:, 128 * t:128 * t + 128], ln.xn[:, 128 * t:128 * t + 128], k.ident[:, :])
                    last.then_inc(xT_ps, 1)
                    pe.wait_ge(xT_ready, after(b + 1))
                    for t in range(DT):
                        last = pe.matmul(t_ps[:, 256:320], xnT[:, t, :], wg[:, t, :], start=(t == 0), stop=(t == DT - 1))
                    last.then_inc(logits, 1)
                    pe.wait_ge(ogT_ready, after(b))
                    for m in range(4):
                        for t in range(DT):
                            last = pe.matmul(q_ps[:, m, :], wq[:, t, 128 * m:128 * m + 128], xnT[:, t, :],
                                             start=(t == 0), stop=(t == DT - 1))
                    last.then_inc(q_done, 1)
                    pe.wait_ge(xo_ready, after(b))
                    for m in range(4):
                        for t in range(DT):
                            last = pe.matmul(k_ps[:, 128 * m:128 * m + 128], wk[:, t, 128 * m:128 * m + 128], xnT[:, t, :],
                                             start=(t == 0), stop=(t == DT - 1))
                    last.then_inc(k_done, 1)
                    pe.wait_ge(q_ready, after(b + 1))
                    pe.wait_ge(k_ready, after(b + 1))
                    pe.wait_ge(pT_ready, after(b * 2))
                    for m in range(4):
                        for j in range(2):
                            rows = slice(64 * j, 64 * j + 64)
                            last = pe.matmul(s_ps[j][:, m, :], qT[rows, m, :], kT[rows, m, :], start=True, stop=True)
                            if m == 3:
                                last.then_inc(s_done, 1)
                    pe.wait_ge(oe_ready, after(b * 8))
                    for e in range(E):
                        if e >= 2:
                            pe.wait_ge(y_taken, after(b * 8 + (e - 1)))
                        for t in range(DT):
                            last = pe.matmul(y_ps[e % 2][:, :, :], xnT[:, t, :], w_value[:, t, e, :],
                                             start=(t == 0), stop=(t == DT - 1))
                        last.then_inc(y_done, 1)
                    pe.wait_ge(onehot_ready, after(b + 1))
                    pe.transpose(oh_view, onehot_b[:, :, :].rearrange("p e h -> p (e h)"), identb[:, :]).then_inc(ohT_ps, 1)
                    for j in range(2):
                        pe.wait_ge(prob_ready, after(b * 8 + (4 * j + 4)))
                        for m in range(4):
                            last = pe.transpose(s_ps[j][:, m, :], prob[:, j, m], k.ident[:, :])
                        last.then_inc(pT_ps, 1)
                    pe.wait_ge(pT_ready, after(b * 2 + 2))
                    pe.wait_ge(v_ready, after(b + 1))
                    pe.wait_ge(og_ready, after(b))
                    for h in range(MH):
                        last = pe.matmul(o_ps[:, h, :], probT[:, h % 2, h // 2], v[:, h, :], start=True, stop=True)
                    last.then_inc(o_done, 1)

                    def mask(e):
                        if e >= 2:
                            pe.wait_ge(oe_ready, after(b * 8 + (e - 1)))
                        for m in range(4):
                            last = pe.matmul(y_ps[e % 2][:, m, :], spread[:, (4 * e + m) * 128:(4 * e + m) * 128 + 128],
                                             ohT[:, :], start=True, stop=True)
                        last.then_inc(mask_done, 1)

                    pe.wait_ge(ohT_ready, after(b + 1))
                    pe.wait_ge(y_taken, after(b * 8 + 8))
                    mask(0)
                    mask(1)
                    pe.wait_ge(og_ready, after(b + 1))
                    for m in range(4):
                        last = pe.transpose(q_ps[:, m, :], og[:, 2 * m:2 * m + 2, :].rearrange("p h k -> p (h k)"), k.ident[:, :])
                    last.then_inc(ogT_ps, 1)
                    for e in range(E):
                        pe.wait_ge(oe_ready, after(b * 8 + (e + 1)))
                        for m in range(4):
                            last = pe.matmul(k_ps[:, 0:D], oe[e % 2][:, m, :], w_out[:, e, m, :],
                                             start=(e == 0 and m == 0), stop=(e == E - 1 and m == 3))
                        last.then_inc(out_done, 1)
                        if e + 2 < E:
                            mask(e + 2)


BIG = 1.0e30


def stage_distances(k, x_in, dist):
    nc = k.nc
    TINY = 1.0e-30
    with ExitStack() as ctx:
        sb = lambda n, s, t=F32: ctx.enter_context(nc.sbuf_tensor("dist_" + n, s, t))
        ps = lambda n, s, t=F32: ctx.enter_context(nc.psum_tensor("dist_" + n, s, t))
        sem = lambda n: k.semaphore(ctx, "dist_" + n)
        x = [sb(f"x{u}", [128, D]) for u in range(2)]
        c = [sb(f"c{u}", [128, D]) for u in range(2)]
        cT = [sb(f"cT{u}", [128, DT, S]) for u in range(2)]
        ln = LayerNorm(k, ctx, "dist_ln")
        ones = sb("ones", [128, 128])
        yT, y2T = sb("yT", [128, DT, S]), sb("y2T", [128, DT, S])
        csq, aa = sb("csq", [128, D]), sb("aa", [128, 1])
        norms, d2, root, safe, quot = (sb(n, [128, S]) for n in ("norms", "d2", "root", "safe", "quot"))
        d = [sb(f"d{u}", [128, S]) for u in range(2)]
        t_ps = ps("t_ps", [128, 512])
        ab_ps, bb_ps = ps("ab_ps", [128, 512]), ps("bb_ps", [128, 512])
        in_loaded = [sem(f"in_loaded{u}") for u in range(2)]
        d_stored = [sem(f"d_stored{u}") for u in range(2)]
        ones_set, xT_ps, yT_ready, aa_ready, products, step, root_ready, d_ready = map(sem, (
            "ones_set", "xT_ps", "yT_ready", "aa_ready", "products", "step", "root_ready", "d_ready"))
        quot_ready = sem("quot_ready")
        STEPS = 5

        with nc.Block() as block:

            @block.sync
            def _(sp):
                def load(b, u):
                    sp.dma_start(x[u][:, :], x_in[b]).then_inc(in_loaded[u], 16)
                    sp.dma_start(c[u][:, :], k.ins["ctx_1024"][b]).then_inc(in_loaded[u], 16)
                    sp.dma_start(cT[u][:, :, :], k.ins["ctxT_pairs"][b, 0].rearrange("(t p) s -> p t s", p=128)).then_inc(in_loaded[u], 16)

                def store(b, u):
                    sp.wait_ge(d_ready, after(b + 1))
                    sp.dma_start(dist[b], d[u][:, :]).then_inc(d_stored[u], 16)

                load(0, 0)
                load(1, 1)
                with sp.Fori(0, B // 2 - 1) as i:
                    for u in range(2):
                        b = i * 2 + u
                        store(b, u)
                        load(b + 2, u)
                for u in range(2):
                    store(B - 2 + u, u)
                for u in range(2):
                    sp.wait_ge(d_stored[u], after(16 * B // 2))

            @block.gpsimd
            def _(pool):
                k.prime(pool)
                pool.memset(ones[:, :], 1.0).then_inc(ones_set, 1)
                with pool.Fori(0, B) as b:
                    ln.inverse_root(pool, b)

            @block.vector
            def _(dve):
                with dve.Fori(0, B // 2) as i:
                    for u in range(2):
                        b = i * 2 + u
                        dve.wait_ge(in_loaded[u], after(i * 48 + 48))
                        ln.statistics(dve, b, x[u][:, :])
                        dve.wait_ge(xT_ps, after(b))
                        ln.normalize(dve, b, x[u][:, :])
                        dve.wait_ge(products, after(b + 1))
                        dve.wait_ge(aa_ready, after(b + 1))
                        dve.tensor_scalar(norms[:, :], bb_ps[:, 0:S], aa[:, :], None, ALU.add).then_inc(step, 1)
                        dve.wait_ge(step, after(b * STEPS + 1))
                        dve.scalar_tensor_tensor(quot[:, :], ab_ps[:, 0:S], -2.0, norms[:, :], ALU.mult, ALU.add).then_inc(step, 1)
                        dve.wait_ge(step, after(b * STEPS + 2))
                        dve.tensor_scalar(d2[:, :], quot[:, :], 0.0, None, ALU.max).then_inc(step, 1)
                        dve.wait_ge(root_ready, after(b + 1))
                        dve.tensor_scalar(quot[:, :], root[:, :], TINY, None, ALU.max).then_inc(step, 1)
                        dve.wait_ge(step, after(b * STEPS + 4))
                        dve.reciprocal(safe[:, :], quot[:, :]).then_inc(step, 1)
                        dve.wait_ge(step, after(b * STEPS + 5))
                        dve.tensor_tensor(norms[:, :], d2[:, :], safe[:, :], ALU.mult).then_inc(quot_ready, 1)
                        dve.wait_ge(quot_ready, after(b + 1))
                        dve.wait_ge(d_stored[u], after(i * 16))
                        dve.tensor_tensor(d[u][:, :], norms[:, :], root[:, :], ALU.add).then_inc(d_ready, 1)

            @block.scalar
            def _(act):
                with act.Fori(0, B // 2) as i:
                    for u in range(2):
                        b = i * 2 + u
                        act.wait_ge(in_loaded[u], after(i * 48 + 48))
                        act.wait_ge(step, after(b * STEPS))
                        act.activation(csq[:, :], c[u][:, :], ACT.Square, accum_out=aa[:, :]).then_inc(aa_ready, 1)
                        act.wait_ge(products, after(b))
                        act.wait_ge(xT_ps, after(b + 1))
                        act.activation(yT[:, :, :], t_ps[:, 0:D].rearrange("p (t s) -> p t s", s=S), ACT.Copy)
                        act.activation(y2T[:, :, :], t_ps[:, 0:D].rearrange("p (t s) -> p t s", s=S), ACT.Square).then_inc(yT_ready, 1)
                        act.wait_ge(step, after(b * STEPS + 3))
                        act.wait_ge(d_ready, after(b))
                        act.activation(root[:, :], d2[:, :], ACT.Sqrt).then_inc(root_ready, 1)

            @block.tensor
            def _(pe):
                pe.wait_ge(ones_set, after(1))
                with pe.Fori(0, B // 2) as i:
                    for u in range(2):
                        b = i * 2 + u
                        pe.wait_ge(ln.xn_ready, after(b + 1))
                        pe.wait_ge(yT_ready, after(b))
                        for t in range(DT):
                            last = pe.transpose(t_ps[:, 128 * t:128 * t + 128], ln.xn[:, 128 * t:128 * t + 128], k.ident[:, :])
                        last.then_inc(xT_ps, 1)
                        pe.wait_ge(in_loaded[u], after(i * 48 + 48))
                        pe.wait_ge(yT_ready, after(b + 1))
                        pe.wait_ge(step, after(b * STEPS))
                        for t in range(DT):
                            pe.matmul(ab_ps[:, 0:S], cT[u][:, t, :], yT[:, t, :], start=(t == 0), stop=(t == DT - 1))
                        for t in range(DT):
                            last = pe.matmul(bb_ps[:, 0:S], ones[:, :], y2T[:, t, :], start=(t == 0), stop=(t == DT - 1))
                        last.then_inc(products, 1)


def stage_warp(k, dist, costs, steps, path):
    nc = k.nc
    with ExitStack() as ctx:
        sb = lambda n, s, t=F32: ctx.enter_context(nc.sbuf_tensor("warp_" + n, s, t))
        ps = lambda n, s, t=F32: ctx.enter_context(nc.psum_tensor("warp_" + n, s, t))
        sem = lambda n: k.semaphore(ctx, "warp_" + n)
        W = S + 1
        entry = sb("entry", [128, S])
        iota_j = sb("iota_j", [128, S])
        t_ps = ps("t_ps", [128, 512])
        dist_in, big_set, zero_set, row_min, row_ready, costs_out = map(sem, ("dist_in", "big_set", "zero_set", "row_min", "row_ready", "costs_out"))
        tables_in, bulk, steps_out, steps_in, entry_ready, entry_T, onehot_ready = map(sem, (
            "tables_in", "bulk", "steps_out", "steps_in", "entry_ready", "entry_T", "onehot_ready"))
        GO = 4
        with ExitStack() as forward:
            sbf = lambda n, s, t=F32: forward.enter_context(nc.sbuf_tensor("warpf_" + n, s, t))
            dd = sbf("dd", [B, S, S])
            rr = sbf("rr", [B, S, W])
            low = [sbf(f"low{j}", [B, S]) for j in range(2)]
            zeros = sbf("zeros", [B, S])
            big = sbf("big", [B, W])
            with nc.Block() as block:
                @block.sync
                def _(sp):
                    sp.dma_start(dd[:, :, :].rearrange("b i j -> b (i j)"), dist.rearrange("b i j -> b (i j)")).then_inc(dist_in, 16)
                    sp.dma_start(iota_j[:, :], k.ins["c_iota"]).then_inc(dist_in, 16)
                    sp.wait_ge(big_set, after(2))
                    sp.dma_start(costs[:, 0, :], big[:, :]).then_inc(costs_out, 16)
                    sp.wait_ge(row_ready, after(S))
                    sp.dma_start(costs[:, 1:S + 1, :].rearrange("b i j -> b (i j)"), rr[:, :, :].rearrange("b i j -> b (i j)")).then_inc(costs_out, 16)
                    sp.wait_ge(costs_out, after(32))

                @block.gpsimd
                def _(pool):
                    k.prime(pool)
                    pool.memset(big[:, :], BIG).then_inc(big_set, 1)
                    pool.memset(rr[:, :, 0:1], BIG).then_inc(big_set, 1)
                    pool.memset(zeros[:, :], 0.0).then_inc(zero_set, 1)
                    pool.memset(entry[:, :], 0.0).then_inc(zero_set, 1)

                @block.vector
                def _(dve):
                    dve.wait_ge(dist_in, after(32))
                    dve.wait_ge(big_set, after(2))
                    dve.wait_ge(zero_set, after(2))
                    dve.tensor_tensor_scan(rr[:, 0, 1:W], dd[:, 0, :], zeros[:, :], 0.0, ALU.add, ALU.add).then_inc(row_ready, 1)

                    def row(i, j):
                        dve.wait_ge(row_ready, after(i))
                        dve.tensor_tensor(low[j][:, :], rr[:, bass.ds(i - 1, 1), 1:W].rearrange("b a j -> b (a j)"),
                                          rr[:, bass.ds(i - 1, 1), 0:S].rearrange("b a j -> b (a j)"), ALU.min).then_inc(row_min, 1)
                        dve.wait_ge(row_min, after(i))
                        dve.tensor_tensor_scan(rr[:, bass.ds(i, 1), 1:W].rearrange("b a j -> b (a j)"), low[j][:, :],
                                               dd[:, bass.ds(i, 1), :].rearrange("b a j -> b (a j)"), BIG, ALU.min, ALU.add).then_inc(row_ready, 1)

                    for i in range(1, GO):
                        row(i, i % 2)
                    with dve.Fori(1, S // GO) as g:
                        for j in range(GO):
                            row(g * GO + j, j % 2)

        with ExitStack() as bulk_ctx:
            sbb = lambda n, s, t=F32: bulk_ctx.enter_context(nc.sbuf_tensor("warpb_" + n, s, t))
            cost, above = sbb("cost", [128, B, W]), sbb("above", [128, B, W])
            low = sbb("lowb", [128, B, S])
            go_left = sbb("go_left", [128, B * S + 8])
            stay, diag = sbb("stay", [128, B, S]), sbb("diag", [128, B, S])
            nxt = sbb("nxt", [128, B * S])
            leftv = go_left[:, 0:B * S].rearrange("p (b j) -> p b j", j=S)
            chase = sbb("chase", [B, S, S])
            hit = sbb("hit", [B, S])
            with nc.Block() as block:
                @block.sync
                def _(sp):
                    sp.dma_start(cost[:, :, :], costs[:, 1:S + 1, :].rearrange("b i j -> i b j")).then_inc(tables_in, 16)
                    sp.dma_start(above[:, :, :], costs[:, 0:S, :].rearrange("b i j -> i b j")).then_inc(tables_in, 16)
                    sp.wait_ge(bulk, after(7))
                    sp.dma_start(steps.rearrange("b i j -> i b j"), nxt[:, :].rearrange("p (b j) -> p b j", j=S)).then_inc(steps_out, 16)
                    sp.wait_ge(steps_out, after(16))
                    sp.dma_start(chase[:, :, :].rearrange("b i j -> b (i j)"), steps.rearrange("b i j -> b (i j)")).then_inc(steps_in, 16)
                    sp.wait_ge(bulk, after(9))
                    sp.dma_start(path.rearrange("i b j -> i (b j)"), nxt[:, :]).then_inc(steps_out, 16)
                    sp.wait_ge(steps_out, after(32))

                @block.vector
                def _(dve):
                    iota_b = iota_j[:, :].unsqueeze(1).to_broadcast([128, B, S])
                    dve.memset(go_left[:, B * S:B * S + 8], 0.0)
                    dve.wait_ge(tables_in, after(32))
                    dve.tensor_tensor(low[:, :, :], above[:, :, 1:W], above[:, :, 0:S], ALU.min).then_inc(bulk, 1)
                    dve.tensor_tensor(diag[:, :, :], above[:, :, 0:S], above[:, :, 1:W], ALU.is_le).then_inc(bulk, 1)
                    dve.wait_ge(bulk, after(2))
                    dve.tensor_tensor(leftv, cost[:, :, 0:S], low[:, :, :], ALU.is_lt).then_inc(bulk, 1)
                    dve.tensor_tensor(stay[:, :, :], cost[:, :, 0:S], low[:, :, :], ALU.is_ge).then_inc(bulk, 1)
                    dve.wait_ge(bulk, after(4))
                    dve.tensor_tensor(low[:, :, :], iota_b, diag[:, :, :], ALU.subtract).then_inc(bulk, 1)
                    dve.wait_ge(bulk, after(5))
                    dve.tensor_tensor(diag[:, :, :], low[:, :, :], stay[:, :, :], ALU.mult).then_inc(bulk, 1)
                    dve.wait_ge(bulk, after(6))
                    dve.tensor_tensor_scan(nxt[:, :], go_left[:, 0:B * S], diag[:, :, :].rearrange("p b j -> p (b j)"), 0.0,
                                           ALU.mult, ALU.add).then_inc(bulk, 1)
                    dve.memset(entry[0:B, S - 1:S], float(S - 1)).then_inc(entry_ready, 1)
                    dve.wait_ge(steps_in, after(16))
                    iota_row = iota_j[0:B, :]

                    def lookup(n):
                        dve.wait_ge(entry_ready, after(n))
                        dve.scalar_tensor_tensor(hit[:, :], iota_row, entry[0:B, bass.ds(n * -1 + S, 1)],
                                                 chase[:, bass.ds(n * -1 + S, 1), :].rearrange("b a j -> b (a j)"),
                                                 ALU.is_equal, ALU.mult,
                                                 accum_out=entry[0:B, bass.ds(n * -1 + (S - 1), 1)]).then_inc(entry_ready, 1)

                    for n in range(1, GO):
                        lookup(n)
                    with dve.Fori(1, S // GO) as g:
                        for j in range(GO):
                            lookup(g * GO + j)
                    dve.wait_ge(entry_T, after(1))
                    dve.wait_ge(steps_out, after(16))
                    dve.tensor_tensor(low[:, :, :], iota_b, t_ps[:, 0:B].unsqueeze(2).to_broadcast([128, B, S]), ALU.is_equal).then_inc(bulk, 1)
                    dve.wait_ge(bulk, after(8))
                    dve.tensor_tensor_scan(nxt[:, ::-1], go_left[:, 1:B * S + 1][:, ::-1],
                                           low[:, :, :].rearrange("p b j -> p (b j)")[:, ::-1], 0.0, ALU.mult, ALU.add).then_inc(bulk, 1)

                @block.tensor
                def _(pe):
                    pe.wait_ge(entry_ready, after(S))
                    pe.transpose(t_ps[:, 0:128], entry[:, :], k.ident[:, :]).then_inc(entry_T, 1)


def stage_align_int8(k, x_in, path, x_out):
    nc = k.nc
    ROUND = 1.5 * 2.0 ** 23
    QMAX, QMIN, QEPS = 127.0, -128.0, 1e-6
    with ExitStack() as ctx:
        sb = lambda n, s, t=F32: ctx.enter_context(nc.sbuf_tensor("int8_" + n, s, t))
        ps = lambda n, s, t=F32: ctx.enter_context(nc.psum_tensor("int8_" + n, s, t))
        sem = lambda n: k.semaphore(ctx, "int8_" + n)
        x = [sb(f"x{u}", [128, D]) for u in range(2)]
        c = [sb(f"c{u}", [128, D]) for u in range(2)]
        p = [sb(f"p{u}", [128, S]) for u in range(2)]
        xo = [sb(f"xo{u}", [128, D]) for u in range(2)]
        w8, w = sb("w8", [128, DT, D // 4], I32), sb("w", [128, DT, D], BF16)
        w_scale, bias = sb("w_scale", [128, D]), sb("bias", [128, D])
        identb = sb("identb", [128, 128], BF16)
        ln = LayerNorm(k, ctx, "int8_ln")
        xa = sb("xa", [128, D])
        amax, scale, inv = sb("amax", [128, 1]), sb("scale", [128, 1]), sb("inv", [128, 1])
        shifted, q = sb("shifted", [128, D]), sb("q", [128, D], BF16)
        qT = sb("qT", [128, DT, S], BF16)
        scaled, biased = sb("scaled", [128, D]), sb("biased", [128, D])
        e_ps, t_ps, a_ps = ps("e_ps", [128, 512]), ps("t_ps", [128, 1024], BF16), ps("a_ps", [128, 512])
        in_loaded = [sem(f"in_loaded{u}") for u in range(2)]
        x_stored = [sem(f"x_stored{u}") for u in range(2)]
        weights_in, weights_cast, expanded, xa_ready, step, qT_ps, qT_ready, acc_done, out_step, xo_ready = map(sem, (
            "weights_in", "weights_cast", "expanded", "xa_ready", "step", "qT_ps", "qT_ready", "acc_done", "out_step", "xo_ready"))
        with nc.Block() as block:

            @block.sync
            def _(sp):
                def load(b, u):
                    sp.dma_start(x[u][:, :], x_in[b]).then_inc(in_loaded[u], 16)
                    sp.dma_start(c[u][:, :], k.ins["ctx_1024"][b]).then_inc(in_loaded[u], 16)
                    sp.dma_start(p[u][:, :], path[:, bass.ds(b, 1), :].rearrange("i a j -> i (a j)")).then_inc(in_loaded[u], 16)

                def store(b, u):
                    sp.wait_ge(xo_ready, after(b + 1))
                    sp.dma_start(x_out[b], xo[u][:, :]).then_inc(x_stored[u], 16)

                sp.dma_start(w8[:, :, :], k.ins["w_int8T"].rearrange("(t p) n -> p t n", p=128)).then_inc(weights_in, 16)
                sp.dma_start(w_scale[:, :], k.ins["L1_ffn_weight_scale"].rearrange("(a n) -> a n", a=1).to_broadcast([128, D])).then_inc(weights_in, 16)
                sp.dma_start(bias[:, :], k.ins["L1_ffn_bias"].rearrange("(a n) -> a n", a=1).to_broadcast([128, D])).then_inc(weights_in, 16)
                load(0, 0)
                load(1, 1)
                with sp.Fori(0, B // 2 - 1) as i:
                    for u in range(2):
                        b = i * 2 + u
                        store(b, u)
                        load(b + 2, u)
                for u in range(2):
                    store(B - 2 + u, u)
                for u in range(2):
                    sp.wait_ge(x_stored[u], after(16 * B // 2))

            @block.gpsimd
            def _(pool):
                k.prime(pool)
                pool.tensor_copy(identb[:, :], k.ident[:, :]).then_inc(weights_cast, 1)
                pool.wait_ge(weights_in, after(48))
                pool.tensor_copy(w[:, :, :], w8[:, :, :].bitcast(I8)).then_inc(weights_cast, 1)
                with pool.Fori(0, B) as b:
                    ln.inverse_root(pool, b)

            @block.vector
            def _(dve):
                dve.wait_ge(weights_in, after(48))
                with dve.Fori(0, B // 2) as i:
                    for u in range(2):
                        b = i * 2 + u
                        dve.wait_ge(in_loaded[u], after(i * 48 + 48))
                        dve.wait_ge(expanded, after(b + 1))
                        dve.wait_ge(xo_ready, after(b))
                        dve.scalar_tensor_tensor(xa[:, :], e_ps[:, 0:D], k.gates[:, 1:2], x[u][:, :],
                                                 ALU.mult, ALU.add).then_inc(xa_ready, 1)
                        dve.wait_ge(xa_ready, after(b + 1))
                        ln.statistics(dve, b, xa[:, :])
                        ln.normalize(dve, b, xa[:, :])
                        dve.wait_ge(ln.xn_ready, after(b + 1))
                        dve.tensor_reduce(amax[:, :], ln.xn[:, :], AX.X, ALU.max, apply_absolute_value=True).then_inc(step, 1)
                        dve.wait_ge(step, after(b * 5 + 1))
                        dve.wait_ge(out_step, after(b * 2))
                        dve.tensor_scalar(scale[:, :], amax[:, :], QEPS, 1.0 / QMAX, ALU.max, ALU.mult).then_inc(step, 1)
                        dve.wait_ge(step, after(b * 5 + 2))
                        dve.reciprocal(inv[:, :], scale[:, :]).then_inc(step, 1)
                        dve.wait_ge(step, after(b * 5 + 3))
                        dve.tensor_scalar(shifted[:, :], ln.xn[:, :], inv[:, :], ROUND, ALU.mult, ALU.add).then_inc(step, 1)
                        dve.wait_ge(step, after(b * 5 + 4))
                        dve.wait_ge(qT_ps, after(b))
                        dve.tensor_scalar(q[:, :], shifted[:, :], -ROUND, QMAX, ALU.add, ALU.min).then_inc(step, 1)
                        dve.wait_ge(qT_ps, after(b + 1))
                        dve.wait_ge(acc_done, after(b))
                        dve.tensor_scalar(qT[:, :, :], t_ps[:, 0:D].rearrange("p (t s) -> p t s", s=S), QMIN, None, ALU.max).then_inc(qT_ready, 1)
                        dve.wait_ge(acc_done, after(b + 1))
                        dve.scalar_tensor_tensor(scaled[:, :], a_ps[:, 0:D], scale[:, :], w_scale[:, :], ALU.mult, ALU.mult).then_inc(out_step, 1)
                        dve.wait_ge(out_step, after(b * 2 + 1))
                        dve.tensor_tensor(biased[:, :], scaled[:, :], bias[:, :], ALU.add).then_inc(out_step, 1)
                        dve.wait_ge(out_step, after(b * 2 + 2))
                        dve.wait_ge(x_stored[u], after(i * 16))
                        dve.scalar_tensor_tensor(xo[u][:, :], biased[:, :], k.gates[:, 5:6], xa[:, :], ALU.mult, ALU.add).then_inc(xo_ready, 1)

            @block.tensor
            def _(pe):
                pe.wait_ge(weights_cast, after(2))
                with pe.Fori(0, B // 2) as i:
                    for u in range(2):
                        b = i * 2 + u
                        pe.wait_ge(in_loaded[u], after(i * 48 + 48))
                        pe.wait_ge(xa_ready, after(b))
                        pe.matmul(e_ps[:, 0:D], p[u][:, :], c[u][:, :], start=True, stop=True).then_inc(expanded, 1)
                        pe.wait_ge(step, after(b * 5 + 5))
                        pe.wait_ge(qT_ready, after(b))
                        for t in range(DT):
                            last = pe.transpose(t_ps[:, 128 * t:128 * t + 128], q[:, 128 * t:128 * t + 128], identb[:, :])
                        last.then_inc(qT_ps, 1)
                        pe.wait_ge(qT_ready, after(b + 1))
                        pe.wait_ge(out_step, after(b * 2))
                        for t in range(DT):
                            last = pe.matmul(a_ps[:, 0:D], qT[:, t, :], w[:, t, :], start=(t == 0), stop=(t == DT - 1))
                        last.then_inc(acc_done, 1)


def sinusoid_reversed_T():
    f = np.float32
    pos = np.arange(S - 1, -1, -1, dtype=f)
    n = D // 2
    inv = np.exp(np.arange(n, dtype=f) * f(-math.log(10000.0) / (n - 1))).astype(f)
    st = (pos[:, None] * inv[None, :]).astype(f)
    return np.ascontiguousarray(np.concatenate([np.sin(st), np.cos(st)], axis=-1).astype(f).T)


def stage_attention(k, x_in, x_out, layer, gate, relative, bounce=None):
    nc = k.nc
    w = lambda n: k.ins[f"{layer}_xattn_{n}"]
    SCALE = 1.0 / math.sqrt(HD)
    with ExitStack() as ctx:
        sb = lambda n, s, t=F32: ctx.enter_context(nc.sbuf_tensor(f"{layer}_{n}", s, t))
        ps = lambda n, s, t=F32: ctx.enter_context(nc.psum_tensor(f"{layer}_{n}", s, t))
        sem = lambda n: k.semaphore(ctx, f"{layer}_{n}")
        x = [sb(f"x{u}", [128, D]) for u in range(2)]
        cT = [sb(f"cT{u}", [128, DT, S]) for u in range(2)]
        xo = [sb(f"xo{u}", [128, D]) for u in range(2)]
        wq, wk, wv, wo = (sb(n, [128, DT, D]) for n in ("wq", "wk", "wv", "wo"))
        bq, bk = sb("bq", [128, DT]), sb("bk", [128, DT])
        bv, bo = sb("bv", [1, D]), sb("bo", [1, D])
        ones = sb("ones", [1, 128])
        ln = LayerNorm(k, ctx, f"{layer}_ln")
        xnT = sb("xnT", [128, DT, S])
        qT = sb("qT", [128, DT, S])
        kz = sb("kz", [128, DT, 2, S])
        v = sb("v", [128, H, HD + 1])
        att, prob = sb("att", [128, H, S]), sb("prob", [128, H, S])
        nmax = sb("nmax", [128, H])
        pT = sb("pT", [128, H, S])
        rtotal, on, oT = sb("rtotal", [128, H]), sb("on", [128, H, HD]), sb("oT", [128, DT, S])
        if relative:
            mask = [sb(f"mask{u}", [128, S]) for u in range(2)]
            wp, sinT, bp = sb("wp", [128, DT, D]), sb("sinT", [128, DT, S]), sb("bp", [128, DT])
            rw, rr = sb("rw", [128, DT]), sb("rr", [128, DT])
            pz = sb("pz", [128, DT, 2, S])
            qrT = sb("qrT", [128, DT, S])
            rel = sb("rel", [128, S + 1, H])
            shifted = sb("shifted", [128, S, H])
            mask_s, mask_add = sb("mask_s", [128, S]), sb("mask_add", [128, S])

        a_ps = ps("a_ps", [128, 512])
        b_ps = ps("b_ps", [128, 512])
        r_ps = [ps(f"r_ps{j}", [128, 4, S]) for j in range(2)]
        s_ps = [ps(f"s_ps{j}", [128, 4, S]) for j in range(4)]
        o_view = b_ps[:, 0:H * (HD + 1)].rearrange("p (h d) -> p h d", d=HD + 1)

        N_LOADS = 3 if relative else 2
        weights_in = sem("weights_in")
        in_loaded = [sem(f"in_loaded{u}") for u in range(2)]
        x_stored = [sem(f"x_stored{u}") for u in range(2)]
        setup, pe_ps = sem("setup"), sem("pe_ps")
        xT_ps, xT_ready, qk_done, v_done, q_ready, k_ready, v_ready = map(sem, (
            "xT_ps", "xT_ready", "qk_done", "v_done", "q_ready", "k_ready", "v_ready"))
        rel_done, rel_out, rel_written, rel_read, s_done, mask_ready, att_ready, att_step, sub_ready = map(sem, (
            "rel_done", "rel_out", "rel_written", "rel_read", "s_done", "mask_ready", "att_ready", "att_step", "sub_ready"))
        max_ready, prob_ready, pT_ps, pT_ready, o_done, rt_ready, on_ready, oT_ps, oT_ready, out_done, xo_ready = map(sem, (
            "max_ready", "prob_ready", "pT_ps", "pT_ready", "o_done", "rt_ready", "on_ready", "oT_ps", "oT_ready", "out_done", "xo_ready"))
        column = lambda a: a.rearrange("(t p) -> p t", p=128)
        row = lambda a: a.rearrange("(a n) -> a n", a=1)
        pT_ready_act = sem("pT_ready_act")
        n_weights_all = 8 + (5 if relative else 0)
        n_setup = 2 + (7 if relative else 0)

        with nc.Block() as block:

            @block.sync
            def _(sp):
                def load(b, u):
                    sp.dma_start(x[u][:, :], x_in[b]).then_inc(in_loaded[u], 16)
                    sp.dma_start(cT[u][:, :, :], k.ins["ctxT_pairs"][b, 0].rearrange("(t p) s -> p t s", p=128)).then_inc(in_loaded[u], 16)
                    if relative:
                        sp.dma_start(mask[u][:, :], k.ins["mask_Bx1xSxS2_ff1"][b, 0]).then_inc(in_loaded[u], 16)

                def bounce_scores(b, u):
                    sp.wait_ge(rel_out, after(b * 4 + 4))
                    sp.dma_start(bounce[u][0:S * (S + 1) * H].rearrange("(s n) -> s n", s=S),
                                 rel[:, :, :].rearrange("p j h -> p (j h)")).then_inc(rel_written, 16)
                    sp.wait_ge(rel_written, after(b * 16 + 16))
                    sp.dma_start(shifted[:, :, :].rearrange("p j h -> p (j h)"),
                                 bounce[u][S * H:S * H + S * S * H].rearrange("(s n) -> s n", s=S)).then_inc(rel_read, 16)

                def store(b, u):
                    sp.wait_ge(xo_ready, after(b + 1))
                    sp.dma_start(x_out[b], xo[u][:, :]).then_inc(x_stored[u], 16)

                load(0, 0)
                load(1, 1)
                for tile, name in ((wq, "Wq"), (wk, "Wk"), (wv, "Wv"), (wo, "Wo")) + (((wp, "Wp"),) if relative else ()):
                    sp.dma_start(tile[:, :, :], w(name).rearrange("(t p) n -> p t n", p=128)).then_inc(weights_in, 16)
                with nc.allow_non_contiguous_dma(reason="small bias columns"):
                    sp.dma_start(bq[:, :], column(w("bq"))).then_inc(weights_in, 16)
                    sp.dma_start(bk[:, :], column(w("bk"))).then_inc(weights_in, 16)
                    if relative:
                        sp.dma_start(bp[:, :], column(w("bp"))).then_inc(weights_in, 16)
                        sp.dma_start(rw[:, :], column(w("r_w_bias").rearrange("a b h d -> (a b h d)"))).then_inc(weights_in, 16)
                        sp.dma_start(rr[:, :], column(w("r_r_bias").rearrange("a b h d -> (a b h d)"))).then_inc(weights_in, 16)
                sp.dma_start(bv[:, :], row(w("bv"))).then_inc(weights_in, 16)
                sp.dma_start(bo[:, :], row(w("bo"))).then_inc(weights_in, 16)
                if relative:
                    sp.dma_start(sinT[:, :, :], k.ins["c_sinT"].rearrange("(t p) s -> p t s", p=128)).then_inc(weights_in, 16)
                with sp.Fori(0, B // 2 - 1) as i:
                    for u in range(2):
                        b = i * 2 + u
                        if relative:
                            bounce_scores(b, u)
                        store(b, u)
                        load(b + 2, u)
                for u in range(2):
                    if relative:
                        bounce_scores(B - 2 + u, u)
                    store(B - 2 + u, u)
                for u in range(2):
                    sp.wait_ge(x_stored[u], after(16 * B // 2))

            @block.gpsimd
            def _(pool):
                k.prime(pool)
                pool.memset(ones[:, :], 1.0).then_inc(setup, 1)
                pool.memset(v[:, :, :], 1.0).then_inc(setup, 1)
                if relative:
                    pool.memset(rel[:, :, :], 0.0).then_inc(setup, 1)
                with pool.Fori(0, B) as b:
                    ln.inverse_root(pool, b)

            @block.vector
            def _(dve):
                dve.wait_ge(weights_in, after(16 * n_weights_all))
                if relative:
                    dve.tensor_tensor(rw[:, :], rw[:, :], bq[:, :], ALU.add).then_inc(setup, 1)
                    dve.tensor_tensor(rr[:, :], rr[:, :], bq[:, :], ALU.add).then_inc(setup, 1)
                    dve.wait_ge(pe_ps, after(1))
                    for t in range(DT):
                        for par in range(2):
                            dve.tensor_scalar(pz[:, t, par, :], a_ps[:, t * S:t * S + S], bp[:, t:t + 1],
                                              k.pair_mask[:, par:par + 1], ALU.add, ALU.mult).then_inc(setup, 1)
                with dve.Fori(0, B // 2) as i:
                    for u in range(2):
                        b = i * 2 + u
                        dve.wait_ge(in_loaded[u], after(i * 16 * N_LOADS + 16 * N_LOADS))
                        ln.statistics(dve, b, x[u][:, :])
                        dve.wait_ge(xT_ps, after(b))
                        ln.normalize(dve, b, x[u][:, :])
                        dve.wait_ge(q_ready, after(b + 1))
                        dve.wait_ge(s_done, after(b * 4))
                        for t in range(DT):
                            for par in range(2):
                                last = dve.tensor_scalar(kz[:, t, par, :], b_ps[:, D + t * S:D + t * S + S], bk[:, t:t + 1],
                                                         k.pair_mask[:, par:par + 1], ALU.add, ALU.mult)
                        last.then_inc(k_ready, 1)
                        if relative:
                            dve.wait_ge(att_step, after(b * 2))
                            dve.tensor_scalar(mask_s[:, :], mask[u][:, :], SCALE, None, ALU.mult)
                            dve.tensor_scalar(mask_add[:, :], mask[u][:, :], -1.0, 1.0e10, ALU.add, ALU.mult).then_inc(mask_ready, 1)
                            dve.wait_ge(rel_read, after(b * 16 + 16))
                            dve.wait_ge(prob_ready, after(b))
                            for r in range(4):
                                dve.wait_ge(s_done, after(b * 4 + (r + 1)))
                                dve.tensor_tensor(att[:, 4 * r:4 * r + 4, :], s_ps[r][:, :, :],
                                                  shifted[:, :, 4 * r:4 * r + 4].rearrange("p j h -> p h j"), ALU.add).then_inc(att_ready, 1)
                            dve.wait_ge(att_ready, after(b * 4 + 4))
                            dve.wait_ge(mask_ready, after(b + 1))
                            dve.tensor_tensor(prob[:, :, :], att[:, :, :], mask_s[:, :].unsqueeze(1).to_broadcast([128, H, S]), ALU.mult).then_inc(att_step, 1)
                            dve.wait_ge(att_step, after(b * 2 + 1))
                            dve.tensor_tensor(att[:, :, :], prob[:, :, :], mask_add[:, :].unsqueeze(1).to_broadcast([128, H, S]), ALU.add).then_inc(att_step, 1)
                            dve.wait_ge(att_step, after(b * 2 + 2))
                            dve.tensor_reduce(nmax[:, :], att[:, :, :], AX.X, ALU.max, negate=True).then_inc(max_ready, 4)
                            dve.wait_ge(max_ready, after(b * 4 + 4))
                            dve.tensor_tensor(prob[:, :, :], att[:, :, :], nmax[:, :].unsqueeze(2).to_broadcast([128, H, S]), ALU.add).then_inc(sub_ready, 4)
                        else:
                            for r in range(4):
                                heads = slice(4 * r, 4 * r + 4)
                                dve.wait_ge(s_done, after(b * 4 + (r + 1)))
                                dve.tensor_reduce(nmax[:, heads], s_ps[r][:, :, :], AX.X, ALU.max, negate=True).then_inc(max_ready, 1)
                                dve.wait_ge(max_ready, after(b * 4 + (r + 1)))
                                dve.wait_ge(pT_ps, after(b * 4))
                                dve.tensor_tensor(prob[:, heads, :], s_ps[r][:, :, :], nmax[:, heads].unsqueeze(2).to_broadcast([128, 4, S]),
                                                  ALU.add).then_inc(sub_ready, 1)
                        for g in (1, 3):
                            dve.wait_ge(pT_ps, after(b * 4 + (g + 1)))
                            dve.wait_ge(o_done, after(b))
                            dve.tensor_copy(pT[:, 4 * g:4 * g + 4, :], r_ps[1][:, :, :]).then_inc(pT_ready, 1)
                        dve.wait_ge(o_done, after(b + 1))
                        dve.reciprocal(rtotal[:, :].unsqueeze(2), o_view[:, :, HD:HD + 1]).then_inc(rt_ready, 1)
                        dve.wait_ge(rt_ready, after(b + 1))
                        dve.wait_ge(oT_ps, after(b))
                        dve.tensor_tensor(on[:, :, :], o_view[:, :, 0:HD], rtotal[:, :].unsqueeze(2).to_broadcast([128, H, HD]),
                                          ALU.mult).then_inc(on_ready, 1)
                        dve.wait_ge(out_done, after(b + 1))
                        dve.wait_ge(x_stored[u], after(i * 16))
                        dve.scalar_tensor_tensor(xo[u][:, :], a_ps[:, 0:D], k.gates[:, gate:gate + 1], x[u][:, :],
                                                 ALU.mult, ALU.add).then_inc(xo_ready, 1)

            @block.scalar
            def _(act):
                act.wait_ge(weights_in, after(16 * n_weights_all))
                if relative:
                    act.wait_ge(setup, after(n_setup))
                with act.Fori(0, B) as b:
                    act.wait_ge(xT_ps, after(b + 1))
                    act.wait_ge(qk_done, after(b))
                    act.activation(xnT[:, :, :], a_ps[:, 0:D].rearrange("p (t s) -> p t s", s=S), ACT.Copy).then_inc(xT_ready, 1)
                    act.wait_ge(qk_done, after(b + 1))
                    act.wait_ge(s_done, after(b * 4))
                    for t in range(DT):
                        if relative:
                            act.activation(qrT[:, t, :], b_ps[:, t * S:t * S + S], ACT.Identity, bias=rr[:, t:t + 1])
                        last = act.activation(qT[:, t, :], b_ps[:, t * S:t * S + S], ACT.Identity,
                                              bias=(rw if relative else bq)[:, t:t + 1])
                    last.then_inc(q_ready, 1)
                    act.wait_ge(v_done, after(b + 1))
                    act.wait_ge(o_done, after(b))
                    act.activation(v[:, :, 0:HD], a_ps[:, 0:D].rearrange("p (h d) -> p h d", d=HD), ACT.Copy).then_inc(v_ready, 1)
                    if relative:
                        act.wait_ge(rel_written, after(b * 16))
                        for r in range(4):
                            act.wait_ge(rel_done, after(b * 4 + (r + 1)))
                            act.activation(rel[:, 1:S + 1, 4 * r:4 * r + 4].rearrange("p j h -> p h j"), r_ps[r % 2][:, :, :],
                                           ACT.Copy).then_inc(rel_out, 1)
                        act.wait_ge(pT_ps, after(b * 4))
                        act.wait_ge(sub_ready, after(b * 4 + 4))
                        act.activation(att[:, :, :], prob[:, :, :], ACT.Exp).then_inc(prob_ready, 1)
                    else:
                        act.wait_ge(pT_ps, after(b * 4))
                        act.wait_ge(sub_ready, after(b * 4 + 4))
                        act.activation(att[:, :, :], prob[:, :, :], ACT.Exp, scale=SCALE).then_inc(prob_ready, 1)
                    for g in (0, 2):
                        act.wait_ge(pT_ps, after(b * 4 + (g + 1)))
                        act.wait_ge(o_done, after(b))
                        act.activation(pT[:, 4 * g:4 * g + 4, :], r_ps[0][:, :, :], ACT.Copy).then_inc(pT_ready_act, 1)
                    act.wait_ge(oT_ps, after(b + 1))
                    act.wait_ge(out_done, after(b))
                    act.activation(oT[:, :, :], a_ps[:, 0:D].rearrange("p (t s) -> p t s", s=S), ACT.Copy).then_inc(oT_ready, 1)

            @block.tensor
            def _(pe):
                pe.wait_ge(weights_in, after(16 * n_weights_all))
                if relative:
                    for m in range(DT):
                        for t in range(DT):
                            last = pe.matmul(a_ps[:, m * S:m * S + S], wp[:, t, 128 * m:128 * m + 128], sinT[:, t, :],
                                             start=(t == 0), stop=(t == DT - 1))
                    last.then_inc(pe_ps, 1)
                pe.wait_ge(setup, after(n_setup))
                with pe.Fori(0, B // 2) as i:
                    for u in range(2):
                        b = i * 2 + u
                        pe.wait_ge(ln.xn_ready, after(b + 1))
                        pe.wait_ge(xo_ready, after(b))
                        for t in range(DT):
                            last = pe.transpose(a_ps[:, 128 * t:128 * t + 128], ln.xn[:, 128 * t:128 * t + 128], k.ident[:, :])
                        last.then_inc(xT_ps, 1)
                        pe.wait_ge(in_loaded[u], after(i * 16 * N_LOADS + 16 * N_LOADS))
                        pe.wait_ge(on_ready, after(b))
                        pe.wait_ge(xT_ready, after(b + 1))
                        for off, wt, src in ((0, wq, xnT), (D, wk, cT[u])):
                            for m in range(DT):
                                for t in range(DT):
                                    last = pe.matmul(b_ps[:, off + m * S:off + m * S + S], wt[:, t, 128 * m:128 * m + 128],
                                                     src[:, t, :], start=(t == 0), stop=(t == DT - 1))
                        last.then_inc(qk_done, 1)
                        for t in range(DT):
                            pe.matmul(a_ps[:, 0:D], cT[u][:, t, :], wv[:, t, :], start=(t == 0), stop=False)
                        pe.matmul(a_ps[:, 0:D], ones[:, :], bv[:, :], start=False, stop=True).then_inc(v_done, 1)
                        pe.wait_ge(q_ready, after(b + 1))
                        if relative:
                            for r in range(4):
                                if r < 2:
                                    pe.wait_ge(pT_ready if r else pT_ready_act, after(b * 2))
                                else:
                                    pe.wait_ge(rel_out, after(b * 4 + (r - 1)))
                                rows = slice(32 * r, 32 * r + 32)
                                for half in range(2):
                                    last = pe.matmul(r_ps[r % 2][:, 2 * half:2 * half + 2, :], qrT[rows, half, :],
                                                     pz[rows, half, :, :], start=True, stop=True, tile_position=(32 * r, 0))
                                last.then_inc(rel_done, 1)
                        pe.wait_ge(k_ready, after(b + 1))
                        pe.wait_ge(att_ready if relative else sub_ready, after(b * 4))
                        for half in range(2):
                            for r in range(4):
                                rows = slice(32 * r, 32 * r + 32)
                                last = pe.matmul(s_ps[r][:, 2 * half:2 * half + 2, :], qT[rows, half, :], kz[rows, half, :, :],
                                                 start=True, stop=True, tile_position=(32 * r, 0))
                                if half:
                                    last.then_inc(s_done, 1)
                        pe.wait_ge(prob_ready, after(b + 1))
                        for g in range(4):
                            if g >= 2:
                                pe.wait_ge(pT_ready if g % 2 else pT_ready_act, after(b * 2 + 1))
                            elif relative:
                                pe.wait_ge(rel_out, after(b * 4 + 4))
                            else:
                                pe.wait_ge(pT_ready if g % 2 else pT_ready_act, after(b * 2))
                            for j in range(4):
                                last = pe.transpose(r_ps[g % 2][:, j, :], att[:, 4 * g + j, :], k.ident[:, :])
                            last.then_inc(pT_ps, 1)
                        pe.wait_ge(v_ready, after(b + 1))
                        pe.wait_ge(pT_ready, after(b * 2 + 2))
                        pe.wait_ge(pT_ready_act, after(b * 2 + 2))
                        for g in range(4):
                            for j, h in enumerate(heads_of_bank(g)):
                                last = pe.matmul(o_view[:, h, :], pT[:, 4 * g + j, :], v[:, h, :], start=True, stop=True)
                        last.then_inc(o_done, 1)
                        pe.wait_ge(on_ready, after(b + 1))
                        for t in range(DT):
                            last = pe.transpose(a_ps[:, 128 * t:128 * t + 128], on[:, 8 * t:8 * t + 8, :].rearrange("p h d -> p (h d)"), k.ident[:, :])
                        last.then_inc(oT_ps, 1)
                        pe.wait_ge(oT_ready, after(b + 1))
                        for t in range(DT):
                            pe.matmul(a_ps[:, 0:D], oT[:, t, :], wo[:, t, :], start=(t == 0), stop=False)
                        pe.matmul(a_ps[:, 0:D], ones[:, :], bo[:, :], start=False, stop=True).then_inc(out_done, 1)


FF, RANK = 1024, 64


def stage_low_rank_ffn(k, x_in, x_out):
    nc = k.nc
    FT = FF // 128
    with ExitStack() as ctx:
        sb = lambda n, s, t=F32: ctx.enter_context(nc.sbuf_tensor("lr_" + n, s, t))
        ps = lambda n, s, t=F32: ctx.enter_context(nc.psum_tensor("lr_" + n, s, t))
        sem = lambda n: k.semaphore(ctx, "lr_" + n)
        x = [sb(f"x{u}", [128, D]) for u in range(2)]
        xo = [sb(f"xo{u}", [128, D]) for u in range(2)]
        u1, v1 = sb("u1", [128, DT, RANK]), sb("v1", [RANK + 1, FF])
        u2, v2 = sb("u2", [128, FT, RANK]), sb("v2", [RANK + 1, D])
        ln = LayerNorm(k, ctx, "lr_ln")
        xnT = sb("xnT", [128, DT, S])
        p, q = sb("p", [RANK + 1, S]), sb("q", [RANK + 1, S])
        h = sb("h", [128, FT, S])
        t_ps, p_ps, q_ps, o_ps = (ps(n, [128, 512]) for n in ("t_ps", "p_ps", "q_ps", "o_ps"))
        h_ps = [ps(f"h_ps{j}", [128, 4, S]) for j in range(2)]
        weights_in = sem("weights_in")
        in_loaded = [sem(f"in_loaded{u}") for u in range(2)]
        x_stored = [sem(f"x_stored{u}") for u in range(2)]
        ones_set, xT_ps, xT_ready, p_done, p_ready, h_done, h_ready, q_done, q_ready, out_done, xo_ready = map(sem, (
            "ones_set", "xT_ps", "xT_ready", "p_done", "p_ready", "h_done", "h_ready", "q_done", "q_ready", "out_done", "xo_ready"))
        row = lambda a: a.rearrange("(a n) -> a n", a=1)
        with nc.Block() as block:

            @block.sync
            def _(sp):
                def load(b, u):
                    sp.dma_start(x[u][:, :], x_in[b]).then_inc(in_loaded[u], 16)

                def store(b, u):
                    sp.wait_ge(xo_ready, after(b + 1))
                    sp.dma_start(x_out[b], xo[u][:, :]).then_inc(x_stored[u], 16)

                load(0, 0)
                load(1, 1)
                sp.dma_start(u1[:, :, :], k.ins["L2_ffn_U1"].rearrange("(t p) n -> p t n", p=128)).then_inc(weights_in, 16)
                sp.dma_start(u2[:, :, :], k.ins["L2_ffn_U2"].rearrange("(t p) n -> p t n", p=128)).then_inc(weights_in, 16)
                sp.dma_start(v1[0:RANK, :], k.ins["L2_ffn_V1"]).then_inc(weights_in, 16)
                sp.dma_start(v1[RANK:RANK + 1, :], row(k.ins["L2_ffn_b1"])).then_inc(weights_in, 16)
                sp.dma_start(v2[0:RANK, :], k.ins["L2_ffn_V2"]).then_inc(weights_in, 16)
                sp.dma_start(v2[RANK:RANK + 1, :], row(k.ins["L2_ffn_b2"])).then_inc(weights_in, 16)
                with sp.Fori(0, B // 2 - 1) as i:
                    for u in range(2):
                        b = i * 2 + u
                        store(b, u)
                        load(b + 2, u)
                for u in range(2):
                    store(B - 2 + u, u)
                for u in range(2):
                    sp.wait_ge(x_stored[u], after(16 * B // 2))

            @block.gpsimd
            def _(pool):
                k.prime(pool)
                pool.memset(p[RANK:RANK + 1, :], 1.0).then_inc(ones_set, 1)
                pool.memset(q[RANK:RANK + 1, :], 1.0).then_inc(ones_set, 1)
                pool.wait_ge(ones_set, after(2))
                with pool.Fori(0, B) as b:
                    ln.inverse_root(pool, b)

            @block.vector
            def _(dve):
                with dve.Fori(0, B // 2) as i:
                    for u in range(2):
                        b = i * 2 + u
                        dve.wait_ge(in_loaded[u], after(i * 16 + 16))
                        ln.statistics(dve, b, x[u][:, :])
                        dve.wait_ge(xT_ps, after(b))
                        ln.normalize(dve, b, x[u][:, :])
                        dve.wait_ge(xT_ps, after(b + 1))
                        dve.wait_ge(p_done, after(b))
                        dve.tensor_copy(xnT[:, :, :], t_ps[:, 0:D].rearrange("p (t s) -> p t s", s=S)).then_inc(xT_ready, 1)
                        dve.wait_ge(p_done, after(b + 1))
                        dve.wait_ge(h_done, after(b * 2))
                        dve.tensor_copy(p[0:RANK, :], p_ps[0:RANK, 0:S]).then_inc(p_ready, 1)
                        dve.wait_ge(q_done, after(b + 1))
                        dve.wait_ge(out_done, after(b))
                        dve.tensor_copy(q[0:RANK, :], q_ps[0:RANK, 0:S]).then_inc(q_ready, 1)
                        dve.wait_ge(out_done, after(b + 1))
                        dve.wait_ge(x_stored[u], after(i * 16))
                        dve.scalar_tensor_tensor(xo[u][:, :], o_ps[:, 0:D], k.gates[:, 6:7], x[u][:, :],
                                                 ALU.mult, ALU.add).then_inc(xo_ready, 1)

            @block.scalar
            def _(act):
                with act.Fori(0, B) as b:
                    for j in range(2):
                        act.wait_ge(h_done, after(b * 2 + (j + 1)))
                        act.wait_ge(q_done, after(b))
                        act.activation(h[:, 4 * j:4 * j + 4, :], h_ps[j][:, :, :], ACT.Gelu_apprx_tanh).then_inc(h_ready, 1)

            @block.tensor
            def _(pe):
                pe.wait_ge(weights_in, after(16 * 6))
                pe.wait_ge(ones_set, after(2))
                with pe.Fori(0, B) as b:
                    pe.wait_ge(ln.xn_ready, after(b + 1))
                    pe.wait_ge(xT_ready, after(b))
                    for t in range(DT):
                        last = pe.transpose(t_ps[:, 128 * t:128 * t + 128], ln.xn[:, 128 * t:128 * t + 128], k.ident[:, :])
                    last.then_inc(xT_ps, 1)
                    pe.wait_ge(xT_ready, after(b + 1))
                    pe.wait_ge(p_ready, after(b))
                    for t in range(DT):
                        last = pe.matmul(p_ps[0:RANK, 0:S], u1[:, t, :], xnT[:, t, :], start=(t == 0), stop=(t == DT - 1))
                    last.then_inc(p_done, 1)
                    pe.wait_ge(p_ready, after(b + 1))
                    pe.wait_ge(h_ready, after(b * 2))
                    for j in range(2):
                        for m in range(4):
                            f = 4 * j + m
                            last = pe.matmul(h_ps[j][:, m, :], v1[:, 128 * f:128 * f + 128], p[:, :], start=True, stop=True)
                        last.then_inc(h_done, 1)
                    pe.wait_ge(q_ready, after(b))
                    for f in range(FT):
                        if f % 4 == 0:
                            pe.wait_ge(h_ready, after(b * 2 + (f // 4 + 1)))
                        last = pe.matmul(q_ps[0:RANK, 0:S], u2[:, f, :], h[:, f, :], start=(f == 0), stop=(f == FT - 1))
                    last.then_inc(q_done, 1)
                    pe.wait_ge(q_ready, after(b + 1))
                    pe.wait_ge(xo_ready, after(b))
                    pe.matmul(o_ps[:, 0:D], q[:, :], v2[:, :], start=True, stop=True).then_inc(out_done, 1)


HE = 128


def stage_mixture_ffn(k, x_in, x_out):
    nc = k.nc
    w = lambda n: k.ins["L3_ffn_" + n]
    NT = E + 2
    with ExitStack() as ctx:
        sb = lambda n, s, t=F32: ctx.enter_context(nc.sbuf_tensor("mix_" + n, s, t))
        ps = lambda n, s, t=F32: ctx.enter_context(nc.psum_tensor("mix_" + n, s, t))
        sem = lambda n: k.semaphore(ctx, "mix_" + n)
        x = [sb(f"x{u}", [128, D]) for u in range(2)]
        xo = [sb(f"xo{u}", [128, D]) for u in range(2)]
        w_router = sb("w_router", [128, DT, E])
        w_gate, w_up = sb("w_gate", [128, DT, E, HE]), sb("w_up", [128, DT, E, HE])
        w_sgate, w_sup = sb("w_sgate", [128, DT, D]), sb("w_sup", [128, DT, D])
        w_down = sb("w_down", [128, NT, D])
        iota_j, base_e = sb("iota_j", [128, S]), sb("base_e", [128, E])
        ln = LayerNorm(k, ctx, "mix_ln")
        xnT = sb("xnT", [128, DT, S])
        z, top, top_i, top_f = sb("z", [128, E]), sb("top", [128, 8]), sb("top_i", [128, 8], mybir.dt.uint32), sb("top_f", [128, 8])
        zs, ez, total, rtotal = sb("zs", [128, E]), sb("ez", [128, E]), sb("total", [128, 1]), sb("rtotal", [128, 1])
        first, both, coef = sb("first", [128, E]), sb("both", [128, E]), sb("coef", [128, E])
        act_g = sb("act_g", [128, NT * HE])
        hid = sb("hid", [128, NT * HE])
        hT = sb("hT", [128, NT, S])
        t_ps, o_ps = ps("t_ps", [128, 512]), ps("o_ps", [128, 512])
        g_ps = [ps(f"g_ps{j}", [128, 512]) for j in range(3)]
        u_ps = [ps(f"u_ps{j}", [128, 512]) for j in range(3)]
        weights_in = sem("weights_in")
        in_loaded = [sem(f"in_loaded{u}") for u in range(2)]
        x_stored = [sem(f"x_stored{u}") for u in range(2)]
        consts, xT_ps, xT_ready, logits, rstep, zs_ready, ez_ready, gu_done, act_ready, hid_ready, hT_ps, hT_ready, out_done, xo_ready = map(sem, (
            "consts", "xT_ps", "xT_ready", "logits", "rstep", "zs_ready", "ez_ready", "gu_done", "act_ready", "hid_ready",
            "hT_ps", "hT_ready", "out_done", "xo_ready"))
        with nc.Block() as block:

            @block.sync
            def _(sp):
                def load(b, u):
                    sp.dma_start(x[u][:, :], x_in[b]).then_inc(in_loaded[u], 16)

                def store(b, u):
                    sp.wait_ge(xo_ready, after(b + 1))
                    sp.dma_start(x_out[b], xo[u][:, :]).then_inc(x_stored[u], 16)

                load(0, 0)
                load(1, 1)
                sp.dma_start(w_router[:, :, :], w("router").rearrange("(t p) n -> p t n", p=128)).then_inc(weights_in, 16)
                for t in range(DT):
                    rows = slice(128 * t, 128 * t + 128)
                    sp.dma_start(w_gate[:, t, :, :], w("experts_gate")[:, rows, :].rearrange("e p n -> p e n")).then_inc(weights_in, 16)
                    sp.dma_start(w_up[:, t, :, :], w("experts_up")[:, rows, :].rearrange("e p n -> p e n")).then_inc(weights_in, 16)
                sp.dma_start(w_sgate[:, :, :], w("shared_gate").rearrange("(t p) n -> p t n", p=128)).then_inc(weights_in, 16)
                sp.dma_start(w_sup[:, :, :], w("shared_up").rearrange("(t p) n -> p t n", p=128)).then_inc(weights_in, 16)
                sp.dma_start(w_down[:, 0:E, :], w("experts_down").rearrange("e p n -> p e n")).then_inc(weights_in, 16)
                sp.dma_start(w_down[:, E:NT, :], w("shared_down").rearrange("(t p) n -> p t n", p=128)).then_inc(weights_in, 16)
                sp.dma_start(iota_j[:, :], k.ins["c_iota"]).then_inc(weights_in, 16)
                with sp.Fori(0, B // 2 - 1) as i:
                    for u in range(2):
                        b = i * 2 + u
                        store(b, u)
                        load(b + 2, u)
                for u in range(2):
                    store(B - 2 + u, u)
                for u in range(2):
                    sp.wait_ge(x_stored[u], after(16 * B // 2))

            @block.gpsimd
            def _(pool):
                k.prime(pool)
                pool.memset(base_e[:, :], math.e).then_inc(consts, 1)
                pool.wait_ge(consts, after(1))
                with pool.Fori(0, B) as b:
                    ln.inverse_root(pool, b)
                    pool.wait_ge(zs_ready, after(b + 1))
                    pool.wait_ge(rstep, after(b * RSTEPS))
                    pool.tensor_tensor(ez[:, :], base_e[:, :], zs[:, :], ALU.pow).then_inc(ez_ready, 1)

            @block.vector
            def _(dve):
                dve.wait_ge(weights_in, after(16 * 10))
                with dve.Fori(0, B // 2) as i:
                    for u in range(2):
                        b = i * 2 + u
                        dve.wait_ge(in_loaded[u], after(i * 16 + 16))
                        ln.statistics(dve, b, x[u][:, :])
                        dve.wait_ge(xT_ps, after(b))
                        ln.normalize(dve, b, x[u][:, :])
                        dve.wait_ge(logits, after(b + 1))
                        step = lambda n: dve.wait_ge(rstep, after(b * RSTEPS + n))
                        dve.tensor_copy(z[:, :], t_ps[:, 256:256 + E]).then_inc(rstep, 1)
                        step(1)
                        dve.memset(ln.pace[:, :], 0.0)
                        dve.max(top[:, :], z[:, :]).then_inc(rstep, 1)
                        step(2)
                        dve.memset(ln.pace[:, :], 0.0)
                        dve.max_index(top_i[:, :], top[:, :], z[:, :]).then_inc(rstep, 1)
                        dve.wait_ge(ez_ready, after(b))
                        dve.tensor_scalar(zs[:, :], z[:, :], top[:, 0:1], None, ALU.subtract).then_inc(zs_ready, 1)
                        step(3)
                        dve.tensor_copy(top_f[:, :], top_i[:, :]).then_inc(rstep, 1)
                        step(4)
                        dve.tensor_scalar(first[:, :], iota_j[:, 0:E], top_f[:, 0:1], None, ALU.is_equal).then_inc(rstep, 1)
                        step(5)
                        dve.scalar_tensor_tensor(both[:, :], iota_j[:, 0:E], top_f[:, 1:2], first[:, :], ALU.is_equal, ALU.add).then_inc(rstep, 1)
                        dve.wait_ge(ez_ready, after(b + 1))
                        dve.tensor_reduce(total[:, :], ez[:, :], AX.X, ALU.add).then_inc(rstep, 1)
                        step(7)
                        dve.reciprocal(rtotal[:, :], total[:, :]).then_inc(rstep, 1)
                        step(8)
                        dve.scalar_tensor_tensor(coef[:, :], ez[:, :], rtotal[:, :], both[:, :], ALU.mult, ALU.mult).then_inc(rstep, 1)
                        step(9)
                        for j in range(3):
                            dve.wait_ge(act_ready, after(b * 3 + (j + 1)))
                            dve.wait_ge(hT_ps, after(b * 3 + j))
                            if j < 2:
                                for e in range(4):
                                    cols = slice((4 * j + e) * HE, (4 * j + e) * HE + HE)
                                    last = dve.scalar_tensor_tensor(hid[:, cols], act_g[:, cols], coef[:, 4 * j + e:4 * j + e + 1],
                                                                    u_ps[j][:, e * HE:e * HE + HE], ALU.mult, ALU.mult)
                            else:
                                last = dve.tensor_tensor(hid[:, E * HE:], act_g[:, E * HE:], u_ps[2][:, 0:D], ALU.mult)
                            last.then_inc(hid_ready, 1)
                        dve.wait_ge(hT_ps, after(b * 3 + 2))
                        dve.wait_ge(out_done, after(b))
                        dve.tensor_copy(hT[:, 4:8, :], g_ps[1][:, :].rearrange("p (m s) -> p m s", s=S)).then_inc(hT_ready, 1)
                        dve.wait_ge(out_done, after(b + 1))
                        dve.wait_ge(x_stored[u], after(i * 16))
                        dve.scalar_tensor_tensor(xo[u][:, :], o_ps[:, 0:D], k.gates[:, 7:8], x[u][:, :],
                                                 ALU.mult, ALU.add).then_inc(xo_ready, 1)

            @block.scalar
            def _(act):
                with act.Fori(0, B) as b:
                    act.wait_ge(xT_ps, after(b + 1))
                    act.wait_ge(gu_done, after(b * 3))
                    act.activation(xnT[:, :, :], t_ps[:, 0:D].rearrange("p (t s) -> p t s", s=S), ACT.Copy).then_inc(xT_ready, 1)
                    for j in range(3):
                        act.wait_ge(gu_done, after(b * 3 + (j + 1)))
                        act.wait_ge(hid_ready, after(b * 3))
                        n = 512 if j < 2 else D
                        act.activation(act_g[:, 512 * j:512 * j + n], g_ps[j][:, 0:n], ACT.Silu).then_inc(act_ready, 1)
                    for j in (0, 2):
                        n = 4 if j < 2 else 2
                        act.wait_ge(hT_ps, after(b * 3 + (j + 1)))
                        act.wait_ge(out_done, after(b))
                        act.activation(hT[:, 4 * j:4 * j + n, :], g_ps[j][:, 0:n * S].rearrange("p (m s) -> p m s", s=S),
                                       ACT.Copy).then_inc(hT_ready, 1)

            @block.tensor
            def _(pe):
                pe.wait_ge(weights_in, after(16 * 10))
                with pe.Fori(0, B) as b:
                    pe.wait_ge(ln.xn_ready, after(b + 1))
                    pe.wait_ge(rstep, after(b * RSTEPS))
                    pe.wait_ge(xT_ready, after(b))
                    for t in range(DT):
                        last = pe.transpose(t_ps[:, 128 * t:128 * t + 128], ln.xn[:, 128 * t:128 * t + 128], k.ident[:, :])
                    last.then_inc(xT_ps, 1)
                    pe.wait_ge(xT_ready, after(b + 1))
                    for t in range(DT):
                        last = pe.matmul(t_ps[:, 256:256 + E], xnT[:, t, :], w_router[:, t, :], start=(t == 0), stop=(t == DT - 1))
                    last.then_inc(logits, 1)
                    pe.wait_ge(hT_ready, after(b * 3))
                    for j in range(3):
                        for out, wt, ws in ((g_ps[j], w_gate, w_sgate), (u_ps[j], w_up, w_sup)):
                            for t in range(DT):
                                rhs = wt[:, t, 4 * j:4 * j + 4, :] if j < 2 else ws[:, t, :]
                                last = pe.matmul(out[:, 0:512] if j < 2 else out[:, 0:D], xnT[:, t, :], rhs, start=(t == 0), stop=(t == DT - 1))
                        last.then_inc(gu_done, 1)
                    for j in range(3):
                        pe.wait_ge(hid_ready, after(b * 3 + (j + 1)))
                        for m in range(4 if j < 2 else 2):
                            c = 4 * j + m
                            last = pe.transpose(g_ps[j][:, m * S:m * S + S], hid[:, c * HE:c * HE + HE], k.ident[:, :])
                        last.then_inc(hT_ps, 1)
                    pe.wait_ge(hT_ready, after(b * 3 + 3))
                    pe.wait_ge(xo_ready, after(b))
                    for c in range(NT):
                        last = pe.matmul(o_ps[:, 0:D], hT[:, c, :], w_down[:, c, :], start=(c == 0), stop=(c == NT - 1))
                    last.then_inc(out_done, 1)


RSTEPS = 9


def build(nc, ins, out):
    k = Kernel(nc, ins, out)
    with ExitStack() as ctx:
        sb = lambda n, s, t=F32: ctx.enter_context(nc.sbuf_tensor(n, s, t))
        sem = lambda n: ctx.enter_context(nc.semaphore(n))
        k.ident = sb("ident", [128, 128])
        k.minus_half = sb("minus_half", [128, 1])
        k.eps = sb("eps", [128, 1])
        k.pair_mask = sb("pair_mask", [128, 2])
        k.gates = sb("gates", [128, 8])
        raw_gates = sb("raw_gates", [128, 8])
        setup_in, mh = sem("setup_in"), sem("minus_half_set")
        k.setup_in = setup_in
        with nc.Block() as block:
            @block.sync
            def _(sp):
                sp.dma_start(k.ident[:, :], ins["c_ident"]).then_inc(setup_in, 16)
                sp.dma_start(k.pair_mask[:, :], ins["c_pair_mask"]).then_inc(setup_in, 16)
                sp.dma_start(raw_gates[:, 0:4], ins["g_xattn"].rearrange("(a n) -> a n", a=1).to_broadcast([128, 4])).then_inc(setup_in, 16)
                sp.dma_start(raw_gates[:, 4:8], ins["g_ffn"].rearrange("(a n) -> a n", a=1).to_broadcast([128, 4])).then_inc(setup_in, 16)

            @block.gpsimd
            def _(pool):
                pool.memset(k.minus_half[:, :], -0.5).then_inc(mh, 1)
                pool.memset(k.eps[:, :], LN_EPS).then_inc(mh, 1)

            @block.scalar
            def _(act):
                act.wait_ge(setup_in, 64)
                act.activation(k.gates[:, :], raw_gates[:, :], ACT.Tanh).then_inc(mh, 1)
                act.wait_ge(mh, 3)
        def scratch(name, shape):
            return nc.dram_tensor(name, shape, F32).ap()

        def x_after(n):
            return out if n == LAYERS - 1 else scratch(f"x_after_{n}", (B, S, D))

        x = x_after(0)
        stage_retention(k, ins["x"], x)
        k.clear_semaphores()
        x, x_in = x_after(1), x
        stage_switch_attention(k, x_in, x)
        k.clear_semaphores()
        x, x_in = x_after(3), x
        dist, costs = scratch("dist", (B, S, S)), scratch("costs", (B, S + 1, S + 1))
        steps, path = scratch("steps", (B, S, S)), scratch("path", (S, B, S))
        stage_distances(k, x_in, dist)
        k.clear_semaphores()
        stage_warp(k, dist, costs, steps, path)
        k.clear_semaphores()
        stage_align_int8(k, x_in, path, x)
        k.clear_semaphores()
        x, x_in = x_after(4), x
        bounce = [scratch(f"bounce{u}", ((S * (S + 1)) * H,)) for u in range(2)]
        stage_attention(k, x_in, x, "L2", 2, True, bounce)
        k.clear_semaphores()
        x, x_in = x_after(5), x
        stage_low_rank_ffn(k, x_in, x)
        k.clear_semaphores()
        x, x_in = x_after(6), x
        stage_attention(k, x_in, x, "L3", 3, False)
        k.clear_semaphores()
        stage_mixture_ffn(k, x, out)
        k.clear_semaphores()


def kernel(**inputs):
    import numpy as _np
    import concourse.bacc as _bacc
    from concourse import mybir as _mybir
    from concourse.bass_utils import run_bass_kernel_spmd as _run

    nc = _bacc.Bacc("TRN2", target_bir_lowering=False, num_devices=1)
    arrays = {n: _np.ascontiguousarray(a) for n, a in inputs.items()}
    cT = _np.ascontiguousarray(_np.swapaxes(arrays["ctx_1024"], 1, 2))
    swapped = cT.reshape(B, D // 2, 2, S)[:, :, ::-1, :].reshape(B, D, S)
    arrays["ctxT_pairs"] = _np.ascontiguousarray(_np.stack([cT, swapped], axis=1))
    q_rot, k_rot, decay = retention_tables()
    arrays.update(c_q_rot=q_rot, c_k_rot=k_rot, c_decay=decay, c_ident=_np.eye(128, dtype=_np.float32),
                  c_pair_mask=pair_masks())
    arrays["w_value"] = _np.ascontiguousarray(arrays.pop("L0_ffn_value_experts").transpose(2, 0, 1, 3).reshape(D, E * HK))
    arrays["w_out"] = _np.ascontiguousarray(
        arrays.pop("L0_ffn_output_experts").reshape(E, HK // 128, 128, D).transpose(2, 0, 1, 3))
    arrays["c_causal"] = _np.where(_np.arange(S)[None, :] > _np.arange(S)[:, None], MASKED, 0.0).astype(_np.float32)
    arrays["c_rank"] = _np.broadcast_to(_np.arange(E, 0, -1).astype(_np.float32), (128, MH, E)).copy()
    arrays["c_spread"] = expert_spread()
    arrays["w_int8T"] = _np.ascontiguousarray(arrays.pop("L1_ffn_weight_q").T).view(_np.int32)
    arrays["c_iota"] = _np.broadcast_to(_np.arange(S, dtype=_np.float32), (128, S)).copy()
    arrays["c_sinT"] = sinusoid_reversed_T()
    feed = {f"in_{n}_dram": a for n, a in arrays.items()}
    ins = {n: nc.dram_tensor(f"in_{n}_dram", a.shape, _mybir.dt.from_np(a.dtype), kind="ExternalInput").ap()
           for n, a in arrays.items()}
    out = nc.dram_tensor("out_0_dram", (B, S, D), F32, kind="ExternalOutput").ap()
    build(nc, ins, out)
    r = _run(nc, [feed], core_ids=[0])
    return r.results[0]["out_0_dram"]
```

```python
from contextlib import ExitStack
import math

import numpy as np
import concourse.bass as bass
from concourse import mybir

ALU = mybir.AluOpType
ACT = mybir.ActivationFunctionType
AX = mybir.AxisListType
F32 = mybir.dt.float32
BF16 = mybir.dt.bfloat16
I32 = mybir.dt.int32
I8 = mybir.dt.int8


B = 16
S = 128
D = 256
DT = D // 128
H = 16
HD = D // H
LN_EPS = 1e-5
LAYERS = 8


def retention_tables():
    f = np.float32
    half = HD // 2
    base = (np.arange(0, HD, 2, dtype=f) + f(0.4 * HD)) / f(1.4 * HD)
    pos = np.arange(S, dtype=f)
    scale = (base[None, :] ** (pos / f(512.0))[:, None]).astype(f)
    inv_freq = (f(1.0) / f(10000.0) ** (np.arange(half, dtype=f) / f(half))).astype(f)
    ang = (pos[:, None] * inv_freq[None, :]).astype(f)
    sign = np.tile(np.array([-1.0, 1.0], f), half)

    def table(sc):
        cos = np.repeat(np.cos(ang).astype(f) * sc, 2, axis=-1)
        sin = np.repeat(np.sin(ang).astype(f) * sc, 2, axis=-1) * sign[None, :]
        t = np.stack([cos.T, sin.T], axis=1)
        return np.ascontiguousarray(np.tile(t, (128 // HD, 1, 1)).astype(f))

    gam = (f(1.0) - np.exp(np.linspace(math.log(1 / 32), math.log(1 / 512), H).astype(f))).astype(f)
    s, t = np.arange(S)[None, :], np.arange(S)[:, None]
    decay = np.where(s >= t, gam[:, None, None] ** np.maximum(s - t, 0).astype(f), f(0)).astype(f)
    order = [h for bank in range(4) for h in heads_of_bank(bank)]
    decay = np.ascontiguousarray(decay[order].transpose(1, 0, 2))
    return table(scale), table((f(1.0) / scale).astype(f)), decay


def heads_of_bank(bank):
    return [2 * bank, 2 * bank + 1, 2 * bank + 8, 2 * bank + 9]


def pair_masks():
    odd = (np.arange(128) // HD) % 2
    return np.stack([1 - odd, odd], axis=1).astype(np.float32)


PRIME = 16


def after(n):
    return n + PRIME


def loads(n, parity, transfers=1):
    return after(n * (8 * transfers) + (16 - 8 * parity) * transfers)


def stores(n, parity):
    return after(n * 8 + (-8 * parity))


def in_three_phases(engine, step):
    step(-1, 1, middle=False, tail=False)
    step(0, 0, tail=False)
    with engine.Fori(0, (B - 4) // 2) as i:
        step(i * 2 + 1, 1)
        step(i * 2 + 2, 0)
    step(B - 3, 1)
    step(B - 2, 0, ahead=False)
    step(B - 1, 1, ahead=False, front=False)
    step(B, 0, ahead=False, front=False, middle=False)


def in_two_phases(engine, step):
    step(-1, 1, main=False)
    with engine.Fori(0, (B - 2) // 2) as i:
        step(i * 2, 0)
        step(i * 2 + 1, 1)
    step(B - 2, 0)
    step(B - 1, 1, front=False)


class Kernel:

    def __init__(self, nc, ins, out):
        self.nc, self.ins, self.out = nc, ins, out
        self.unprimed, self.used = [], []

    def semaphore(self, ctx, name):
        s = self.nc.alloc_semaphore(name)
        self.unprimed.append(s)
        self.used.append(s)
        return s

    def clear_semaphores(self):
        numbers = sorted(s.num for s in self.used)
        with self.nc.Block() as block:
            @block.gpsimd
            def _(pool):
                first = 0
                for n in range(1, len(numbers) + 1):
                    if n == len(numbers) or numbers[n] != numbers[n - 1] + 1:
                        pool.sem_clear(range(numbers[first], numbers[n - 1] + 1))
                        first = n
        for s in self.used:
            self.nc.release_semaphore(s)
        self.used = []

    def prime(self, pool):
        for s in self.unprimed:
            pool.sem_inc(s, PRIME)
        self.unprimed = []


class LayerNorm:

    def __init__(self, k, ctx, name):
        nc = k.nc
        self.k = k
        sb = lambda n, s: ctx.enter_context(nc.sbuf_tensor(f"{name}_{n}", s, F32))
        sem = lambda n: k.semaphore(ctx, f"{name}_{n}")
        self.stats, self.mv = sb("stats", [128, 6]), sb("mv", [128, 2])
        self.ve, self.rstd, self.xn = sb("ve", [128, 1]), sb("rstd", [128, 1]), sb("xn", [128, D])
        self.pace = sb("pace", [128, 1])
        self.stats_ready, self.mv_ready, self.ve_ready = sem("stats"), sem("mean_var"), sem("var_eps")
        self.rstd_ready, self.xn_ready = sem("rstd"), sem("xn")

    def statistics(self, dve, b, x):
        dve.bn_stats(self.stats[:, :], x).then_inc(self.stats_ready, 1)
        dve.wait_ge(self.stats_ready, after(b + 1))
        dve.memset(self.pace[:, :], 0.0)
        dve.bn_aggr(self.mv[:, :], self.stats[:, :]).then_inc(self.mv_ready, 1)

    def inverse_root(self, pool, b):
        pool.wait_ge(self.mv_ready, after(b + 1))
        pool.tensor_tensor(self.ve[:, :], self.mv[:, 1:2], self.k.eps[:, :], ALU.add).then_inc(self.ve_ready, 1)
        pool.wait_ge(self.ve_ready, after(b + 1))
        pool.tensor_tensor(self.rstd[:, :], self.ve[:, :], self.k.minus_half[:, :],
                           ALU.pow).then_inc(self.rstd_ready, 1)

    def normalize(self, dve, b, x):
        dve.wait_ge(self.rstd_ready, after(b + 1))
        return dve.tensor_scalar(self.xn[:, :], x, self.mv[:, 0:1], self.rstd[:, :],
                                 ALU.subtract, ALU.mult).then_inc(self.xn_ready, 1)


def stage_retention(k, x_in, x_out):
    nc = k.nc
    with ExitStack() as ctx:
        sb = lambda n, s, t=F32: ctx.enter_context(nc.sbuf_tensor("ret_" + n, s, t))
        ps = lambda n, s, t=F32: ctx.enter_context(nc.psum_tensor("ret_" + n, s, t))
        sem = lambda n: k.semaphore(ctx, "ret_" + n)

        x = [sb(f"x{u}", [128, D]) for u in range(2)]
        res = [sb(f"res{u}", [128, D]) for u in range(2)]
        c = [sb(f"c{u}", [128, D]) for u in range(2)]
        cT = [sb(f"cT{u}", [128, 2, DT, S]) for u in range(2)]
        q_rot = sb("q_rot", [128, 2, 1, S])
        k_rot = sb("k_rot", [128, 2, 1, S])
        decay = sb("decay", [128, H, S])
        ln = LayerNorm(k, ctx, "ret_ln")
        xn = ln.xn
        xs = sb("xs", [128, D])
        q_parts = sb("q_parts", [128, 2, DT, S])
        qT = sb("qT", [128, DT, S])
        qz = sb("qz", [128, DT, 2, S])
        k_parts = sb("k_parts", [128, 2, DT, S])
        kT = [sb(f"kT{u}", [128, DT, S]) for u in range(2)]
        sc = sb("sc", [128, H, S])
        xo = [sb(f"xo{u}", [128, D]) for u in range(2)]

        q_ps = ps("q_ps", [128, 2, DT, S])
        sc_ps = [ps(f"sc_ps{r}", [128, 4, S]) for r in range(4)]
        o_ps = ps("o_ps", [128, 512])

        tables_in = sem("tables_in")
        x_loaded, cT_loaded, main_loaded = ([sem(f"{n}{u}") for u in range(2)] for n in ("x_loaded", "cT_loaded", "main_loaded"))
        out_s = [sem(f"x_stored{u}") for u in range(2)]
        xs_r = sem("xs")
        xT_r, qp_r, qT_r, qz_r = sem("xT"), sem("qp"), sem("qT"), sem("qz")
        kp_r, kT_r = sem("kp"), sem("kT")
        scps_r, sc_r, ops_r, xo_r = sem("scps"), sem("sc"), sem("ops"), sem("xo")

        with nc.Block() as block:

            @block.sync
            def _(sp):
                def load_x(n, v):
                    sp.dma_start(x[v][:, :], x_in[n]).then_inc(x_loaded[v], 16)

                def load_transposed(n, v):
                    sp.dma_start(cT[v][:, :, :, :].rearrange("p a t s -> p (a t) s"),
                                 k.ins["ctxT_pairs"][n].rearrange("a (t p) s -> p (a t) s", p=128)).then_inc(cT_loaded[v], 16)

                def load_main(n, v):
                    sp.dma_start(c[v][:, :], k.ins["ctx_1024"][n]).then_inc(main_loaded[v], 16)
                    sp.dma_start(res[v][:, :], x_in[n]).then_inc(main_loaded[v], 16)

                def step(b, u, front=True, main=True):
                    more = not isinstance(b, int) or b + 2 < B
                    if front and main and more:
                        sp.wait_ge(xs_r, after(b + 1))
                        load_x(b + 2, u)
                        sp.wait_ge(kT_r, after(b + 1))
                        load_transposed(b + 2, u)
                    if main:
                        sp.wait_ge(xo_r, after(b + 1))
                        sp.dma_start(x_out[b], xo[u][:, :]).then_inc(out_s[u], 16)
                        if more:
                            load_main(b + 2, u)

                load_x(0, 0)
                load_x(1, 1)
                sp.dma_start(q_rot[:, :, 0, :], k.ins["c_q_rot"]).then_inc(tables_in, 16)
                sp.dma_start(k_rot[:, :, 0, :], k.ins["c_k_rot"]).then_inc(tables_in, 16)
                sp.dma_start(decay[:, :, :], k.ins["c_decay"]).then_inc(tables_in, 16)
                for n in range(2):
                    load_transposed(n, n)
                    load_main(n, n)
                in_two_phases(sp, step)
                for u in range(2):
                    sp.wait_ge(out_s[u], after(16 * B // 2))

            @block.gpsimd
            def _(pool):
                def step(b, u, front=True, main=True):
                    nu = 1 - u
                    if front:
                        ln.inverse_root(pool, b + 1)
                        pool.wait_ge(cT_loaded[nu], loads(b + 1, nu))
                        pool.tensor_tensor(k_parts[:, :, :, :], cT[nu][:, :, :, :],
                                           k_rot[:, :, :, :].to_broadcast([128, 2, DT, S]), ALU.mult).then_inc(kp_r, 1)
                        pool.wait_ge(kp_r, after(b + 2))
                        pool.wait_ge(scps_r, after(b * 4))
                        pool.tensor_tensor(kT[nu][:, :, :], k_parts[:, 0], k_parts[:, 1], ALU.add).then_inc(kT_r, 1)

                k.prime(pool)
                pool.wait_ge(tables_in, after(48))
                in_two_phases(pool, step)

            @block.vector
            def _(dve):
                def step(b, u, front=True, main=True):
                    nu = 1 - u
                    if main:
                        for r in range(4):
                            dve.wait_ge(scps_r, after(b * 4 + (r + 1)))
                            dve.wait_ge(ops_r, after(b))
                            dve.tensor_tensor(sc[:, 4 * r:4 * r + 4, :], sc_ps[r][:, :, :],
                                              decay[:, 4 * r:4 * r + 4, :], ALU.mult).then_inc(sc_r, 1)
                    if front:
                        dve.wait_ge(xT_r, after(b + 2))
                        dve.tensor_tensor(q_parts[:, :, :, :], q_ps[:, :, :, :],
                                          q_rot[:, :, :, :].to_broadcast([128, 2, DT, S]), ALU.mult).then_inc(qp_r, 1)
                        dve.wait_ge(qp_r, after(b + 2))
                        dve.wait_ge(qz_r, after(b + 1))
                        dve.tensor_tensor(qT[:, :, :], q_parts[:, 0], q_parts[:, 1], ALU.add).then_inc(qT_r, 1)
                    if main:
                        if front and not (isinstance(b, int) and b + 2 >= B):
                            layer_norm(b + 2, u)
                        dve.wait_ge(ops_r, after(b + 1))
                        dve.wait_ge(out_s[u], stores(b, u))
                        dve.wait_ge(main_loaded[u], loads(b, u, 2))
                        dve.scalar_tensor_tensor(xo[u][:, :], o_ps[:, 0:D], k.gates[:, 0:1], res[u][:, :],
                                                 ALU.mult, ALU.add).then_inc(xo_r, 1)
                    else:
                        layer_norm(1, 1)

                def layer_norm(n, v):
                    dve.wait_ge(x_loaded[v], loads(n, v))
                    ln.statistics(dve, n, x[v][:, :])
                    dve.wait_ge(xT_r, after(n))
                    ln.normalize(dve, n, x[v][:, :])
                    dve.tensor_scalar(xs[:, :].rearrange("p (n two) -> p n two", two=2)[:, :, ::-1],
                                      x[v][:, :].rearrange("p (n two) -> p n two", two=2), ln.mv[:, 0:1],
                                      ln.rstd[:, :], ALU.subtract, ALU.mult).then_inc(xs_r, 1)

                layer_norm(0, 0)
                dve.wait_ge(tables_in, after(48))
                in_two_phases(dve, step)

            @block.scalar
            def _(act):
                with act.Fori(0, B) as b:
                    act.wait_ge(qT_r, after(b + 1))
                    act.wait_ge(scps_r, after(b * 4))
                    for par in range(2):
                        last = act.activation(qz[:, :, par, :], qT[:, :, :], ACT.Copy, scale=k.pair_mask[:, par:par + 1])
                    last.then_inc(qz_r, 1)

            @block.tensor
            def _(pe):
                def step(b, u, front=True, main=True):
                    nu = 1 - u
                    if front:
                        pe.wait_ge(xs_r, after(b + 2))
                        pe.wait_ge(qp_r, after(b + 1))
                        for t in range(DT):
                            pe.transpose(q_ps[:, 0, t, :], xn[:, 128 * t:128 * t + 128], k.ident[:, :])
                        for t in range(DT):
                            last = pe.transpose(q_ps[:, 1, t, :], xs[:, 128 * t:128 * t + 128], k.ident[:, :])
                        last.then_inc(xT_r, 1)
                    if main:
                        pe.wait_ge(main_loaded[u], loads(b, u, 2))
                        pe.wait_ge(xo_r, after(b))
                        for r in range(4):
                            pe.wait_ge(sc_r, after(b * 4 + (r + 1)))
                            for j, h in enumerate(heads_of_bank(r)):
                                last = pe.matmul(o_ps[:, h * HD:h * HD + HD], sc[:, 4 * r + j, :],
                                                 c[u][:, h * HD:h * HD + HD], start=True, stop=True)
                        last.then_inc(ops_r, 1)
                    if front:
                        pe.wait_ge(qz_r, after(b + 2))
                        pe.wait_ge(kT_r, after(b + 2))
                        pe.wait_ge(sc_r, after(b * 4 + 4))
                        for half in range(2):
                            for r in range(4):
                                rows = slice(32 * r, 32 * r + 32)
                                last = pe.matmul(sc_ps[r][:, 2 * half:2 * half + 2, :], kT[nu][rows, half, :],
                                                 qz[rows, half, :, :], start=True, stop=True, tile_position=(32 * r, 0))
                                if half:
                                    last.then_inc(scps_r, 1)

                in_two_phases(pe, step)


MH = 8
MD = 64
E = 8
HK = MH * MD
MASKED = -1.0e30


def expert_spread():
    t = np.zeros((E, MH, E, HK), np.float32)
    for e in range(E):
        for h in range(MH):
            t[e, h, e, h * MD:(h + 1) * MD] = 1.0
    return np.ascontiguousarray(t.reshape(E * MH, E * HK))


def stage_switch_attention(k, x_in, x_out):
    nc = k.nc
    TOP = 17.33
    with ExitStack() as ctx:
        sb = lambda n, s, t=F32: ctx.enter_context(nc.sbuf_tensor("moa_" + n, s, t))
        ps = lambda n, s, t=F32: ctx.enter_context(nc.psum_tensor("moa_" + n, s, t))
        sem = lambda n: k.semaphore(ctx, "moa_" + n)

        x = [sb(f"x{u}", [128, D]) for u in range(2)]
        xo = [sb(f"xo{u}", [128, D]) for u in range(2)]
        wq, wk, wg = sb("wq", [128, DT, HK]), sb("wk", [128, DT, HK]), sb("wg", [128, DT, MH * E])
        w_value = sb("w_value", [128, DT, E, HK])
        w_out = sb("w_out", [128, E, 4, D])
        spread_f = sb("spread_f", [E * MH, E * HK])
        spread = sb("spread", [E * MH, E * HK], BF16)
        identb = sb("identb", [128, 128], BF16)
        causal = sb("causal", [128, S])
        rank = sb("rank", [128, MH, E])
        ln = LayerNorm(k, ctx, "moa_ln")
        xnT = sb("xnT", [128, DT, S])
        qT, kT = sb("qT", [128, 4, S]), sb("kT", [128, 4, S])
        z = sb("z", [128, MH, E])
        z_top, tied, key, key_top = sb("z_top", [128, MH]), sb("tied", [128, MH, E]), sb("key", [128, MH, E]), sb("key_top", [128, MH])
        onehot = sb("onehot", [128, E, MH])
        onehot_b = sb("onehot_b", [128, 2 * E, MH], BF16)
        ohT = sb("ohT", [E * MH, S], BF16)
        eneg, gden, gate = sb("eneg", [128, MH]), sb("gden", [128, MH]), sb("gate", [128, MH])
        att = sb("att", [128, 2, 4, S])
        nmax = sb("nmax", [128, 2, 4])
        prob = sb("prob", [128, 2, 4, S])
        total = sb("total", [128, 2, 4])
        rtotal, scale_o = sb("rtotal", [128, 2, 4]), sb("scale_o", [128, MH])
        probT = sb("probT", [128, 2, 4, S])
        v_sel, v = sb("v_sel", [128, MH, MD]), sb("v", [128, MH, MD])
        og = sb("og", [128, MH, MD])
        ogT = sb("ogT", [128, 4, S])
        oe = [sb(f"oe{j}", [128, 4, S]) for j in range(2)]

        t_ps = ps("t_ps", [128, 512])
        q_ps, k_ps = ps("q_ps", [128, 512]), ps("k_ps", [128, 512])
        s_ps = [ps(f"s_ps{j}", [128, 4, S]) for j in range(2)]
        y_ps = [ps(f"y_ps{j}", [128, 4, S]) for j in range(2)]
        o_ps = ps("o_ps", [128, 512])
        oh_view = t_ps[:, 384:448].bitcast(BF16)

        weights_in = sem("weights_in")
        x_loaded = [sem(f"x_loaded{u}") for u in range(2)]
        x_stored = [sem(f"x_stored{u}") for u in range(2)]
        consts_cast = sem("consts_cast")
        xT_ps, xT_ready, logits, q_done, k_done, q_ready, k_ready = map(sem, (
            "xT_ps", "xT_ready", "logits", "q_done", "k_done", "q_ready", "k_ready"))
        s_done, att_masked, max_ready, prob_ready = map(sem, ("s_done", "att_masked", "max_ready", "prob_ready"))
        gate_step, onehot_ready, eneg_ready, gate_ready = map(sem, ("gate_step", "onehot_ready", "eneg_ready", "gate_ready"))
        y_done, y_taken, v_ready = map(sem, ("y_done", "y_taken", "v_ready"))
        ohT_ps, ohT_ready, pT_ps, pT_ready = map(sem, ("ohT_ps", "ohT_ready", "pT_ps", "pT_ready"))
        o_done, scale_step, og_ready, ogT_ps, ogT_ready = map(sem, ("o_done", "scale_step", "og_ready", "ogT_ps", "ogT_ready"))
        mask_done, oe_ready, out_done, xo_ready = map(sem, ("mask_done", "oe_ready", "out_done", "xo_ready"))

        with nc.Block() as block:

            @block.sync
            def _(sp):
                def load(b, u):
                    sp.dma_start(x[u][:, :], x_in[b]).then_inc(x_loaded[u], 16)

                def store(b, u):
                    sp.wait_ge(xo_ready, after(b + 1))
                    sp.dma_start(x_out[b], xo[u][:, :]).then_inc(x_stored[u], 16)

                load(0, 0)
                load(1, 1)
                for tile, name in ((wg, "w_gate"), (wq, "w_q"), (wk, "w_k")):
                    sp.dma_start(tile[:, :, :], k.ins["L0_ffn_" + name].rearrange("(t p) n -> p t n", p=128)).then_inc(weights_in, 16)
                sp.dma_start(causal[:, :], k.ins["c_causal"]).then_inc(weights_in, 16)
                sp.dma_start(rank[:, :, :], k.ins["c_rank"]).then_inc(weights_in, 16)
                sp.dma_start(spread_f[:, :], k.ins["c_spread"]).then_inc(weights_in, 16)
                sp.dma_start(w_value[:, :, :, :].rearrange("p t e n -> p t (e n)"), k.ins["w_value"].rearrange("(t p) n -> p t n", p=128)).then_inc(weights_in, 16)
                sp.dma_start(w_out[:, :, :, :], k.ins["w_out"]).then_inc(weights_in, 16)
                with sp.Fori(0, B // 2 - 1) as i:
                    for u in range(2):
                        b = i * 2 + u
                        store(b, u)
                        load(b + 2, u)
                for u in range(2):
                    store(B - 2 + u, u)
                for u in range(2):
                    sp.wait_ge(x_stored[u], after(16 * B // 2))

            @block.gpsimd
            def _(pool):
                k.prime(pool)
                pool.wait_ge(weights_in, after(128))
                pool.tensor_copy(spread[:, :], spread_f[:, :]).then_inc(consts_cast, 1)
                pool.tensor_copy(identb[:, :], k.ident[:, :]).then_inc(consts_cast, 1)
                pool.memset(onehot_b[:, E:2 * E, :], 0.0).then_inc(consts_cast, 1)
                with pool.Fori(0, B) as b:
                    ln.inverse_root(pool, b)

            @block.vector
            def _(dve):
                def layer_norm(n, v):
                    dve.wait_ge(x_loaded[v], loads(n, v))
                    ln.statistics(dve, n, x[v][:, :])
                    dve.wait_ge(xT_ps, after(n))
                    ln.normalize(dve, n, x[v][:, :])

                def choose_experts(n):
                    dve.wait_ge(logits, after(n + 1))
                    dve.tensor_scalar(z[:, :, :], t_ps[:, 256:320].rearrange("p (h e) -> p h e", e=E), TOP, None,
                                      ALU.min).then_inc(gate_step, 1)
                    dve.wait_ge(gate_step, after(n * 5 + 1))
                    dve.wait_ge(eneg_ready, after(n))
                    dve.tensor_reduce(z_top[:, :], z[:, :, :], AX.X, ALU.max).then_inc(gate_step, 1)
                    dve.wait_ge(gate_step, after(n * 5 + 2))
                    dve.tensor_tensor(tied[:, :, :], z[:, :, :], z_top[:, :].unsqueeze(2).to_broadcast([128, MH, E]),
                                      ALU.is_equal).then_inc(gate_step, 1)
                    dve.wait_ge(gate_step, after(n * 5 + 3))
                    dve.tensor_tensor(key[:, :, :], tied[:, :, :], rank[:, :, :], ALU.mult).then_inc(gate_step, 1)
                    dve.wait_ge(gate_step, after(n * 5 + 4))
                    dve.tensor_reduce(key_top[:, :], key[:, :, :], AX.X, ALU.max).then_inc(gate_step, 1)
                    dve.wait_ge(gate_step, after(n * 5 + 5))
                    dve.wait_ge(ohT_ps, after(n))
                    dve.wait_ge(y_taken, after(n * 8))
                    dve.tensor_tensor(onehot[:, :, :].rearrange("p e h -> p h e"), key[:, :, :],
                                      key_top[:, :].unsqueeze(2).to_broadcast([128, MH, E]), ALU.is_equal)
                    dve.tensor_tensor(onehot_b[:, 0:E, :].rearrange("p e h -> p h e"), key[:, :, :],
                                      key_top[:, :].unsqueeze(2).to_broadcast([128, MH, E]),
                                      ALU.is_equal).then_inc(onehot_ready, 1)

                def step(b, u, front=True, main=True):
                    nu = 1 - u
                    if not main:
                        layer_norm(b + 1, nu)
                        choose_experts(b + 1)
                        return
                    for j in range(2):
                        dve.wait_ge(s_done, after(b * 2 + (j + 1)))
                        dve.wait_ge(prob_ready, after(b * 8))
                        dve.tensor_tensor(att[:, j], s_ps[j][:, :, :], causal[:, :].unsqueeze(1).to_broadcast([128, 4, S]),
                                          ALU.add).then_inc(att_masked, 1)
                        dve.wait_ge(att_masked, after(b * 2 + (j + 1)))
                        dve.tensor_reduce(nmax[:, j], att[:, j], AX.X, ALU.max, negate=True).then_inc(max_ready, 1)
                    dve.wait_ge(eneg_ready, after(b + 1))
                    dve.tensor_scalar(gden[:, :], eneg[:, :], 1.0, None, ALU.add).then_inc(gate_ready, 1)
                    dve.wait_ge(gate_ready, after(b * 2 + 1))
                    dve.reciprocal(gate[:, :], gden[:, :]).then_inc(gate_ready, 1)
                    dve.wait_ge(onehot_ready, after(b + 1))
                    for e in range(1, E):
                        dve.wait_ge(y_taken, after(b * 8 + e))
                        dve.wait_ge(y_done, after(b * 8 + (e + 1)))
                        dve.memset(ln.pace[:, :], 0.0)
                        dve.copy_predicated(v_sel[:, :, :], onehot[:, e, :].bitcast(I32).unsqueeze(2).to_broadcast([128, MH, MD]),
                                            y_ps[e % 2][:, :, :].rearrange("p m (h k) -> p (m h) k", k=MD)).then_inc(y_taken, 1)
                        if e == 4 and front:
                            layer_norm(b + 1, nu)
                    dve.wait_ge(y_taken, after(b * 8 + 8))
                    dve.wait_ge(gate_ready, after(b * 2 + 2))
                    dve.wait_ge(o_done, after(b))
                    dve.tensor_tensor(v[:, :, :], v_sel[:, :, :], gate[:, :].unsqueeze(2).to_broadcast([128, MH, MD]),
                                      ALU.mult).then_inc(v_ready, 1)
                    dve.wait_ge(pT_ps, after(b * 2 + 2))
                    dve.tensor_copy(probT[:, 1], s_ps[1][:, :, :]).then_inc(pT_ready, 1)
                    dve.wait_ge(prob_ready, after(b * 8 + 8))
                    dve.reciprocal(rtotal[:, :, :], total[:, :, :]).then_inc(scale_step, 1)
                    dve.wait_ge(scale_step, after(b * 2 + 1))
                    dve.tensor_tensor(scale_o[:, :].rearrange("p (m j) -> p j m", j=2), rtotal[:, :, :],
                                      gate[:, :].rearrange("p (m j) -> p j m", j=2), ALU.mult).then_inc(scale_step, 1)
                    dve.wait_ge(scale_step, after(b * 2 + 2))
                    dve.wait_ge(o_done, after(b + 1))
                    dve.wait_ge(ogT_ps, after(b))
                    dve.tensor_tensor(og[:, :, :], o_ps[:, :].rearrange("p (h k) -> p h k", k=MD),
                                      scale_o[:, :].unsqueeze(2).to_broadcast([128, MH, MD]), ALU.mult).then_inc(og_ready, 1)
                    if front:
                        choose_experts(b + 1)
                    dve.wait_ge(ogT_ready, after(b + 1))
                    for e in range(E):
                        dve.wait_ge(mask_done, after(b * 8 + (e + 1)))
                        dve.wait_ge(out_done, after(b * 8 + (e - 1)))
                        dve.tensor_tensor(oe[e % 2][:, :, :], y_ps[e % 2][:, :, :], ogT[:, :, :],
                                          ALU.mult).then_inc(oe_ready, 1)
                    dve.wait_ge(out_done, after(b * 8 + 8))
                    dve.wait_ge(x_stored[u], stores(b, u))
                    dve.scalar_tensor_tensor(xo[u][:, :], k_ps[:, 0:D], k.gates[:, 4:5], x[u][:, :],
                                             ALU.mult, ALU.add).then_inc(xo_ready, 1)

                dve.wait_ge(weights_in, after(128))
                in_two_phases(dve, step)

            @block.scalar
            def _(act):
                def step(b, u, front=True, main=True):
                    if main:
                        act.wait_ge(v_ready, after(b))
                        act.wait_ge(y_done, after(b * 8 + 1))
                        act.activation(v_sel[:, :, :], y_ps[0][:, :, :].rearrange("p m (h k) -> p (m h) k", k=MD),
                                       ACT.Copy).then_inc(y_taken, 1)
                        act.wait_ge(pT_ps, after(b * 2))
                        act.wait_ge(scale_step, after(b * 2))
                        for j in range(2):
                            act.wait_ge(max_ready, after(b * 2 + (j + 1)))
                            for m in range(4):
                                act.activation(prob[:, j, m], att[:, j, m], ACT.Exp, bias=nmax[:, j, m:m + 1],
                                               accum_out=total[:, j, m:m + 1]).then_inc(prob_ready, 1)
                        act.wait_ge(ohT_ps, after(b + 1))
                        act.wait_ge(mask_done, after(b * 8))
                        act.activation(ohT[:, :], oh_view[0:E * MH, :], ACT.Copy).then_inc(ohT_ready, 1)
                        act.wait_ge(pT_ps, after(b * 2 + 1))
                        act.wait_ge(o_done, after(b))
                        act.activation(probT[:, 0], s_ps[0][:, :, :], ACT.Copy).then_inc(pT_ready, 1)
                    if front:
                        act.wait_ge(xT_ps, after(b + 2))
                        act.wait_ge(y_done, after(b * 8 + 8))
                        act.activation(xnT[:, :, :], t_ps[:, 0:D].rearrange("p (t s) -> p t s", t=DT), ACT.Copy).then_inc(xT_ready, 1)
                        act.wait_ge(s_done, after(b * 2 + 2))
                        act.wait_ge(k_done, after(b + 2))
                        act.activation(kT[:, :, :], k_ps[:, :].rearrange("p (m s) -> p m s", s=S), ACT.Copy).then_inc(k_ready, 1)
                        act.wait_ge(gate_step, after(b * 5 + 7))
                        act.wait_ge(gate_ready, after(b * 2 + 2))
                        act.activation(eneg[:, :], z_top[:, :], ACT.Exp, scale=-1.0).then_inc(eneg_ready, 1)
                    if main:
                        act.wait_ge(ogT_ps, after(b + 1))
                        act.wait_ge(oe_ready, after(b * 8))
                        act.activation(ogT[:, :, :], o_ps[:, :].rearrange("p (m s) -> p m s", s=S), ACT.Copy).then_inc(ogT_ready, 1)
                    if front:
                        act.wait_ge(q_done, after(b + 2))
                        act.activation(qT[:, :, :], q_ps[:, :].rearrange("p (m s) -> p m s", s=S), ACT.Copy, scale=MD ** -0.5).then_inc(q_ready, 1)

                in_two_phases(act, step)

            @block.tensor
            def _(pe):
                def project(out, wt, done):
                    for m in range(4):
                        for t in range(DT):
                            last = pe.matmul(out[:, m * S:m * S + S], wt[:, t, 128 * m:128 * m + 128], xnT[:, t, :],
                                             start=(t == 0), stop=(t == DT - 1))
                    last.then_inc(done, 1)

                def step(b, u, front=True, main=True):
                    def mask(e):
                        if e >= 2:
                            pe.wait_ge(oe_ready, after(b * 8 + (e - 1)))
                        for m in range(4):
                            last = pe.matmul(y_ps[e % 2][:, m, :], spread[:, (4 * e + m) * 128:(4 * e + m) * 128 + 128],
                                             ohT[:, :], start=True, stop=True)
                        last.then_inc(mask_done, 1)

                    if main:
                        pe.wait_ge(oe_ready, after(b * 8))
                        for e in range(E):
                            if e >= 2:
                                pe.wait_ge(y_taken, after(b * 8 + (e - 1)))
                            for t in range(DT):
                                last = pe.matmul(y_ps[e % 2][:, :, :], xnT[:, t, :], w_value[:, t, e, :],
                                                 start=(t == 0), stop=(t == DT - 1))
                            last.then_inc(y_done, 1)
                        pe.wait_ge(onehot_ready, after(b + 1))
                        pe.transpose(oh_view, onehot_b[:, :, :].rearrange("p e h -> p (e h)"), identb[:, :]).then_inc(ohT_ps, 1)
                        for j in range(2):
                            pe.wait_ge(prob_ready, after(b * 8 + (4 * j + 4)))
                            for m in range(4):
                                last = pe.transpose(s_ps[j][:, m, :], prob[:, j, m], k.ident[:, :])
                            last.then_inc(pT_ps, 1)
                    if front:
                        pe.wait_ge(ln.xn_ready, after(b + 2))
                        pe.wait_ge(ohT_ready, after(b + 1))
                        for t in range(DT):
                            last = pe.transpose(t_ps[:, 128 * t:128 * t + 128], ln.xn[:, 128 * t:128 * t + 128], k.ident[:, :])
                        last.then_inc(xT_ps, 1)
                    if main:
                        pe.wait_ge(pT_ready, after(b * 2 + 2))
                        pe.wait_ge(v_ready, after(b + 1))
                        pe.wait_ge(ogT_ready, after(b))
                        for h in range(MH):
                            last = pe.matmul(o_ps[:, h * MD:h * MD + MD], probT[:, h % 2, h // 2], v[:, h, :], start=True, stop=True)
                        last.then_inc(o_done, 1)
                        pe.wait_ge(ohT_ready, after(b + 1))
                        pe.wait_ge(y_taken, after(b * 8 + 8))
                        mask(0)
                        mask(1)
                    if front:
                        pe.wait_ge(xT_ready, after(b + 2))
                        for t in range(DT):
                            last = pe.matmul(t_ps[:, 256:320], xnT[:, t, :], wg[:, t, :], start=(t == 0), stop=(t == DT - 1))
                        last.then_inc(logits, 1)
                        pe.wait_ge(xo_ready, after(b))
                        project(k_ps, wk, k_done)
                    if main:
                        pe.wait_ge(og_ready, after(b + 1))
                        for m in range(4):
                            last = pe.transpose(o_ps[:, m * S:m * S + S], og[:, 2 * m:2 * m + 2, :].rearrange("p h k -> p (h k)"), k.ident[:, :])
                        last.then_inc(ogT_ps, 1)
                    if front:
                        pe.wait_ge(q_ready, after(b + 1))
                        project(q_ps, wq, q_done)
                        pe.wait_ge(k_ready, after(b + 2))
                    elif main:
                        pe.wait_ge(xo_ready, after(b))
                    if main:
                        for e in range(E):
                            pe.wait_ge(oe_ready, after(b * 8 + (e + 1)))
                            for m in range(4):
                                last = pe.matmul(k_ps[:, 0:D], oe[e % 2][:, m, :], w_out[:, e, m, :],
                                                 start=(e == 0 and m == 0), stop=(e == E - 1 and m == 3))
                            last.then_inc(out_done, 1)
                            if e + 2 < E:
                                mask(e + 2)
                    if front:
                        pe.wait_ge(q_ready, after(b + 2))
                        pe.wait_ge(k_ready, after(b + 2))
                        pe.wait_ge(pT_ready, after(b * 2 + 2))
                        for m in range(4):
                            for j in range(2):
                                rows = slice(64 * j, 64 * j + 64)
                                last = pe.matmul(s_ps[j][:, m, :], qT[rows, m, :], kT[rows, m, :], start=True, stop=True)
                                if m == 3:
                                    last.then_inc(s_done, 1)

                pe.wait_ge(weights_in, after(128))
                pe.wait_ge(consts_cast, after(3))
                in_two_phases(pe, step)


BIG = 1.0e30


def stage_distances(k, x_in, dist):
    nc = k.nc
    TINY = 1.0e-30
    with ExitStack() as ctx:
        sb = lambda n, s, t=F32: ctx.enter_context(nc.sbuf_tensor("dist_" + n, s, t))
        ps = lambda n, s, t=F32: ctx.enter_context(nc.psum_tensor("dist_" + n, s, t))
        sem = lambda n: k.semaphore(ctx, "dist_" + n)
        x = [sb(f"x{u}", [128, D]) for u in range(2)]
        c = [sb(f"c{u}", [128, D]) for u in range(2)]
        cT = [sb(f"cT{u}", [128, DT, S]) for u in range(2)]
        ln = LayerNorm(k, ctx, "dist_ln")
        ones = sb("ones", [128, 128])
        yT, y2T = sb("yT", [128, DT, S]), sb("y2T", [128, DT, S])
        csq, aa = sb("csq", [128, D]), sb("aa", [128, 1])
        norms, d2, root, safe, quot = (sb(n, [128, S]) for n in ("norms", "d2", "root", "safe", "quot"))
        d = [sb(f"d{u}", [128, S]) for u in range(2)]
        t_ps = ps("t_ps", [128, 512])
        ab_ps, bb_ps = ps("ab_ps", [128, 512]), ps("bb_ps", [128, 512])
        in_loaded = [sem(f"in_loaded{u}") for u in range(2)]
        d_stored = [sem(f"d_stored{u}") for u in range(2)]
        ones_set, xT_ps, yT_ready, aa_ready, products, step, root_ready, d_ready = map(sem, (
            "ones_set", "xT_ps", "yT_ready", "aa_ready", "products", "step", "root_ready", "d_ready"))
        quot_ready = sem("quot_ready")
        STEPS = 5

        with nc.Block() as block:

            @block.sync
            def _(sp):
                def load(b, u):
                    sp.dma_start(x[u][:, :], x_in[b]).then_inc(in_loaded[u], 16)
                    sp.dma_start(c[u][:, :], k.ins["ctx_1024"][b]).then_inc(in_loaded[u], 16)
                    sp.dma_start(cT[u][:, :, :], k.ins["ctxT_pairs"][b, 0].rearrange("(t p) s -> p t s", p=128)).then_inc(in_loaded[u], 16)

                def store(b, u):
                    sp.wait_ge(d_ready, after(b + 1))
                    sp.dma_start(dist[b], d[u][:, :]).then_inc(d_stored[u], 16)

                load(0, 0)
                load(1, 1)
                with sp.Fori(0, B // 2 - 1) as i:
                    for u in range(2):
                        b = i * 2 + u
                        store(b, u)
                        load(b + 2, u)
                for u in range(2):
                    store(B - 2 + u, u)
                for u in range(2):
                    sp.wait_ge(d_stored[u], after(16 * B // 2))

            @block.gpsimd
            def _(pool):
                k.prime(pool)
                pool.memset(ones[:, :], 1.0).then_inc(ones_set, 1)
                with pool.Fori(0, B) as b:
                    ln.inverse_root(pool, b)

            @block.vector
            def _(dve):
                with dve.Fori(0, B // 2) as i:
                    for u in range(2):
                        b = i * 2 + u
                        dve.wait_ge(in_loaded[u], after(i * 48 + 48))
                        ln.statistics(dve, b, x[u][:, :])
                        dve.wait_ge(xT_ps, after(b))
                        ln.normalize(dve, b, x[u][:, :])
                        dve.wait_ge(products, after(b + 1))
                        dve.wait_ge(aa_ready, after(b + 1))
                        dve.tensor_scalar(norms[:, :], bb_ps[:, 0:S], aa[:, :], None, ALU.add).then_inc(step, 1)
                        dve.wait_ge(step, after(b * STEPS + 1))
                        dve.scalar_tensor_tensor(quot[:, :], ab_ps[:, 0:S], -2.0, norms[:, :], ALU.mult, ALU.add).then_inc(step, 1)
                        dve.wait_ge(step, after(b * STEPS + 2))
                        dve.tensor_scalar(d2[:, :], quot[:, :], 0.0, None, ALU.max).then_inc(step, 1)
                        dve.wait_ge(root_ready, after(b + 1))
                        dve.tensor_scalar(quot[:, :], root[:, :], TINY, None, ALU.max).then_inc(step, 1)
                        dve.wait_ge(step, after(b * STEPS + 4))
                        dve.reciprocal(safe[:, :], quot[:, :]).then_inc(step, 1)
                        dve.wait_ge(step, after(b * STEPS + 5))
                        dve.tensor_tensor(norms[:, :], d2[:, :], safe[:, :], ALU.mult).then_inc(quot_ready, 1)
                        dve.wait_ge(quot_ready, after(b + 1))
                        dve.wait_ge(d_stored[u], after(i * 16))
                        dve.tensor_tensor(d[u][:, :], norms[:, :], root[:, :], ALU.add).then_inc(d_ready, 1)

            @block.scalar
            def _(act):
                with act.Fori(0, B // 2) as i:
                    for u in range(2):
                        b = i * 2 + u
                        act.wait_ge(in_loaded[u], after(i * 48 + 48))
                        act.wait_ge(step, after(b * STEPS))
                        act.activation(csq[:, :], c[u][:, :], ACT.Square, accum_out=aa[:, :]).then_inc(aa_ready, 1)
                        act.wait_ge(products, after(b))
                        act.wait_ge(xT_ps, after(b + 1))
                        act.activation(yT[:, :, :], t_ps[:, 0:D].rearrange("p (t s) -> p t s", s=S), ACT.Copy)
                        act.activation(y2T[:, :, :], t_ps[:, 0:D].rearrange("p (t s) -> p t s", s=S), ACT.Square).then_inc(yT_ready, 1)
                        act.wait_ge(step, after(b * STEPS + 3))
                        act.wait_ge(d_ready, after(b))
                        act.activation(root[:, :], d2[:, :], ACT.Sqrt).then_inc(root_ready, 1)

            @block.tensor
            def _(pe):
                pe.wait_ge(ones_set, after(1))
                with pe.Fori(0, B // 2) as i:
                    for u in range(2):
                        b = i * 2 + u
                        pe.wait_ge(ln.xn_ready, after(b + 1))
                        pe.wait_ge(yT_ready, after(b))
                        for t in range(DT):
                            last = pe.transpose(t_ps[:, 128 * t:128 * t + 128], ln.xn[:, 128 * t:128 * t + 128], k.ident[:, :])
                        last.then_inc(xT_ps, 1)
                        pe.wait_ge(in_loaded[u], after(i * 48 + 48))
                        pe.wait_ge(yT_ready, after(b + 1))
                        pe.wait_ge(step, after(b * STEPS))
                        for t in range(DT):
                            pe.matmul(ab_ps[:, 0:S], cT[u][:, t, :], yT[:, t, :], start=(t == 0), stop=(t == DT - 1))
                        for t in range(DT):
                            last = pe.matmul(bb_ps[:, 0:S], ones[:, :], y2T[:, t, :], start=(t == 0), stop=(t == DT - 1))
                        last.then_inc(products, 1)


def stage_warp(k, dist, costs, steps, path):
    nc = k.nc
    with ExitStack() as ctx:
        sb = lambda n, s, t=F32: ctx.enter_context(nc.sbuf_tensor("warp_" + n, s, t))
        ps = lambda n, s, t=F32: ctx.enter_context(nc.psum_tensor("warp_" + n, s, t))
        sem = lambda n: k.semaphore(ctx, "warp_" + n)
        W = S + 1
        entry = sb("entry", [128, S])
        iota_j = sb("iota_j", [128, S])
        t_ps = ps("t_ps", [128, 512])
        dist_in, big_set, zero_set, row_min, row_ready, costs_out = map(sem, ("dist_in", "big_set", "zero_set", "row_min", "row_ready", "costs_out"))
        tables_in, bulk, steps_out, steps_in, entry_ready, entry_T, onehot_ready = map(sem, (
            "tables_in", "bulk", "steps_out", "steps_in", "entry_ready", "entry_T", "onehot_ready"))
        GO = 4
        with ExitStack() as forward:
            sbf = lambda n, s, t=F32: forward.enter_context(nc.sbuf_tensor("warpf_" + n, s, t))
            dd = sbf("dd", [B, S, S])
            rr = sbf("rr", [B, S, W])
            low = [sbf(f"low{j}", [B, S]) for j in range(2)]
            zeros = sbf("zeros", [B, S])
            big = sbf("big", [B, W])
            with nc.Block() as block:
                @block.sync
                def _(sp):
                    sp.dma_start(dd[:, :, :].rearrange("b i j -> b (i j)"), dist.rearrange("b i j -> b (i j)")).then_inc(dist_in, 16)
                    sp.dma_start(iota_j[:, :], k.ins["c_iota"]).then_inc(dist_in, 16)
                    sp.wait_ge(big_set, after(2))
                    sp.dma_start(costs[:, 0, :], big[:, :]).then_inc(costs_out, 16)
                    sp.wait_ge(row_ready, after(S))
                    sp.dma_start(costs[:, 1:S + 1, :].rearrange("b i j -> b (i j)"), rr[:, :, :].rearrange("b i j -> b (i j)")).then_inc(costs_out, 16)
                    sp.wait_ge(costs_out, after(32))

                @block.gpsimd
                def _(pool):
                    k.prime(pool)
                    pool.memset(big[:, :], BIG).then_inc(big_set, 1)
                    pool.memset(rr[:, :, 0:1], BIG).then_inc(big_set, 1)
                    pool.memset(zeros[:, :], 0.0).then_inc(zero_set, 1)
                    pool.memset(entry[:, :], 0.0).then_inc(zero_set, 1)

                @block.vector
                def _(dve):
                    dve.wait_ge(dist_in, after(32))
                    dve.wait_ge(big_set, after(2))
                    dve.wait_ge(zero_set, after(2))
                    dve.tensor_tensor_scan(rr[:, 0, 1:W], dd[:, 0, :], zeros[:, :], 0.0, ALU.add, ALU.add).then_inc(row_ready, 1)

                    def row(i, j):
                        dve.wait_ge(row_ready, after(i))
                        dve.tensor_tensor(low[j][:, :], rr[:, bass.ds(i - 1, 1), 1:W].rearrange("b a j -> b (a j)"),
                                          rr[:, bass.ds(i - 1, 1), 0:S].rearrange("b a j -> b (a j)"), ALU.min).then_inc(row_min, 1)
                        dve.wait_ge(row_min, after(i))
                        dve.tensor_tensor_scan(rr[:, bass.ds(i, 1), 1:W].rearrange("b a j -> b (a j)"), low[j][:, :],
                                               dd[:, bass.ds(i, 1), :].rearrange("b a j -> b (a j)"), BIG, ALU.min, ALU.add).then_inc(row_ready, 1)

                    for i in range(1, GO):
                        row(i, i % 2)
                    with dve.Fori(1, S // GO) as g:
                        for j in range(GO):
                            row(g * GO + j, j % 2)

        with ExitStack() as bulk_ctx:
            sbb = lambda n, s, t=F32: bulk_ctx.enter_context(nc.sbuf_tensor("warpb_" + n, s, t))
            cost, above = sbb("cost", [128, B, W]), sbb("above", [128, B, W])
            low = sbb("lowb", [128, B, S])
            go_left = sbb("go_left", [128, B * S + 8])
            stay, diag = sbb("stay", [128, B, S]), sbb("diag", [128, B, S])
            nxt = sbb("nxt", [128, B * S])
            leftv = go_left[:, 0:B * S].rearrange("p (b j) -> p b j", j=S)
            chase = sbb("chase", [B, S, S])
            hit = sbb("hit", [B, S])
            with nc.Block() as block:
                @block.sync
                def _(sp):
                    sp.dma_start(cost[:, :, :], costs[:, 1:S + 1, :].rearrange("b i j -> i b j")).then_inc(tables_in, 16)
                    sp.dma_start(above[:, :, :], costs[:, 0:S, :].rearrange("b i j -> i b j")).then_inc(tables_in, 16)
                    sp.wait_ge(bulk, after(7))
                    sp.dma_start(steps.rearrange("b i j -> i b j"), nxt[:, :].rearrange("p (b j) -> p b j", j=S)).then_inc(steps_out, 16)
                    sp.wait_ge(steps_out, after(16))
                    sp.dma_start(chase[:, :, :].rearrange("b i j -> b (i j)"), steps.rearrange("b i j -> b (i j)")).then_inc(steps_in, 16)
                    sp.wait_ge(bulk, after(9))
                    sp.dma_start(path.rearrange("i b j -> i (b j)"), nxt[:, :]).then_inc(steps_out, 16)
                    sp.wait_ge(steps_out, after(32))

                @block.vector
                def _(dve):
                    iota_b = iota_j[:, :].unsqueeze(1).to_broadcast([128, B, S])
                    dve.memset(go_left[:, B * S:B * S + 8], 0.0)
                    dve.wait_ge(tables_in, after(32))
                    dve.tensor_tensor(low[:, :, :], above[:, :, 1:W], above[:, :, 0:S], ALU.min).then_inc(bulk, 1)
                    dve.tensor_tensor(diag[:, :, :], above[:, :, 0:S], above[:, :, 1:W], ALU.is_le).then_inc(bulk, 1)
                    dve.wait_ge(bulk, after(2))
                    dve.tensor_tensor(leftv, cost[:, :, 0:S], low[:, :, :], ALU.is_lt).then_inc(bulk, 1)
                    dve.tensor_tensor(stay[:, :, :], cost[:, :, 0:S], low[:, :, :], ALU.is_ge).then_inc(bulk, 1)
                    dve.wait_ge(bulk, after(4))
                    dve.tensor_tensor(low[:, :, :], iota_b, diag[:, :, :], ALU.subtract).then_inc(bulk, 1)
                    dve.wait_ge(bulk, after(5))
                    dve.tensor_tensor(diag[:, :, :], low[:, :, :], stay[:, :, :], ALU.mult).then_inc(bulk, 1)
                    dve.wait_ge(bulk, after(6))
                    dve.tensor_tensor_scan(nxt[:, :], go_left[:, 0:B * S], diag[:, :, :].rearrange("p b j -> p (b j)"), 0.0,
                                           ALU.mult, ALU.add).then_inc(bulk, 1)
                    dve.memset(entry[0:B, S - 1:S], float(S - 1)).then_inc(entry_ready, 1)
                    dve.wait_ge(steps_in, after(16))
                    iota_row = iota_j[0:B, :]

                    def lookup(n):
                        dve.wait_ge(entry_ready, after(n))
                        dve.scalar_tensor_tensor(hit[:, :], iota_row, entry[0:B, bass.ds(n * -1 + S, 1)],
                                                 chase[:, bass.ds(n * -1 + S, 1), :].rearrange("b a j -> b (a j)"),
                                                 ALU.is_equal, ALU.mult,
                                                 accum_out=entry[0:B, bass.ds(n * -1 + (S - 1), 1)]).then_inc(entry_ready, 1)

                    for n in range(1, GO):
                        lookup(n)
                    with dve.Fori(1, S // GO) as g:
                        for j in range(GO):
                            lookup(g * GO + j)
                    dve.wait_ge(entry_T, after(1))
                    dve.wait_ge(steps_out, after(16))
                    dve.tensor_tensor(low[:, :, :], iota_b, t_ps[:, 0:B].unsqueeze(2).to_broadcast([128, B, S]), ALU.is_equal).then_inc(bulk, 1)
                    dve.wait_ge(bulk, after(8))
                    dve.tensor_tensor_scan(nxt[:, ::-1], go_left[:, 1:B * S + 1][:, ::-1],
                                           low[:, :, :].rearrange("p b j -> p (b j)")[:, ::-1], 0.0, ALU.mult, ALU.add).then_inc(bulk, 1)

                @block.tensor
                def _(pe):
                    pe.wait_ge(entry_ready, after(S))
                    pe.transpose(t_ps[:, 0:128], entry[:, :], k.ident[:, :]).then_inc(entry_T, 1)


def stage_align_int8(k, x_in, path, x_out):
    nc = k.nc
    ROUND = 1.5 * 2.0 ** 23
    QMAX, QMIN, QEPS = 127.0, -128.0, 1e-6
    with ExitStack() as ctx:
        sb = lambda n, s, t=F32: ctx.enter_context(nc.sbuf_tensor("int8_" + n, s, t))
        ps = lambda n, s, t=F32: ctx.enter_context(nc.psum_tensor("int8_" + n, s, t))
        sem = lambda n: k.semaphore(ctx, "int8_" + n)
        x = [sb(f"x{u}", [128, D]) for u in range(2)]
        c = [sb(f"c{u}", [128, D]) for u in range(2)]
        p = [sb(f"p{u}", [128, S]) for u in range(2)]
        xo = [sb(f"xo{u}", [128, D]) for u in range(2)]
        w8, w = sb("w8", [128, DT, D // 4], I32), sb("w", [128, DT, D], BF16)
        w_scale, bias = sb("w_scale", [128, D]), sb("bias", [128, D])
        identb = sb("identb", [128, 128], BF16)
        ln = LayerNorm(k, ctx, "int8_ln")
        xa = sb("xa", [128, D])
        amax, scale, inv = sb("amax", [128, 1]), sb("scale", [128, 1]), sb("inv", [128, 1])
        shifted, q = sb("shifted", [128, D]), sb("q", [128, D], BF16)
        qT = sb("qT", [128, DT, S], BF16)
        scaled, biased = sb("scaled", [128, D]), sb("biased", [128, D])
        e_ps, t_ps, a_ps = ps("e_ps", [128, 512]), ps("t_ps", [128, 1024], BF16), ps("a_ps", [128, 512])
        in_loaded = [sem(f"in_loaded{u}") for u in range(2)]
        x_stored = [sem(f"x_stored{u}") for u in range(2)]
        weights_in, weights_cast, expanded, xa_ready, step, qT_ps, qT_ready, acc_done, out_step, xo_ready = map(sem, (
            "weights_in", "weights_cast", "expanded", "xa_ready", "step", "qT_ps", "qT_ready", "acc_done", "out_step", "xo_ready"))
        with nc.Block() as block:

            @block.sync
            def _(sp):
                def load(b, u):
                    sp.dma_start(x[u][:, :], x_in[b]).then_inc(in_loaded[u], 16)
                    sp.dma_start(c[u][:, :], k.ins["ctx_1024"][b]).then_inc(in_loaded[u], 16)
                    sp.dma_start(p[u][:, :], path[:, bass.ds(b, 1), :].rearrange("i a j -> i (a j)")).then_inc(in_loaded[u], 16)

                def store(b, u):
                    sp.wait_ge(xo_ready, after(b + 1))
                    sp.dma_start(x_out[b], xo[u][:, :]).then_inc(x_stored[u], 16)

                sp.dma_start(w8[:, :, :], k.ins["w_int8T"].rearrange("(t p) n -> p t n", p=128)).then_inc(weights_in, 16)
                sp.dma_start(w_scale[:, :], k.ins["L1_ffn_weight_scale"].rearrange("(a n) -> a n", a=1).to_broadcast([128, D])).then_inc(weights_in, 16)
                sp.dma_start(bias[:, :], k.ins["L1_ffn_bias"].rearrange("(a n) -> a n", a=1).to_broadcast([128, D])).then_inc(weights_in, 16)
                load(0, 0)
                load(1, 1)
                with sp.Fori(0, B // 2 - 1) as i:
                    for u in range(2):
                        b = i * 2 + u
                        store(b, u)
                        load(b + 2, u)
                for u in range(2):
                    store(B - 2 + u, u)
                for u in range(2):
                    sp.wait_ge(x_stored[u], after(16 * B // 2))

            @block.gpsimd
            def _(pool):
                k.prime(pool)
                pool.tensor_copy(identb[:, :], k.ident[:, :]).then_inc(weights_cast, 1)
                pool.wait_ge(weights_in, after(48))
                pool.tensor_copy(w[:, :, :], w8[:, :, :].bitcast(I8)).then_inc(weights_cast, 1)
                with pool.Fori(0, B) as b:
                    ln.inverse_root(pool, b)

            @block.vector
            def _(dve):
                dve.wait_ge(weights_in, after(48))
                with dve.Fori(0, B // 2) as i:
                    for u in range(2):
                        b = i * 2 + u
                        dve.wait_ge(in_loaded[u], after(i * 48 + 48))
                        dve.wait_ge(expanded, after(b + 1))
                        dve.wait_ge(xo_ready, after(b))
                        dve.scalar_tensor_tensor(xa[:, :], e_ps[:, 0:D], k.gates[:, 1:2], x[u][:, :],
                                                 ALU.mult, ALU.add).then_inc(xa_ready, 1)
                        dve.wait_ge(xa_ready, after(b + 1))
                        ln.statistics(dve, b, xa[:, :])
                        ln.normalize(dve, b, xa[:, :])
                        dve.wait_ge(ln.xn_ready, after(b + 1))
                        dve.tensor_reduce(amax[:, :], ln.xn[:, :], AX.X, ALU.max, apply_absolute_value=True).then_inc(step, 1)
                        dve.wait_ge(step, after(b * 5 + 1))
                        dve.wait_ge(out_step, after(b * 2))
                        dve.tensor_scalar(scale[:, :], amax[:, :], QEPS, 1.0 / QMAX, ALU.max, ALU.mult).then_inc(step, 1)
                        dve.wait_ge(step, after(b * 5 + 2))
                        dve.reciprocal(inv[:, :], scale[:, :]).then_inc(step, 1)
                        dve.wait_ge(step, after(b * 5 + 3))
                        dve.tensor_scalar(shifted[:, :], ln.xn[:, :], inv[:, :], ROUND, ALU.mult, ALU.add).then_inc(step, 1)
                        dve.wait_ge(step, after(b * 5 + 4))
                        dve.wait_ge(qT_ps, after(b))
                        dve.tensor_scalar(q[:, :], shifted[:, :], -ROUND, QMAX, ALU.add, ALU.min).then_inc(step, 1)
                        dve.wait_ge(qT_ps, after(b + 1))
                        dve.wait_ge(acc_done, after(b))
                        dve.tensor_scalar(qT[:, :, :], t_ps[:, 0:D].rearrange("p (t s) -> p t s", s=S), QMIN, None, ALU.max).then_inc(qT_ready, 1)
                        dve.wait_ge(acc_done, after(b + 1))
                        dve.scalar_tensor_tensor(scaled[:, :], a_ps[:, 0:D], scale[:, :], w_scale[:, :], ALU.mult, ALU.mult).then_inc(out_step, 1)
                        dve.wait_ge(out_step, after(b * 2 + 1))
                        dve.tensor_tensor(biased[:, :], scaled[:, :], bias[:, :], ALU.add).then_inc(out_step, 1)
                        dve.wait_ge(out_step, after(b * 2 + 2))
                        dve.wait_ge(x_stored[u], after(i * 16))
                        dve.scalar_tensor_tensor(xo[u][:, :], biased[:, :], k.gates[:, 5:6], xa[:, :], ALU.mult, ALU.add).then_inc(xo_ready, 1)

            @block.tensor
            def _(pe):
                pe.wait_ge(weights_cast, after(2))
                with pe.Fori(0, B // 2) as i:
                    for u in range(2):
                        b = i * 2 + u
                        pe.wait_ge(in_loaded[u], after(i * 48 + 48))
                        pe.wait_ge(xa_ready, after(b))
                        pe.matmul(e_ps[:, 0:D], p[u][:, :], c[u][:, :], start=True, stop=True).then_inc(expanded, 1)
                        pe.wait_ge(step, after(b * 5 + 5))
                        pe.wait_ge(qT_ready, after(b))
                        for t in range(DT):
                            last = pe.transpose(t_ps[:, 128 * t:128 * t + 128], q[:, 128 * t:128 * t + 128], identb[:, :])
                        last.then_inc(qT_ps, 1)
                        pe.wait_ge(qT_ready, after(b + 1))
                        pe.wait_ge(out_step, after(b * 2))
                        for t in range(DT):
                            last = pe.matmul(a_ps[:, 0:D], qT[:, t, :], w[:, t, :], start=(t == 0), stop=(t == DT - 1))
                        last.then_inc(acc_done, 1)


def sinusoid_reversed_T():
    f = np.float32
    pos = np.arange(S - 1, -1, -1, dtype=f)
    n = D // 2
    inv = np.exp(np.arange(n, dtype=f) * f(-math.log(10000.0) / (n - 1))).astype(f)
    st = (pos[:, None] * inv[None, :]).astype(f)
    return np.ascontiguousarray(np.concatenate([np.sin(st), np.cos(st)], axis=-1).astype(f).T)


def stage_attention(k, x_in, x_out, layer, gate, relative, bounce=None):
    nc = k.nc
    w = lambda n: k.ins[f"{layer}_xattn_{n}"]
    SCALE = 1.0 / math.sqrt(HD)
    with ExitStack() as ctx:
        sb = lambda n, s, t=F32: ctx.enter_context(nc.sbuf_tensor(f"{layer}_{n}", s, t))
        ps = lambda n, s, t=F32: ctx.enter_context(nc.psum_tensor(f"{layer}_{n}", s, t))
        sem = lambda n: k.semaphore(ctx, f"{layer}_{n}")
        x = [sb(f"x{u}", [128, D]) for u in range(2)]
        res = [sb(f"res{u}", [128, D]) for u in range(2)]
        cT = [sb(f"cT{u}", [128, DT, S]) for u in range(2)]
        xo = [sb(f"xo{u}", [128, D]) for u in range(2)]
        wq, wk, wv, wo = (sb(n, [128, DT, D]) for n in ("wq", "wk", "wv", "wo"))
        bq, bk = sb("bq", [128, DT]), sb("bk", [128, DT])
        bv, bo = sb("bv", [1, D]), sb("bo", [1, D])
        ones = sb("ones", [1, 128])
        ln = LayerNorm(k, ctx, f"{layer}_ln")
        xnT = sb("xnT", [128, DT, S])
        qT = sb("qT", [128, DT, S])
        kz = sb("kz", [128, DT, 2, S])
        v = sb("v", [128, 2, H, HD + 1])
        att, prob = sb("att", [128, H, S]), sb("prob", [128, H, S])
        nmax = sb("nmax", [128, H])
        pT = sb("pT", [128, H, S])
        rtotal, on, oT = sb("rtotal", [128, H]), sb("on", [128, H, HD]), sb("oT", [128, DT, S])
        if relative:
            mask = [sb(f"mask{u}", [128, S]) for u in range(2)]
            wp, sinT, bp = sb("wp", [128, DT, D]), sb("sinT", [128, DT, S]), sb("bp", [128, DT])
            rw, rr = sb("rw", [128, DT]), sb("rr", [128, DT])
            pz = sb("pz", [128, DT, 2, S])
            qrT = sb("qrT", [128, DT, S])
            rel = sb("rel", [128, S + 1, H])
            shifted = sb("shifted", [128, S, H])
            mask_s, mask_add = sb("mask_s", [128, S]), sb("mask_add", [128, S])

        a_ps = ps("a_ps", [128, 512])
        b_ps = ps("b_ps", [128, 512])
        r_ps = [ps(f"r_ps{j}", [128, 4, S]) for j in range(2)]
        s_ps = [ps(f"s_ps{j}", [128, 4, S]) for j in range(4)]
        o_view = b_ps[:, 0:H * (HD + 1)].rearrange("p (h d) -> p h d", d=HD + 1)

        weights_in = sem("weights_in")
        parity = lambda n: [sem(f"{n}{u}") for u in range(2)]
        x_loaded, res_loaded, cT_loaded, x_stored = map(parity, ("x_loaded", "res_loaded", "cT_loaded", "x_stored"))
        setup, pe_ps = sem("setup"), sem("pe_ps")
        xT_ps, xT_ready, qk_done, v_done, q_ready, k_ready, v_ready = map(sem, (
            "xT_ps", "xT_ready", "qk_done", "v_done", "q_ready", "k_ready", "v_ready"))
        s_done, max_ready, sub_ready, prob_ready, pT_ps, pT_ready, pT_ready_act = map(sem, (
            "s_done", "max_ready", "sub_ready", "prob_ready", "pT_ps", "pT_ready", "pT_ready_act"))
        o_done, rt_ready, on_ready, oT_ps, oT_ready, out_done, xo_ready = map(sem, (
            "o_done", "rt_ready", "on_ready", "oT_ps", "oT_ready", "out_done", "xo_ready"))
        if relative:
            mask_loaded = parity("mask_loaded")
            rel_done, rel_out, rel_written, rel_read, mask_ready, att_ready, att_step = map(sem, (
                "rel_done", "rel_out", "rel_written", "rel_read", "mask_ready", "att_ready", "att_step"))
        column = lambda a: a.rearrange("(t p) -> p t", p=128)
        row = lambda a: a.rearrange("(a n) -> a n", a=1)
        n_weights_all = 8 + (5 if relative else 0)
        n_setup = 2 + (7 if relative else 0)

        with nc.Block() as block:

            @block.sync
            def _(sp):
                def load_x(n, v):
                    sp.dma_start(x[v][:, :], x_in[n]).then_inc(x_loaded[v], 16)

                def load_residual(n, v):
                    sp.dma_start(res[v][:, :], x_in[n]).then_inc(res_loaded[v], 16)

                def load_context(n, v):
                    sp.dma_start(cT[v][:, :, :], k.ins["ctxT_pairs"][n, 0].rearrange("(t p) s -> p t s", p=128)).then_inc(cT_loaded[v], 16)

                def load_mask(n, v):
                    sp.dma_start(mask[v][:, :], k.ins["mask_Bx1xSxS2_ff1"][n, 0]).then_inc(mask_loaded[v], 16)

                load_x(0, 0)
                load_x(1, 1)
                for tile, name in ((wq, "Wq"), (wk, "Wk"), (wv, "Wv"), (wo, "Wo")) + (((wp, "Wp"),) if relative else ()):
                    sp.dma_start(tile[:, :, :], w(name).rearrange("(t p) n -> p t n", p=128)).then_inc(weights_in, 16)
                if relative:
                    sp.dma_start(sinT[:, :, :], k.ins["c_sinT"].rearrange("(t p) s -> p t s", p=128)).then_inc(weights_in, 16)
                with nc.allow_non_contiguous_dma(reason="small bias columns"):
                    sp.dma_start(bq[:, :], column(w("bq"))).then_inc(weights_in, 16)
                    sp.dma_start(bk[:, :], column(w("bk"))).then_inc(weights_in, 16)
                    if relative:
                        sp.dma_start(bp[:, :], column(w("bp"))).then_inc(weights_in, 16)
                        sp.dma_start(rw[:, :], column(w("r_w_bias").rearrange("a b h d -> (a b h d)"))).then_inc(weights_in, 16)
                        sp.dma_start(rr[:, :], column(w("r_r_bias").rearrange("a b h d -> (a b h d)"))).then_inc(weights_in, 16)
                sp.dma_start(bv[:, :], row(w("bv"))).then_inc(weights_in, 16)
                sp.dma_start(bo[:, :], row(w("bo"))).then_inc(weights_in, 16)
                for v_ in range(2):
                    load_context(v_, v_)
                    load_residual(v_, v_)
                    if relative:
                        load_mask(v_, v_)

                def step(b, u, ahead=True, front=True, middle=True, tail=True):
                    nu = 1 - u
                    more = not isinstance(b, int) or b + 3 < B
                    if ahead:
                        if more:
                            sp.wait_ge(ln.xn_ready, after(b + 2))
                            load_x(b + 3, nu)
                            sp.wait_ge(v_done, after(b + 2))
                            load_context(b + 3, nu)
                    if tail:
                        sp.wait_ge(xo_ready, after(b))
                        sp.dma_start(x_out[b - 1], xo[nu][:, :]).then_inc(x_stored[nu], 16)
                        if not isinstance(b, int) or b + 1 < B:
                            load_residual(b + 1, nu)
                    if front and relative:
                        sp.wait_ge(rel_out, after(b * 4 + 8))
                        sp.dma_start(bounce[nu][0:S * (S + 1) * H].rearrange("(s n) -> s n", s=S),
                                     rel[:, :, :].rearrange("p j h -> p (j h)")).then_inc(rel_written, 16)
                        sp.wait_ge(rel_written, after(b * 16 + 32))
                        sp.dma_start(shifted[:, :, :].rearrange("p j h -> p (j h)"),
                                     bounce[nu][S * H:S * H + S * S * H].rearrange("(s n) -> s n", s=S)).then_inc(rel_read, 16)
                        if ahead and more:
                            sp.wait_ge(mask_ready, after(b + 2))
                            load_mask(b + 3, nu)

                in_three_phases(sp, step)
                for u in range(2):
                    sp.wait_ge(x_stored[u], after(16 * B // 2))

            @block.gpsimd
            def _(pool):
                k.prime(pool)
                pool.memset(ones[:, :], 1.0).then_inc(setup, 1)
                pool.memset(v[:, :, :, :], 1.0).then_inc(setup, 1)
                if relative:
                    pool.memset(rel[:, :, :], 0.0).then_inc(setup, 1)
                with pool.Fori(0, B) as b:
                    ln.inverse_root(pool, b)

            @block.vector
            def _(dve):
                def layer_norm(n, v):
                    dve.wait_ge(x_loaded[v], loads(n, v))
                    ln.statistics(dve, n, x[v][:, :])
                    dve.wait_ge(xT_ps, after(n))
                    ln.normalize(dve, n, x[v][:, :])

                layer_norm(0, 0)
                dve.wait_ge(weights_in, after(16 * n_weights_all))
                if relative:
                    dve.tensor_tensor(rw[:, :], rw[:, :], bq[:, :], ALU.add).then_inc(setup, 1)
                    dve.tensor_tensor(rr[:, :], rr[:, :], bq[:, :], ALU.add).then_inc(setup, 1)
                    dve.wait_ge(pe_ps, after(1))
                    for t in range(DT):
                        for par in range(2):
                            dve.tensor_scalar(pz[:, t, par, :], a_ps[:, t * S:t * S + S], bp[:, t:t + 1],
                                              k.pair_mask[:, par:par + 1], ALU.add, ALU.mult).then_inc(setup, 1)

                def step(b, u, ahead=True, front=True, middle=True, tail=True):
                    nu = 1 - u
                    if front:
                        dve.wait_ge(q_ready, after(b + 2))
                        dve.wait_ge(s_done, after(b * 4 + 4))
                        for t in range(DT):
                            for par in range(2):
                                last = dve.tensor_scalar(kz[:, t, par, :], a_ps[:, D + t * S:D + t * S + S], bk[:, t:t + 1],
                                                         k.pair_mask[:, par:par + 1], ALU.add, ALU.mult)
                        last.then_inc(k_ready, 1)
                    if tail:
                        dve.wait_ge(out_done, after(b))
                        if front:
                            dve.wait_ge(v_ready, after(b + 2))
                        dve.wait_ge(res_loaded[nu], loads(b - 1, nu))
                        dve.wait_ge(x_stored[nu], stores(b - 1, nu))
                        dve.scalar_tensor_tensor(xo[nu][:, :], b_ps[:, D:2 * D], k.gates[:, gate:gate + 1], res[nu][:, :],
                                                 ALU.mult, ALU.add).then_inc(xo_ready, 1)
                    if ahead:
                        layer_norm(b + 2, u)
                    if front and relative:
                        dve.wait_ge(mask_loaded[nu], loads(b + 1, nu))
                        dve.wait_ge(att_step, after(b * 2 + 2))
                        dve.tensor_scalar(mask_s[:, :], mask[nu][:, :], SCALE, None, ALU.mult)
                        dve.tensor_scalar(mask_add[:, :], mask[nu][:, :], -1.0, 1.0e10, ALU.add, ALU.mult).then_inc(mask_ready, 1)
                    if middle:
                        for g in (1, 3):
                            dve.wait_ge(pT_ps, after(b * 4 + (g + 1)))
                            dve.wait_ge(o_done, after(b))
                            dve.tensor_copy(pT[:, 4 * g:4 * g + 4, :], r_ps[1][:, :, :]).then_inc(pT_ready, 1)
                    if front and relative:
                        dve.wait_ge(rel_read, after(b * 16 + 32))
                        dve.wait_ge(pT_ps, after(b * 4 + 4))
                        for r in range(4):
                            dve.wait_ge(s_done, after(b * 4 + (r + 5)))
                            dve.tensor_tensor(att[:, 4 * r:4 * r + 4, :], s_ps[r][:, :, :],
                                              shifted[:, :, 4 * r:4 * r + 4].rearrange("p j h -> p h j"), ALU.add).then_inc(att_ready, 1)
                        dve.wait_ge(att_ready, after(b * 4 + 8))
                        dve.wait_ge(mask_ready, after(b + 2))
                        dve.wait_ge(prob_ready, after(b + 1))
                        dve.tensor_tensor(prob[:, :, :], att[:, :, :], mask_s[:, :].unsqueeze(1).to_broadcast([128, H, S]), ALU.mult).then_inc(att_step, 1)
                        dve.wait_ge(att_step, after(b * 2 + 3))
                        dve.tensor_tensor(att[:, :, :], prob[:, :, :], mask_add[:, :].unsqueeze(1).to_broadcast([128, H, S]), ALU.add).then_inc(att_step, 1)
                    if front and not relative:
                        for r in range(4):
                            heads = slice(4 * r, 4 * r + 4)
                            dve.wait_ge(s_done, after(b * 4 + (r + 5)))
                            dve.tensor_reduce(nmax[:, heads], s_ps[r][:, :, :], AX.X, ALU.max, negate=True).then_inc(max_ready, 1)
                            dve.wait_ge(max_ready, after(b * 4 + (r + 5)))
                            dve.wait_ge(prob_ready, after(b + 1))
                            dve.tensor_tensor(prob[:, heads, :], s_ps[r][:, :, :], nmax[:, heads].unsqueeze(2).to_broadcast([128, 4, S]),
                                              ALU.add).then_inc(sub_ready, 1)
                    if middle:
                        dve.wait_ge(o_done, after(b + 1))
                        dve.reciprocal(rtotal[:, :].unsqueeze(2), o_view[:, :, HD:HD + 1]).then_inc(rt_ready, 1)
                        dve.wait_ge(rt_ready, after(b + 1))
                        dve.wait_ge(oT_ps, after(b))
                        dve.tensor_tensor(on[:, :, :], o_view[:, :, 0:HD], rtotal[:, :].unsqueeze(2).to_broadcast([128, H, HD]),
                                          ALU.mult).then_inc(on_ready, 1)
                    if front and relative:
                        dve.wait_ge(att_step, after(b * 2 + 4))
                        dve.tensor_reduce(nmax[:, :], att[:, :, :], AX.X, ALU.max, negate=True).then_inc(max_ready, 4)
                        dve.wait_ge(max_ready, after(b * 4 + 8))
                        dve.tensor_tensor(prob[:, :, :], att[:, :, :], nmax[:, :].unsqueeze(2).to_broadcast([128, H, S]), ALU.add).then_inc(sub_ready, 4)

                in_three_phases(dve, step)

            @block.scalar
            def _(act):
                act.wait_ge(weights_in, after(16 * n_weights_all))
                if relative:
                    act.wait_ge(setup, after(n_setup))

                def step(b, u, ahead=True, front=True, middle=True, tail=True):
                    nu = 1 - u
                    if front:
                        act.wait_ge(xT_ps, after(b + 2))
                        act.wait_ge(qk_done, after(b + 1))
                        act.activation(xnT[:, :, :], a_ps[:, 0:D].rearrange("p (t s) -> p t s", s=S), ACT.Copy).then_inc(xT_ready, 1)
                    if tail:
                        act.wait_ge(oT_ps, after(b))
                        act.wait_ge(out_done, after(b - 1))
                        act.activation(oT[:, :, :], b_ps[:, 0:D].rearrange("p (t s) -> p t s", s=S), ACT.Copy).then_inc(oT_ready, 1)
                    if front:
                        act.wait_ge(qk_done, after(b + 2))
                        act.wait_ge(s_done, after(b * 4 + 4))
                        for t in range(DT):
                            if relative:
                                act.activation(qrT[:, t, :], a_ps[:, t * S:t * S + S], ACT.Identity, bias=rr[:, t:t + 1])
                            last = act.activation(qT[:, t, :], a_ps[:, t * S:t * S + S], ACT.Identity,
                                                  bias=(rw if relative else bq)[:, t:t + 1])
                        last.then_inc(q_ready, 1)
                        if tail:
                            act.wait_ge(out_done, after(b))
                        act.wait_ge(v_done, after(b + 2))
                        act.activation(v[:, nu, :, 0:HD], b_ps[:, 0:D].rearrange("p (h d) -> p h d", d=HD), ACT.Copy).then_inc(v_ready, 1)
                        if relative:
                            act.wait_ge(rel_written, after(b * 16 + 16))
                            act.wait_ge(att_ready, after(b * 4 + 4))
                            for r in range(4):
                                act.wait_ge(rel_done, after(b * 4 + (r + 5)))
                                act.activation(rel[:, 1:S + 1, 4 * r:4 * r + 4].rearrange("p j h -> p h j"), r_ps[r % 2][:, :, :],
                                               ACT.Copy).then_inc(rel_out, 1)
                    if middle:
                        act.wait_ge(pT_ps, after(b * 4))
                        act.wait_ge(sub_ready, after(b * 4 + 4))
                        act.activation(att[:, :, :], prob[:, :, :], ACT.Exp, scale=1.0 if relative else SCALE).then_inc(prob_ready, 1)
                        for g in (0, 2):
                            act.wait_ge(pT_ps, after(b * 4 + (g + 1)))
                            act.wait_ge(o_done, after(b))
                            act.activation(pT[:, 4 * g:4 * g + 4, :], r_ps[0][:, :, :], ACT.Copy).then_inc(pT_ready_act, 1)

                in_three_phases(act, step)

            @block.tensor
            def _(pe):
                pe.wait_ge(weights_in, after(16 * n_weights_all))
                if relative:
                    for m in range(DT):
                        for t in range(DT):
                            last = pe.matmul(a_ps[:, m * S:m * S + S], wp[:, t, 128 * m:128 * m + 128], sinT[:, t, :],
                                             start=(t == 0), stop=(t == DT - 1))
                    last.then_inc(pe_ps, 1)
                pe.wait_ge(setup, after(n_setup))

                def step(b, u, ahead=True, front=True, middle=True, tail=True):
                    nu = 1 - u
                    if front:
                        pe.wait_ge(ln.xn_ready, after(b + 2))
                        pe.wait_ge(k_ready, after(b + 1))
                        for t in range(DT):
                            last = pe.transpose(a_ps[:, 128 * t:128 * t + 128], ln.xn[:, 128 * t:128 * t + 128], k.ident[:, :])
                        last.then_inc(xT_ps, 1)
                    if tail:
                        pe.wait_ge(on_ready, after(b))
                        for t in range(DT):
                            last = pe.transpose(b_ps[:, 128 * t:128 * t + 128], on[:, 8 * t:8 * t + 8, :].rearrange("p h d -> p (h d)"), k.ident[:, :])
                        last.then_inc(oT_ps, 1)
                    if front:
                        pe.wait_ge(cT_loaded[nu], loads(b + 1, nu))
                        pe.wait_ge(xT_ready, after(b + 2))
                        for off, wt, src in ((0, wq, xnT), (D, wk, cT[nu])):
                            for m in range(DT):
                                for t in range(DT):
                                    last = pe.matmul(a_ps[:, off + m * S:off + m * S + S], wt[:, t, 128 * m:128 * m + 128],
                                                     src[:, t, :], start=(t == 0), stop=(t == DT - 1))
                        last.then_inc(qk_done, 1)
                        if tail:
                            pe.wait_ge(oT_ready, after(b))
                        elif middle:
                            pe.wait_ge(v_ready, after(b + 1))
                        for t in range(DT):
                            pe.matmul(b_ps[:, 0:D], cT[nu][:, t, :], wv[:, t, :], start=(t == 0), stop=False)
                        pe.matmul(b_ps[:, 0:D], ones[:, :], bv[:, :], start=False, stop=True).then_inc(v_done, 1)
                    if tail:
                        pe.wait_ge(oT_ready, after(b))
                        for t in range(DT):
                            pe.matmul(b_ps[:, D:2 * D], oT[:, t, :], wo[:, t, :], start=(t == 0), stop=False)
                        pe.matmul(b_ps[:, D:2 * D], ones[:, :], bo[:, :], start=False, stop=True).then_inc(out_done, 1)
                    if front:
                        pe.wait_ge(q_ready, after(b + 2))
                        if relative:
                            for r in range(4):
                                if r < 2:
                                    pe.wait_ge(pT_ready if r else pT_ready_act, after(b * 2))
                                else:
                                    pe.wait_ge(rel_out, after(b * 4 + (r + 3)))
                                rows = slice(32 * r, 32 * r + 32)
                                for half in range(2):
                                    last = pe.matmul(r_ps[r % 2][:, 2 * half:2 * half + 2, :], qrT[rows, half, :],
                                                     pz[rows, half, :, :], start=True, stop=True, tile_position=(32 * r, 0))
                                last.then_inc(rel_done, 1)
                        pe.wait_ge(k_ready, after(b + 2))
                        pe.wait_ge(att_ready if relative else sub_ready, after(b * 4 + 4))
                        for half in range(2):
                            for r in range(4):
                                rows = slice(32 * r, 32 * r + 32)
                                last = pe.matmul(s_ps[r][:, 2 * half:2 * half + 2, :], qT[rows, half, :], kz[rows, half, :, :],
                                                 start=True, stop=True, tile_position=(32 * r, 0))
                                if half:
                                    last.then_inc(s_done, 1)
                    if middle:
                        pe.wait_ge(prob_ready, after(b + 1))
                        for g in range(4):
                            if g >= 2:
                                pe.wait_ge(pT_ready if g % 2 else pT_ready_act, after(b * 2 + 1))
                            elif relative:
                                pe.wait_ge(rel_out, after(b * 4 + 8) if front else after(B * 4))
                            else:
                                pe.wait_ge(pT_ready if g % 2 else pT_ready_act, after(b * 2))
                            for j in range(4):
                                last = pe.transpose(r_ps[g % 2][:, j, :], att[:, 4 * g + j, :], k.ident[:, :])
                            last.then_inc(pT_ps, 1)
                        if front:
                            pe.wait_ge(v_ready, after(b + 2))
                        if tail:
                            pe.wait_ge(xo_ready, after(b))
                        pe.wait_ge(pT_ready, after(b * 2 + 2))
                        pe.wait_ge(pT_ready_act, after(b * 2 + 2))
                        for g in range(4):
                            for j, h in enumerate(heads_of_bank(g)):
                                last = pe.matmul(o_view[:, h, :], pT[:, 4 * g + j, :], v[:, u, h, :], start=True, stop=True)
                        last.then_inc(o_done, 1)

                in_three_phases(pe, step)


FF, RANK = 1024, 64


def stage_low_rank_ffn(k, x_in, x_out):
    nc = k.nc
    FT = FF // 128
    with ExitStack() as ctx:
        sb = lambda n, s, t=F32: ctx.enter_context(nc.sbuf_tensor("lr_" + n, s, t))
        ps = lambda n, s, t=F32: ctx.enter_context(nc.psum_tensor("lr_" + n, s, t))
        sem = lambda n: k.semaphore(ctx, "lr_" + n)
        x = [sb(f"x{u}", [128, D]) for u in range(2)]
        xo = [sb(f"xo{u}", [128, D]) for u in range(2)]
        res = [sb(f"res{u}", [128, D]) for u in range(2)]
        u1, v1 = sb("u1", [128, DT, RANK]), sb("v1", [RANK + 1, FF])
        u2, v2 = sb("u2", [128, FT, RANK]), sb("v2", [RANK + 1, D])
        ln = LayerNorm(k, ctx, "lr_ln")
        xnT = sb("xnT", [128, DT, S])
        p, q = sb("p", [RANK + 1, S]), sb("q", [RANK + 1, S])
        h = sb("h", [128, FT, S])
        t_ps, p_ps, q_ps, o_ps = (ps(n, [128, 512]) for n in ("t_ps", "p_ps", "q_ps", "o_ps"))
        h_ps = [ps(f"h_ps{j}", [128, 4, S]) for j in range(2)]
        weights_in = sem("weights_in")
        x_loaded, res_loaded, x_stored = ([sem(f"{n}{u}") for u in range(2)] for n in ("x_loaded", "res_loaded", "x_stored"))
        ones_set, xT_ps, xT_ready, p_done, p_ready, h_done, h_ready, q_done, q_ready, out_done, xo_ready = map(sem, (
            "ones_set", "xT_ps", "xT_ready", "p_done", "p_ready", "h_done", "h_ready", "q_done", "q_ready", "out_done", "xo_ready"))
        row = lambda a: a.rearrange("(a n) -> a n", a=1)
        with nc.Block() as block:

            @block.sync
            def _(sp):
                def load_x(n, v):
                    sp.dma_start(x[v][:, :], x_in[n]).then_inc(x_loaded[v], 16)

                def load_residual(n, v):
                    sp.dma_start(res[v][:, :], x_in[n]).then_inc(res_loaded[v], 16)

                load_x(0, 0)
                load_x(1, 1)
                sp.dma_start(u1[:, :, :], k.ins["L2_ffn_U1"].rearrange("(t p) n -> p t n", p=128)).then_inc(weights_in, 16)
                sp.dma_start(u2[:, :, :], k.ins["L2_ffn_U2"].rearrange("(t p) n -> p t n", p=128)).then_inc(weights_in, 16)
                sp.dma_start(v1[0:RANK, :], k.ins["L2_ffn_V1"]).then_inc(weights_in, 16)
                sp.dma_start(v1[RANK:RANK + 1, :], row(k.ins["L2_ffn_b1"])).then_inc(weights_in, 16)
                sp.dma_start(v2[0:RANK, :], k.ins["L2_ffn_V2"]).then_inc(weights_in, 16)
                sp.dma_start(v2[RANK:RANK + 1, :], row(k.ins["L2_ffn_b2"])).then_inc(weights_in, 16)
                load_residual(0, 0)
                load_residual(1, 1)

                def step(b, u, ahead=True, front=True, middle=True, tail=True):
                    nu = 1 - u
                    more = not isinstance(b, int) or b + 3 < B
                    if ahead and more:
                        sp.wait_ge(ln.xn_ready, after(b + 2))
                        load_x(b + 3, nu)
                    if tail:
                        sp.wait_ge(xo_ready, after(b))
                        sp.dma_start(x_out[b - 1], xo[nu][:, :]).then_inc(x_stored[nu], 16)
                        if not isinstance(b, int) or b + 1 < B:
                            load_residual(b + 1, nu)

                in_three_phases(sp, step)
                for u in range(2):
                    sp.wait_ge(x_stored[u], after(16 * B // 2))

            @block.gpsimd
            def _(pool):
                k.prime(pool)
                pool.memset(p[RANK:RANK + 1, :], 1.0).then_inc(ones_set, 1)
                pool.memset(q[RANK:RANK + 1, :], 1.0).then_inc(ones_set, 1)
                pool.wait_ge(ones_set, after(2))
                with pool.Fori(0, B) as b:
                    ln.inverse_root(pool, b)

            @block.vector
            def _(dve):
                def layer_norm(n, v):
                    dve.wait_ge(x_loaded[v], loads(n, v))
                    ln.statistics(dve, n, x[v][:, :])
                    dve.wait_ge(xT_ps, after(n))
                    ln.normalize(dve, n, x[v][:, :])

                def step(b, u, ahead=True, front=True, middle=True, tail=True):
                    nu = 1 - u
                    if front:
                        dve.wait_ge(xT_ps, after(b + 2))
                        dve.wait_ge(p_done, after(b + 1))
                        dve.tensor_copy(xnT[:, :, :], t_ps[:, 0:D].rearrange("p (t s) -> p t s", s=S)).then_inc(xT_ready, 1)
                    if ahead:
                        layer_norm(b + 2, u)
                    if front:
                        dve.wait_ge(p_done, after(b + 2))
                        dve.wait_ge(h_done, after(b * 2 + 2))
                        dve.tensor_copy(p[0:RANK, :], p_ps[0:RANK, 0:S]).then_inc(p_ready, 1)
                    if tail:
                        dve.wait_ge(out_done, after(b))
                        dve.wait_ge(res_loaded[nu], loads(b - 1, nu))
                        dve.wait_ge(x_stored[nu], stores(b - 1, nu))
                        dve.scalar_tensor_tensor(xo[nu][:, :], o_ps[:, 0:D], k.gates[:, 6:7], res[nu][:, :],
                                                 ALU.mult, ALU.add).then_inc(xo_ready, 1)
                    if middle:
                        dve.wait_ge(q_done, after(b + 1))
                        dve.wait_ge(out_done, after(b))
                        dve.tensor_copy(q[0:RANK, :], q_ps[0:RANK, 0:S]).then_inc(q_ready, 1)

                layer_norm(0, 0)
                in_three_phases(dve, step)

            @block.scalar
            def _(act):
                with act.Fori(0, B) as b:
                    for j in range(2):
                        act.wait_ge(h_done, after(b * 2 + (j + 1)))
                        act.wait_ge(q_done, after(b))
                        act.activation(h[:, 4 * j:4 * j + 4, :], h_ps[j][:, :, :], ACT.Gelu_apprx_tanh).then_inc(h_ready, 1)

            @block.tensor
            def _(pe):
                def step(b, u, ahead=True, front=True, middle=True, tail=True):
                    if front:
                        pe.wait_ge(ln.xn_ready, after(b + 2))
                        pe.wait_ge(xT_ready, after(b + 1))
                        for t in range(DT):
                            last = pe.transpose(t_ps[:, 128 * t:128 * t + 128], ln.xn[:, 128 * t:128 * t + 128], k.ident[:, :])
                        last.then_inc(xT_ps, 1)
                    if middle:
                        pe.wait_ge(p_ready, after(b + 1))
                        pe.wait_ge(h_ready, after(b * 2))
                        for j in range(2):
                            for m in range(4):
                                f = 4 * j + m
                                last = pe.matmul(h_ps[j][:, m, :], v1[:, 128 * f:128 * f + 128], p[:, :], start=True, stop=True)
                            last.then_inc(h_done, 1)
                    if front:
                        pe.wait_ge(xT_ready, after(b + 2))
                        pe.wait_ge(p_ready, after(b + 1))
                        for t in range(DT):
                            last = pe.matmul(p_ps[0:RANK, 0:S], u1[:, t, :], xnT[:, t, :], start=(t == 0), stop=(t == DT - 1))
                        last.then_inc(p_done, 1)
                    if tail:
                        pe.wait_ge(q_ready, after(b))
                        pe.wait_ge(xo_ready, after(b - 1))
                        pe.matmul(o_ps[:, 0:D], q[:, :], v2[:, :], start=True, stop=True).then_inc(out_done, 1)
                    if middle:
                        pe.wait_ge(q_ready, after(b))
                        for f in range(FT):
                            if f % 4 == 0:
                                pe.wait_ge(h_ready, after(b * 2 + (f // 4 + 1)))
                            last = pe.matmul(q_ps[0:RANK, 0:S], u2[:, f, :], h[:, f, :], start=(f == 0), stop=(f == FT - 1))
                        last.then_inc(q_done, 1)

                pe.wait_ge(weights_in, after(16 * 6))
                pe.wait_ge(ones_set, after(2))
                in_three_phases(pe, step)


HE = 128


def stage_mixture_ffn(k, x_in, x_out):
    nc = k.nc
    w = lambda n: k.ins["L3_ffn_" + n]
    NT = E + 2
    with ExitStack() as ctx:
        sb = lambda n, s, t=F32: ctx.enter_context(nc.sbuf_tensor("mix_" + n, s, t))
        ps = lambda n, s, t=F32: ctx.enter_context(nc.psum_tensor("mix_" + n, s, t))
        sem = lambda n: k.semaphore(ctx, "mix_" + n)
        x = [sb(f"x{u}", [128, D]) for u in range(2)]
        xo = [sb(f"xo{u}", [128, D]) for u in range(2)]
        w_router = sb("w_router", [128, DT, E])
        w_gate, w_up = sb("w_gate", [128, DT, E, HE]), sb("w_up", [128, DT, E, HE])
        w_sgate, w_sup = sb("w_sgate", [128, DT, D]), sb("w_sup", [128, DT, D])
        w_down = sb("w_down", [128, NT, D])
        iota_j, base_e = sb("iota_j", [128, S]), sb("base_e", [128, E])
        ln = LayerNorm(k, ctx, "mix_ln")
        xnT = sb("xnT", [128, DT, S])
        z, top, top_i, top_f = sb("z", [128, E]), sb("top", [128, 8]), sb("top_i", [128, 8], mybir.dt.uint32), sb("top_f", [128, 8])
        zs, ez, total, rtotal = sb("zs", [128, E]), sb("ez", [128, E]), sb("total", [128, 1]), sb("rtotal", [128, 1])
        first, both, coef = sb("first", [128, E]), sb("both", [128, E]), sb("coef", [128, E])
        act_g = sb("act_g", [128, NT * HE])
        hid = sb("hid", [128, NT * HE])
        hT = sb("hT", [128, NT, S])
        t_ps, o_ps = ps("t_ps", [128, 512]), ps("o_ps", [128, 512])
        g_ps = [ps(f"g_ps{j}", [128, 512]) for j in range(3)]
        u_ps = [ps(f"u_ps{j}", [128, 512]) for j in range(3)]
        weights_in, iota_in = sem("weights_in"), sem("iota_in")
        in_loaded = [sem(f"in_loaded{u}") for u in range(2)]
        x_stored = [sem(f"x_stored{u}") for u in range(2)]
        consts, xT_ps, xT_ready, logits, rstep, zs_ready, ez_ready, gu_done, act_ready, hid_ready, hT_ps, hT_ready, out_done, xo_ready = map(sem, (
            "consts", "xT_ps", "xT_ready", "logits", "rstep", "zs_ready", "ez_ready", "gu_done", "act_ready", "hid_ready",
            "hT_ps", "hT_ready", "out_done", "xo_ready"))
        with nc.Block() as block:

            @block.sync
            def _(sp):
                def load(b, u):
                    sp.dma_start(x[u][:, :], x_in[b]).then_inc(in_loaded[u], 16)

                def store(b, u):
                    sp.wait_ge(xo_ready, after(b + 1))
                    sp.dma_start(x_out[b], xo[u][:, :]).then_inc(x_stored[u], 16)

                load(0, 0)
                load(1, 1)
                sp.dma_start(iota_j[:, :], k.ins["c_iota"]).then_inc(iota_in, 16)
                sp.dma_start(w_router[:, :, :], w("router").rearrange("(t p) n -> p t n", p=128)).then_inc(weights_in, 16)
                for t in range(DT):
                    rows = slice(128 * t, 128 * t + 128)
                    sp.dma_start(w_gate[:, t, :, :], w("experts_gate")[:, rows, :].rearrange("e p n -> p e n")).then_inc(weights_in, 16)
                    sp.dma_start(w_up[:, t, :, :], w("experts_up")[:, rows, :].rearrange("e p n -> p e n")).then_inc(weights_in, 16)
                sp.dma_start(w_sgate[:, :, :], w("shared_gate").rearrange("(t p) n -> p t n", p=128)).then_inc(weights_in, 16)
                sp.dma_start(w_sup[:, :, :], w("shared_up").rearrange("(t p) n -> p t n", p=128)).then_inc(weights_in, 16)
                sp.dma_start(w_down[:, 0:E, :], w("experts_down").rearrange("e p n -> p e n")).then_inc(weights_in, 16)
                sp.dma_start(w_down[:, E:NT, :], w("shared_down").rearrange("(t p) n -> p t n", p=128)).then_inc(weights_in, 16)
                with sp.Fori(0, B // 2 - 1) as i:
                    for u in range(2):
                        b = i * 2 + u
                        store(b, u)
                        load(b + 2, u)
                for u in range(2):
                    store(B - 2 + u, u)
                for u in range(2):
                    sp.wait_ge(x_stored[u], after(16 * B // 2))

            @block.gpsimd
            def _(pool):
                k.prime(pool)
                pool.memset(base_e[:, :], math.e).then_inc(consts, 1)
                pool.wait_ge(consts, after(1))
                with pool.Fori(0, B) as b:
                    ln.inverse_root(pool, b)
                    pool.wait_ge(zs_ready, after(b + 1))
                    pool.wait_ge(rstep, after(b * RSTEPS))
                    pool.tensor_tensor(ez[:, :], base_e[:, :], zs[:, :], ALU.pow).then_inc(ez_ready, 1)

            @block.vector
            def _(dve):
                def layer_norm(n, v):
                    dve.wait_ge(in_loaded[v], loads(n, v))
                    ln.statistics(dve, n, x[v][:, :])
                    dve.wait_ge(xT_ps, after(n))
                    ln.normalize(dve, n, x[v][:, :])

                def router(n):
                    dve.wait_ge(logits, after(n + 1))
                    step = lambda m: dve.wait_ge(rstep, after(n * RSTEPS + m))
                    dve.tensor_copy(z[:, :], t_ps[:, 256:256 + E]).then_inc(rstep, 1)
                    step(1)
                    dve.memset(ln.pace[:, :], 0.0)
                    dve.max(top[:, :], z[:, :]).then_inc(rstep, 1)
                    step(2)
                    dve.memset(ln.pace[:, :], 0.0)
                    dve.max_index(top_i[:, :], top[:, :], z[:, :]).then_inc(rstep, 1)
                    dve.wait_ge(ez_ready, after(n))
                    dve.tensor_scalar(zs[:, :], z[:, :], top[:, 0:1], None, ALU.subtract).then_inc(zs_ready, 1)
                    step(3)
                    dve.tensor_copy(top_f[:, :], top_i[:, :]).then_inc(rstep, 1)
                    step(4)
                    dve.tensor_scalar(first[:, :], iota_j[:, 0:E], top_f[:, 0:1], None, ALU.is_equal).then_inc(rstep, 1)
                    step(5)
                    dve.scalar_tensor_tensor(both[:, :], iota_j[:, 0:E], top_f[:, 1:2], first[:, :], ALU.is_equal, ALU.add).then_inc(rstep, 1)
                    dve.wait_ge(ez_ready, after(n + 1))
                    dve.tensor_reduce(total[:, :], ez[:, :], AX.X, ALU.add).then_inc(rstep, 1)
                    step(7)
                    dve.reciprocal(rtotal[:, :], total[:, :]).then_inc(rstep, 1)
                    step(8)
                    dve.wait_ge(hid_ready, after(n * 3))
                    dve.scalar_tensor_tensor(coef[:, :], ez[:, :], rtotal[:, :], both[:, :], ALU.mult, ALU.mult).then_inc(rstep, 1)

                def step(b, u, front=True, main=True):
                    nu = 1 - u
                    if not main:
                        layer_norm(b + 1, nu)
                        router(b + 1)
                        return
                    dve.wait_ge(rstep, after(b * RSTEPS + 9))
                    for j in range(3):
                        dve.wait_ge(act_ready, after(b * 3 + (j + 1)))
                        dve.wait_ge(hT_ps, after(b * 3 + j))
                        if j < 2:
                            for e in range(4):
                                cols = slice((4 * j + e) * HE, (4 * j + e) * HE + HE)
                                last = dve.scalar_tensor_tensor(hid[:, cols], act_g[:, cols], coef[:, 4 * j + e:4 * j + e + 1],
                                                                u_ps[j][:, e * HE:e * HE + HE], ALU.mult, ALU.mult)
                        else:
                            last = dve.tensor_tensor(hid[:, E * HE:], act_g[:, E * HE:], u_ps[2][:, 0:D], ALU.mult)
                        last.then_inc(hid_ready, 1)
                        if j == 0 and front:
                            layer_norm(b + 1, nu)
                    dve.wait_ge(hT_ps, after(b * 3 + 2))
                    dve.wait_ge(out_done, after(b))
                    dve.tensor_copy(hT[:, 4:8, :], g_ps[1][:, :].rearrange("p (m s) -> p m s", s=S)).then_inc(hT_ready, 1)
                    if front:
                        router(b + 1)
                    dve.wait_ge(out_done, after(b + 1))
                    dve.wait_ge(x_stored[u], stores(b, u))
                    dve.scalar_tensor_tensor(xo[u][:, :], o_ps[:, 0:D], k.gates[:, 7:8], x[u][:, :],
                                             ALU.mult, ALU.add).then_inc(xo_ready, 1)

                dve.wait_ge(iota_in, after(16))
                in_two_phases(dve, step)

            @block.scalar
            def _(act):
                def step(b, u, front=True, main=True):
                    if main:
                        for j in range(3):
                            act.wait_ge(gu_done, after(b * 3 + (j + 1)))
                            act.wait_ge(hid_ready, after(b * 3))
                            n = 512 if j < 2 else D
                            act.activation(act_g[:, 512 * j:512 * j + n], g_ps[j][:, 0:n], ACT.Silu).then_inc(act_ready, 1)
                    if front:
                        act.wait_ge(xT_ps, after(b + 2))
                        act.wait_ge(gu_done, after(b * 3 + 3))
                        act.activation(xnT[:, :, :], t_ps[:, 0:D].rearrange("p (t s) -> p t s", s=S), ACT.Copy).then_inc(xT_ready, 1)
                    if main:
                        for j in (0, 2):
                            n = 4 if j < 2 else 2
                            act.wait_ge(hT_ps, after(b * 3 + (j + 1)))
                            act.wait_ge(out_done, after(b))
                            act.activation(hT[:, 4 * j:4 * j + n, :], g_ps[j][:, 0:n * S].rearrange("p (m s) -> p m s", s=S),
                                           ACT.Copy).then_inc(hT_ready, 1)

                in_two_phases(act, step)

            @block.tensor
            def _(pe):
                def step(b, u, front=True, main=True):
                    if main:
                        pe.wait_ge(xT_ready, after(b + 1))
                        pe.wait_ge(hT_ready, after(b * 3))
                        for j in range(3):
                            for out, wt, ws in ((g_ps[j], w_gate, w_sgate), (u_ps[j], w_up, w_sup)):
                                for t in range(DT):
                                    rhs = wt[:, t, 4 * j:4 * j + 4, :] if j < 2 else ws[:, t, :]
                                    last = pe.matmul(out[:, 0:512] if j < 2 else out[:, 0:D], xnT[:, t, :], rhs, start=(t == 0), stop=(t == DT - 1))
                            last.then_inc(gu_done, 1)
                    if front:
                        pe.wait_ge(ln.xn_ready, after(b + 2))
                        pe.wait_ge(rstep, after(b * RSTEPS + RSTEPS))
                        for t in range(DT):
                            last = pe.transpose(t_ps[:, 128 * t:128 * t + 128], ln.xn[:, 128 * t:128 * t + 128], k.ident[:, :])
                        last.then_inc(xT_ps, 1)
                    if main:
                        for j in range(3):
                            pe.wait_ge(hid_ready, after(b * 3 + (j + 1)))
                            for m in range(4 if j < 2 else 2):
                                c = 4 * j + m
                                last = pe.transpose(g_ps[j][:, m * S:m * S + S], hid[:, c * HE:c * HE + HE], k.ident[:, :])
                            last.then_inc(hT_ps, 1)
                    if front:
                        pe.wait_ge(xT_ready, after(b + 2))
                        for t in range(DT):
                            last = pe.matmul(t_ps[:, 256:256 + E], xnT[:, t, :], w_router[:, t, :], start=(t == 0), stop=(t == DT - 1))
                        last.then_inc(logits, 1)
                    if main:
                        pe.wait_ge(hT_ready, after(b * 3 + 3))
                        pe.wait_ge(xo_ready, after(b))
                        for c in range(NT):
                            last = pe.matmul(o_ps[:, 0:D], hT[:, c, :], w_down[:, c, :], start=(c == 0), stop=(c == NT - 1))
                        last.then_inc(out_done, 1)

                pe.wait_ge(weights_in, after(16 * 9))
                in_two_phases(pe, step)


RSTEPS = 9


def build(nc, ins, out):
    k = Kernel(nc, ins, out)
    with ExitStack() as ctx:
        sb = lambda n, s, t=F32: ctx.enter_context(nc.sbuf_tensor(n, s, t))
        sem = lambda n: ctx.enter_context(nc.semaphore(n))
        k.ident = sb("ident", [128, 128])
        k.minus_half = sb("minus_half", [128, 1])
        k.eps = sb("eps", [128, 1])
        k.pair_mask = sb("pair_mask", [128, 2])
        k.gates = sb("gates", [128, 8])
        raw_gates = sb("raw_gates", [128, 8])
        setup_in, mh = sem("setup_in"), sem("minus_half_set")
        k.setup_in = setup_in
        with nc.Block() as block:
            @block.sync
            def _(sp):
                sp.dma_start(k.ident[:, :], ins["c_ident"]).then_inc(setup_in, 16)
                sp.dma_start(k.pair_mask[:, :], ins["c_pair_mask"]).then_inc(setup_in, 16)
                sp.dma_start(raw_gates[:, 0:4], ins["g_xattn"].rearrange("(a n) -> a n", a=1).to_broadcast([128, 4])).then_inc(setup_in, 16)
                sp.dma_start(raw_gates[:, 4:8], ins["g_ffn"].rearrange("(a n) -> a n", a=1).to_broadcast([128, 4])).then_inc(setup_in, 16)

            @block.gpsimd
            def _(pool):
                pool.memset(k.minus_half[:, :], -0.5).then_inc(mh, 1)
                pool.memset(k.eps[:, :], LN_EPS).then_inc(mh, 1)

            @block.scalar
            def _(act):
                act.wait_ge(setup_in, 64)
                act.activation(k.gates[:, :], raw_gates[:, :], ACT.Tanh).then_inc(mh, 1)
                act.wait_ge(mh, 3)
        def scratch(name, shape):
            return nc.dram_tensor(name, shape, F32).ap()

        def x_after(n):
            return out if n == LAYERS - 1 else scratch(f"x_after_{n}", (B, S, D))

        x = x_after(0)
        stage_retention(k, ins["x"], x)
        k.clear_semaphores()
        x, x_in = x_after(1), x
        stage_switch_attention(k, x_in, x)
        k.clear_semaphores()
        x, x_in = x_after(3), x
        dist, costs = scratch("dist", (B, S, S)), scratch("costs", (B, S + 1, S + 1))
        steps, path = scratch("steps", (B, S, S)), scratch("path", (S, B, S))
        stage_distances(k, x_in, dist)
        k.clear_semaphores()
        stage_warp(k, dist, costs, steps, path)
        k.clear_semaphores()
        stage_align_int8(k, x_in, path, x)
        k.clear_semaphores()
        x, x_in = x_after(4), x
        bounce = [scratch(f"bounce{u}", ((S * (S + 1)) * H,)) for u in range(2)]
        stage_attention(k, x_in, x, "L2", 2, True, bounce)
        k.clear_semaphores()
        x, x_in = x_after(5), x
        stage_low_rank_ffn(k, x_in, x)
        k.clear_semaphores()
        x, x_in = x_after(6), x
        stage_attention(k, x_in, x, "L3", 3, False)
        k.clear_semaphores()
        stage_mixture_ffn(k, x, out)
        k.clear_semaphores()


def kernel(**inputs):
    import numpy as _np
    import concourse.bacc as _bacc
    from concourse import mybir as _mybir
    from concourse.bass_utils import run_bass_kernel_spmd as _run

    nc = _bacc.Bacc("TRN2", target_bir_lowering=False, num_devices=1)
    arrays = {n: _np.ascontiguousarray(a) for n, a in inputs.items()}
    cT = _np.ascontiguousarray(_np.swapaxes(arrays["ctx_1024"], 1, 2))
    swapped = cT.reshape(B, D // 2, 2, S)[:, :, ::-1, :].reshape(B, D, S)
    arrays["ctxT_pairs"] = _np.ascontiguousarray(_np.stack([cT, swapped], axis=1))
    q_rot, k_rot, decay = retention_tables()
    arrays.update(c_q_rot=q_rot, c_k_rot=k_rot, c_decay=decay, c_ident=_np.eye(128, dtype=_np.float32),
                  c_pair_mask=pair_masks())
    arrays["w_value"] = _np.ascontiguousarray(arrays.pop("L0_ffn_value_experts").transpose(2, 0, 1, 3).reshape(D, E * HK))
    arrays["w_out"] = _np.ascontiguousarray(
        arrays.pop("L0_ffn_output_experts").reshape(E, HK // 128, 128, D).transpose(2, 0, 1, 3))
    arrays["c_causal"] = _np.where(_np.arange(S)[None, :] > _np.arange(S)[:, None], MASKED, 0.0).astype(_np.float32)
    arrays["c_rank"] = _np.broadcast_to(_np.arange(E, 0, -1).astype(_np.float32), (128, MH, E)).copy()
    arrays["c_spread"] = expert_spread()
    arrays["w_int8T"] = _np.ascontiguousarray(arrays.pop("L1_ffn_weight_q").T).view(_np.int32)
    arrays["c_iota"] = _np.broadcast_to(_np.arange(S, dtype=_np.float32), (128, S)).copy()
    arrays["c_sinT"] = sinusoid_reversed_T()
    feed = {f"in_{n}_dram": a for n, a in arrays.items()}
    ins = {n: nc.dram_tensor(f"in_{n}_dram", a.shape, _mybir.dt.from_np(a.dtype), kind="ExternalInput").ap()
           for n, a in arrays.items()}
    out = nc.dram_tensor("out_0_dram", (B, S, D), F32, kind="ExternalOutput").ap()
    build(nc, ins, out)
    r = _run(nc, [feed], core_ids=[0])
    return r.results[0]["out_0_dram"]
```

```python
from contextlib import ExitStack
import math

import numpy as np
import concourse.bass as bass
from concourse import mybir

ALU = mybir.AluOpType
ACT = mybir.ActivationFunctionType
AX = mybir.AxisListType
F32 = mybir.dt.float32
F32R = mybir.dt.float32r
BF16 = mybir.dt.bfloat16
I32 = mybir.dt.int32
I8 = mybir.dt.int8


B = 16
S = 128
D = 256
DT = D // 128
H = 16
HD = D // H
LN_EPS = 1e-5
LAYERS = 8


def retention_tables():
    f = np.float32
    half = HD // 2
    base = (np.arange(0, HD, 2, dtype=f) + f(0.4 * HD)) / f(1.4 * HD)
    pos = np.arange(S, dtype=f)
    scale = (base[None, :] ** (pos / f(512.0))[:, None]).astype(f)
    inv_freq = (f(1.0) / f(10000.0) ** (np.arange(half, dtype=f) / f(half))).astype(f)
    ang = (pos[:, None] * inv_freq[None, :]).astype(f)
    sign = np.tile(np.array([-1.0, 1.0], f), half)

    def table(sc):
        cos = np.repeat(np.cos(ang).astype(f) * sc, 2, axis=-1)
        sin = np.repeat(np.sin(ang).astype(f) * sc, 2, axis=-1) * sign[None, :]
        t = np.stack([cos.T, sin.T], axis=1)
        return np.ascontiguousarray(np.tile(t, (128 // HD, 1, 1)).astype(f))

    gam = (f(1.0) - np.exp(np.linspace(math.log(1 / 32), math.log(1 / 512), H).astype(f))).astype(f)
    s, t = np.arange(S)[None, :], np.arange(S)[:, None]
    decay = np.where(s >= t, gam[:, None, None] ** np.maximum(s - t, 0).astype(f), f(0)).astype(f)
    order = [h for bank in range(4) for h in heads_of_bank(bank)]
    decay = np.ascontiguousarray(decay[order].transpose(1, 0, 2))
    return table(scale), table((f(1.0) / scale).astype(f)), decay


def heads_of_bank(bank):
    return [2 * bank, 2 * bank + 1, 2 * bank + 8, 2 * bank + 9]


def pair_masks():
    odd = (np.arange(128) // HD) % 2
    return np.stack([1 - odd, odd], axis=1).astype(np.float32)


PRIME = 16


def after(n):
    return n + PRIME


def loads(n, parity, transfers=1):
    return after(n * (8 * transfers) + (16 - 8 * parity) * transfers)


def stores(n, parity):
    return after(n * 8 + (-8 * parity))


def split_product(pe, out, x_parts, w_parts, first, last):
    (x_hi, x_lo), (w_hi, w_lo) = x_parts, w_parts
    pe.matmul(out, x_hi, w_hi, start=first, stop=False)
    pe.matmul(out, x_hi, w_lo, start=False, stop=False)
    return pe.matmul(out, x_lo, w_hi, start=False, stop=last)


def in_three_phases(engine, step):
    step(-1, 1, middle=False, tail=False)
    step(0, 0, tail=False)
    with engine.Fori(0, (B - 4) // 2) as i:
        step(i * 2 + 1, 1)
        step(i * 2 + 2, 0)
    step(B - 3, 1)
    step(B - 2, 0, ahead=False)
    step(B - 1, 1, ahead=False, front=False)
    step(B, 0, ahead=False, front=False, middle=False)


def in_four_phases(engine, step, chunk=lambda b, expert, kind: None):
    step(-1, 1, middle=False, tail=False, end=False)
    step(0, 0, tail=False, end=False)
    chunk(0, 0, 0)
    step(1, 1, end=False)
    chunk(1, 0, 1)
    with engine.Fori(0, (B - 6) // 2) as i:
        step(i * 2 + 2, 0)
        chunk(i * 2 + 2, i + 1, 0)
        step(i * 2 + 3, 1)
        chunk(i * 2 + 3, i + 1, 1)
    step(B - 4, 0)
    chunk(B - 4, B // 2 - 2, 0)
    step(B - 3, 1)
    chunk(B - 3, B // 2 - 2, 1)
    step(B - 2, 0, ahead=False)
    chunk(B - 2, B // 2 - 1, 0)
    step(B - 1, 1, ahead=False, front=False)
    chunk(B - 1, B // 2 - 1, 1)
    step(B, 0, ahead=False, front=False, middle=False)
    step(B + 1, 1, ahead=False, front=False, middle=False, tail=False)


def in_two_phases(engine, step):
    step(-1, 1, main=False)
    with engine.Fori(0, (B - 2) // 2) as i:
        step(i * 2, 0)
        step(i * 2 + 1, 1)
    step(B - 2, 0)
    step(B - 1, 1, front=False)


class Kernel:

    def __init__(self, nc, ins, out):
        self.nc, self.ins, self.out = nc, ins, out
        self.unprimed, self.used = [], []

    def semaphore(self, ctx, name):
        s = self.nc.alloc_semaphore(name)
        self.unprimed.append(s)
        self.used.append(s)
        return s

    def clear_semaphores(self):
        numbers = sorted(s.num for s in self.used)
        with self.nc.Block() as block:
            @block.gpsimd
            def _(pool):
                first = 0
                for n in range(1, len(numbers) + 1):
                    if n == len(numbers) or numbers[n] != numbers[n - 1] + 1:
                        pool.sem_clear(range(numbers[first], numbers[n - 1] + 1))
                        first = n
        for s in self.used:
            self.nc.release_semaphore(s)
        self.used = []

    def prime(self, pool):
        for s in self.unprimed:
            pool.sem_inc(s, PRIME)
        self.unprimed = []


class LayerNorm:

    def __init__(self, k, ctx, name):
        nc = k.nc
        self.k = k
        sb = lambda n, s: ctx.enter_context(nc.sbuf_tensor(f"{name}_{n}", s, F32))
        sem = lambda n: k.semaphore(ctx, f"{name}_{n}")
        self.stats, self.mv = sb("stats", [128, 6]), sb("mv", [128, 2])
        self.ve, self.rstd, self.xn = sb("ve", [128, 1]), sb("rstd", [128, 1]), sb("xn", [128, D])
        self.pace = sb("pace", [128, 1])
        self.stats_ready, self.mv_ready, self.ve_ready = sem("stats"), sem("mean_var"), sem("var_eps")
        self.rstd_ready, self.xn_ready = sem("rstd"), sem("xn")

    def statistics(self, dve, b, x):
        dve.bn_stats(self.stats[:, :], x).then_inc(self.stats_ready, 1)
        dve.wait_ge(self.stats_ready, after(b + 1))
        dve.memset(self.pace[:, :], 0.0)
        dve.bn_aggr(self.mv[:, :], self.stats[:, :]).then_inc(self.mv_ready, 1)

    def inverse_root(self, pool, b):
        pool.wait_ge(self.mv_ready, after(b + 1))
        pool.tensor_tensor(self.ve[:, :], self.mv[:, 1:2], self.k.eps[:, :], ALU.add).then_inc(self.ve_ready, 1)
        pool.wait_ge(self.ve_ready, after(b + 1))
        pool.tensor_tensor(self.rstd[:, :], self.ve[:, :], self.k.minus_half[:, :],
                           ALU.pow).then_inc(self.rstd_ready, 1)

    def normalize(self, dve, b, x):
        dve.wait_ge(self.rstd_ready, after(b + 1))
        return dve.tensor_scalar(self.xn[:, :], x, self.mv[:, 0:1], self.rstd[:, :],
                                 ALU.subtract, ALU.mult).then_inc(self.xn_ready, 1)


def stage_retention(k, x_in, x_out, next_weights):
    nc = k.nc
    with ExitStack() as ctx:
        sb = lambda n, s, t=F32: ctx.enter_context(nc.sbuf_tensor("ret_" + n, s, t))
        ps = lambda n, s, t=F32: ctx.enter_context(nc.psum_tensor("ret_" + n, s, t))
        sem = lambda n: k.semaphore(ctx, "ret_" + n)

        x = [sb(f"x{u}", [128, D]) for u in range(2)]
        res = [sb(f"res{u}", [128, D]) for u in range(2)]
        c = [sb(f"c{u}", [128, D]) for u in range(2)]
        cT = [sb(f"cT{u}", [128, 2, DT, S]) for u in range(2)]
        q_rot = sb("q_rot", [128, 2, 1, S])
        k_rot = sb("k_rot", [128, 2, 1, S])
        decay = sb("decay", [128, H, S])
        ln = LayerNorm(k, ctx, "ret_ln")
        xn = ln.xn
        xs = sb("xs", [128, D])
        q_parts = sb("q_parts", [128, 2, DT, S])
        qT = sb("qT", [128, DT, S])
        qz = sb("qz", [128, DT, 2, S])
        k_parts = sb("k_parts", [128, 2, DT, S])
        kT = [sb(f"kT{u}", [128, DT, S]) for u in range(2)]
        sc = [sb(f"sc{u}", [128, H, S]) for u in range(2)]
        o_even, oT = sb("o_even", [128, DT, S]), sb("oT", [128, DT, S])
        xo = [sb(f"xo{u}", [128, D]) for u in range(2)]
        staging = [sb("staged_values", [128, DT, HK]), sb("staged_outputs", [128, 4, D])]

        q_ps = ps("q_ps", [128, 2, DT, S])
        sc_ps = [ps(f"sc_ps{r}", [128, 4, S]) for r in range(4)]
        pair_out = ps("pair_out", [128, DT, 2, S])
        o_ps = ps("o_ps", [128, 512])

        tables_in, decay_in = sem("tables_in"), sem("decay_in")
        x_loaded, cT_loaded, c_loaded, res_loaded = ([sem(f"{n}{u}") for u in range(2)] for n in (
            "x_loaded", "cT_loaded", "c_loaded", "res_loaded"))
        out_s = [sem(f"x_stored{u}") for u in range(2)]
        staged = [sem(f"staged{u}") for u in range(2)]
        chunk_hi, chunk_lo = sem("chunk_hi"), sem("chunk_lo")
        xs_r = sem("xs")
        xT_r, qp_r, qT_r, qz_r = sem("xT"), sem("qp"), sem("qT"), sem("qz")
        kp_r, kT_r = sem("kp"), sem("kT")
        scps_r, sc_r, pair_r, even_r, oT_r, ops_r, xo_r = map(sem, ("scps", "sc", "pair_out", "even", "oT", "ops", "xo"))

        with nc.Block() as block:

            @block.sync
            def _(sp):
                def load_x(n, v):
                    sp.dma_start(x[v][:, :], x_in[n]).then_inc(x_loaded[v], 16)

                def load_transposed(n, v):
                    sp.dma_start(cT[v][:, :, :, :].rearrange("p a t s -> p (a t) s"),
                                 k.ins["ctxT_pairs"][n].rearrange("a (t p) s -> p (a t) s", p=128)).then_inc(cT_loaded[v], 16)

                def load_context(n, v):
                    sp.dma_start(c[v][:, :], k.ins["ctx_1024"][n]).then_inc(c_loaded[v], 16)

                def load_residual(n, v):
                    sp.dma_start(res[v][:, :], x_in[n]).then_inc(res_loaded[v], 16)

                def step(b, u, ahead=True, front=True, middle=True, tail=True, end=True):
                    nu = 1 - u
                    if ahead and (not isinstance(b, int) or b + 3 < B):
                        sp.wait_ge(xs_r, after(b + 2))
                        load_x(b + 3, nu)
                        sp.wait_ge(kT_r, after(b + 2))
                        load_transposed(b + 3, nu)
                    if end:
                        sp.wait_ge(xo_r, after(b - 1))
                        sp.dma_start(x_out[b - 2], xo[u][:, :]).then_inc(out_s[u], 16)
                        if not isinstance(b, int) or b < B:
                            load_residual(b, u)
                    if tail and (not isinstance(b, int) or b + 1 < B):
                        sp.wait_ge(pair_r, after(b))
                        load_context(b + 1, nu)

                load_x(0, 0)
                load_x(1, 1)
                sp.dma_start(q_rot[:, :, 0, :], k.ins["c_q_rot"]).then_inc(tables_in, 16)
                sp.dma_start(k_rot[:, :, 0, :], k.ins["c_k_rot"]).then_inc(tables_in, 16)
                for n in range(2):
                    load_transposed(n, n)
                sp.dma_start(decay[:, :, :], k.ins["c_decay"]).then_inc(decay_in, 16)
                for n in range(2):
                    load_context(n, n)
                    load_residual(n, n)
                in_four_phases(sp, step)
                for u in range(2):
                    sp.wait_ge(out_s[u], after(16 * B // 2))

            @block.gpsimd
            def _(pool):
                def step(b, u, ahead=True, front=True, middle=True, tail=True, end=True):
                    nu = 1 - u
                    if ahead:
                        ln.inverse_root(pool, b + 2)
                    if front:
                        pool.wait_ge(cT_loaded[nu], loads(b + 1, nu))
                        pool.wait_ge(kT_r, after(b + 1))
                        pool.tensor_tensor(k_parts[:, :, :, :], cT[nu][:, :, :, :],
                                           k_rot[:, :, :, :].to_broadcast([128, 2, DT, S]), ALU.mult).then_inc(kp_r, 1)
                        pool.wait_ge(kp_r, after(b + 2))
                        pool.wait_ge(scps_r, after(b * 4))
                        pool.tensor_tensor(kT[nu][:, :, :], k_parts[:, 0], k_parts[:, 1], ALU.add).then_inc(kT_r, 1)

                def chunk(b, e, kind):
                    hi, lo = next_weights.chunk_parts(e, kind)
                    pool.wait_ge(chunk_hi, after(b + 1))
                    pool.tensor_tensor(lo, staging[kind][:, :, :], hi.bitcast(F32), ALU.subtract).then_inc(chunk_lo, 1)

                k.prime(pool)
                ln.inverse_root(pool, 0)
                pool.wait_ge(tables_in, after(32))
                in_four_phases(pool, step, chunk)

            @block.vector
            def _(dve):
                def step(b, u, ahead=True, front=True, middle=True, tail=True, end=True):
                    nu = 1 - u
                    if front:
                        dve.wait_ge(xT_r, after(b + 2))
                        dve.tensor_tensor(q_parts[:, :, :, :], q_ps[:, :, :, :],
                                          q_rot[:, :, :, :].to_broadcast([128, 2, DT, S]), ALU.mult).then_inc(qp_r, 1)
                        dve.wait_ge(qp_r, after(b + 2))
                        dve.wait_ge(qz_r, after(b + 1))
                        dve.tensor_tensor(qT[:, :, :], q_parts[:, 0], q_parts[:, 1], ALU.add).then_inc(qT_r, 1)
                    if ahead:
                        layer_norm(b + 2, u)
                    if middle:
                        if isinstance(b, int) and b == 0:
                            dve.wait_ge(decay_in, after(16))
                        for r in range(4):
                            dve.wait_ge(scps_r, after(b * 4 + (r + 1)))
                            dve.wait_ge(pair_r, after(b - 1))
                            dve.tensor_tensor(sc[u][:, 4 * r:4 * r + 4, :], sc_ps[r][:, :, :],
                                              decay[:, 4 * r:4 * r + 4, :], ALU.mult).then_inc(sc_r, 1)
                    if tail:
                        dve.wait_ge(even_r, after(b))
                        dve.wait_ge(ops_r, after(b - 1))
                        dve.scalar_tensor_tensor(oT[:, :, :], pair_out[:, :, 1, :], k.pair_mask[:, 1:2], o_even[:, :, :],
                                                 ALU.mult, ALU.add).then_inc(oT_r, 1)
                    if end:
                        dve.wait_ge(ops_r, after(b - 1))
                        dve.wait_ge(out_s[u], stores(b - 2, u))
                        dve.wait_ge(res_loaded[u], loads(b - 2, u))
                        dve.scalar_tensor_tensor(xo[u][:, :], o_ps[:, 0:D], k.gates[:, 0:1], res[u][:, :],
                                                 ALU.mult, ALU.add).then_inc(xo_r, 1)

                def layer_norm(n, v):
                    dve.wait_ge(x_loaded[v], loads(n, v))
                    ln.statistics(dve, n, x[v][:, :])
                    dve.wait_ge(xT_r, after(n))
                    ln.normalize(dve, n, x[v][:, :])
                    dve.tensor_scalar(xs[:, :].rearrange("p (n two) -> p n two", two=2)[:, :, ::-1],
                                      x[v][:, :].rearrange("p (n two) -> p n two", two=2), ln.mv[:, 0:1],
                                      ln.rstd[:, :], ALU.subtract, ALU.mult).then_inc(xs_r, 1)

                layer_norm(0, 0)
                dve.wait_ge(tables_in, after(32))
                in_four_phases(dve, step)

            @block.scalar
            def _(act):
                def step(b, u, ahead=True, front=True, middle=True, tail=True, end=True):
                    if front:
                        act.wait_ge(qT_r, after(b + 2))
                        act.wait_ge(scps_r, after(b * 4 + 4))
                        for par in range(2):
                            last = act.activation(qz[:, :, par, :], qT[:, :, :], ACT.Copy, scale=k.pair_mask[:, par:par + 1])
                        last.then_inc(qz_r, 1)
                    if tail:
                        act.wait_ge(pair_r, after(b))
                        act.wait_ge(oT_r, after(b - 1))
                        act.activation(o_even[:, :, :], pair_out[:, :, 0, :], ACT.Copy, scale=k.pair_mask[:, 0:1]).then_inc(even_r, 1)

                def round_chunk(b, e, kind):
                    act.wait_ge(staged[kind], loads(b, kind))
                    act.activation(next_weights.chunk_parts(e, kind)[0], staging[kind][:, :, :], ACT.Copy).then_inc(chunk_hi, 1)

                def chunk(b, e, kind):
                    if not isinstance(b, int) or b + 2 < B:
                        act.wait_ge(chunk_lo, after(b + 1))
                        next_weights.load_chunk(act, staging, e + 1, kind, staged)
                    if not isinstance(b, int) or b + 1 < B:
                        round_chunk(b + 1, e + kind, 1 - kind)

                for kind in range(2):
                    next_weights.load_chunk(act, staging, 0, kind, staged)
                next_weights.load(act)
                round_chunk(0, 0, 0)
                in_four_phases(act, step, chunk)

            @block.tensor
            def _(pe):
                def step(b, u, ahead=True, front=True, middle=True, tail=True, end=True):
                    nu = 1 - u
                    if front:
                        pe.wait_ge(xs_r, after(b + 2))
                        pe.wait_ge(qp_r, after(b + 1))
                        for t in range(DT):
                            pe.transpose(q_ps[:, 0, t, :], xn[:, 128 * t:128 * t + 128], k.ident[:, :])
                        for t in range(DT):
                            last = pe.transpose(q_ps[:, 1, t, :], xs[:, 128 * t:128 * t + 128], k.ident[:, :])
                        last.then_inc(xT_r, 1)
                    if middle:
                        pe.wait_ge(qz_r, after(b + 1))
                        pe.wait_ge(kT_r, after(b + 1))
                        pe.wait_ge(sc_r, after(b * 4))
                        for half in range(2):
                            for r in range(4):
                                rows = slice(32 * r, 32 * r + 32)
                                last = pe.matmul(sc_ps[r][:, 2 * half:2 * half + 2, :], kT[u][rows, half, :],
                                                 qz[rows, half, :, :], start=True, stop=True, tile_position=(32 * r, 0))
                                if half:
                                    last.then_inc(scps_r, 1)
                    if tail:
                        pe.wait_ge(c_loaded[nu], loads(b - 1, nu))
                        pe.wait_ge(oT_r, after(b - 1))
                        pe.wait_ge(sc_r, after(b * 4))
                        for half in range(DT):
                            for g in range(4):
                                pair = 4 * half + g
                                last = pe.matmul(pair_out[32 * g:32 * g + 32, half, :, :], c[nu][:, 32 * pair:32 * pair + 32],
                                                 sc[nu][:, 4 * g + 2 * half:4 * g + 2 * half + 2, :], start=True, stop=True,
                                                 tile_position=(0, 32 * g))
                        last.then_inc(pair_r, 1)
                    if end:
                        pe.wait_ge(oT_r, after(b - 1))
                        pe.wait_ge(xo_r, after(b - 2))
                        for t in range(DT):
                            last = pe.transpose(o_ps[:, 128 * t:128 * t + 128], oT[:, t, :], k.ident[:, :])
                        last.then_inc(ops_r, 1)

                in_four_phases(pe, step)


MH = 8
MD = 64
E = 8
HK = MH * MD
MASKED = -1.0e30


def expert_spread():
    t = np.zeros((E, MH, E, HK), np.float32)
    for e in range(E):
        for h in range(MH):
            t[e, h, e, h * MD:(h + 1) * MD] = 1.0
    one_bf16 = 0x3F80
    return (t.reshape(E * MH, E * HK).astype(np.uint16) * one_bf16).astype(np.uint16).view(np.int32)


class SwitchWeights:
    LOADED = 16 * 6

    def __init__(self, k, ctx):
        sb = lambda n, s, t=F32: ctx.enter_context(k.nc.sbuf_tensor("moa_" + n, s, t))
        self.ins = k.ins
        self.loaded = k.nc.alloc_semaphore("moa_weights_loaded")
        self.wq, self.wk, self.wg = sb("wq", [128, DT, HK]), sb("wk", [128, DT, HK]), sb("wg", [128, DT, MH * E])
        self.value_parts = [sb(f"w_value_{n}", [128, E, DT, HK], F32R) for n in ("hi", "lo")]
        self.out_parts = [sb(f"w_out_{n}", [128, E, 4, D], F32R) for n in ("hi", "lo")]
        self.spread = sb("spread", [E * MH, E * HK // 2], I32)
        self.causal = sb("causal", [128, S])
        self.rank = sb("rank", [128, MH, E])

    def load(self, engine):
        for tile, name in ((self.wg, "w_gate"), (self.wq, "w_q"), (self.wk, "w_k")):
            engine.dma_start(tile[:, :, :], self.ins["L0_ffn_" + name].rearrange("(t p) n -> p t n", p=128)).then_inc(self.loaded, 16)
        engine.dma_start(self.causal[:, :], self.ins["c_causal"]).then_inc(self.loaded, 16)
        engine.dma_start(self.rank[:, :, :], self.ins["c_rank"]).then_inc(self.loaded, 16)
        engine.dma_start(self.spread[:, :], self.ins["c_spread"]).then_inc(self.loaded, 16)

    def load_chunk(self, engine, staging, e, kind, loaded):
        if kind == 0:
            engine.dma_start(staging[0][:, :, :], self.ins["w_value"][:, bass.ds(e, 1), :].rearrange(
                "(t p) a n -> p t (a n)", p=128)).then_inc(loaded[0], 16)
        else:
            engine.dma_start(staging[1][:, :, :], self.ins["w_out"][:, bass.ds(e, 1), :, :].rearrange(
                "p a m n -> p (a m) n")).then_inc(loaded[1], 16)

    def chunk_parts(self, e, kind):
        return [w[:, bass.ds(e, 1), :, :].rearrange("p a m n -> p (a m) n") for w in (self.out_parts if kind else self.value_parts)]


def stage_switch_attention(k, x_in, x_out, weights):
    nc = k.nc
    TOP = 17.33
    with ExitStack() as ctx:
        sb = lambda n, s, t=F32: ctx.enter_context(nc.sbuf_tensor("moa_" + n, s, t))
        ps = lambda n, s, t=F32: ctx.enter_context(nc.psum_tensor("moa_" + n, s, t))
        sem = lambda n: k.semaphore(ctx, "moa_" + n)

        x = [sb(f"x{u}", [128, D]) for u in range(2)]
        xo = [sb(f"xo{u}", [128, D]) for u in range(2)]
        wq, wk, wg, value_parts, out_parts = weights.wq, weights.wk, weights.wg, weights.value_parts, weights.out_parts
        spread, causal, rank = weights.spread[:, :].bitcast(BF16), weights.causal, weights.rank
        identb = sb("identb", [128, 128], BF16)
        ln = LayerNorm(k, ctx, "moa_ln")
        pace = sb("pace", [128, 1])
        xnT = sb("xnT", [128, DT, S])
        xnT_hi, xnT_lo = sb("xnT_hi", [128, DT, S], F32R), sb("xnT_lo", [128, DT, S], F32R)
        qT, kT = sb("qT", [128, 4, S]), sb("kT", [128, 4, S])
        z = sb("z", [128, MH, E])
        z_top, tied, key, key_top = sb("z_top", [128, MH]), sb("tied", [128, MH, E]), sb("key", [128, MH, E]), sb("key_top", [128, MH])
        onehot = sb("onehot", [128, E, MH])
        onehot_b = sb("onehot_b", [128, 2 * E, MH], BF16)
        ohT = sb("ohT", [E * MH, S], BF16)
        eneg, gden, gate = sb("eneg", [128, MH]), sb("gden", [128, MH]), sb("gate", [128, MH])
        att = sb("att", [128, 2, 4, S])
        nmax = sb("nmax", [128, 2, 4])
        prob = sb("prob", [128, 2, 4, S])
        total = sb("total", [128, 2, 4])
        rtotal, scale_o = sb("rtotal", [128, 2, 4]), sb("scale_o", [128, MH])
        probT = sb("probT", [128, 2, 4, S])
        v_sel, v = sb("v_sel", [128, MH, MD]), sb("v", [128, MH, MD])
        og = sb("og", [128, MH, MD])
        ogT = sb("ogT", [128, 2, 4, S], F32R)
        oe = [sb(f"oe{j}", [128, 2, 4, S], F32R) for j in range(2)]

        t_ps = ps("t_ps", [128, 512])
        q_ps, k_ps = ps("q_ps", [128, 512]), ps("k_ps", [128, 512])
        s_ps = [ps(f"s_ps{j}", [128, 4, S]) for j in range(2)]
        y_ps = [ps(f"y_ps{j}", [128, 4, S]) for j in range(2)]
        o_ps = ps("o_ps", [128, 512])
        oh_view = t_ps[:, 384:448].bitcast(BF16)

        x_loaded = [sem(f"x_loaded{u}") for u in range(2)]
        x_stored = [sem(f"x_stored{u}") for u in range(2)]
        consts_cast = sem("consts_cast")
        xT_ps, xT_ready, xT_lo_ready, logits, q_done, k_done, q_ready, k_ready = map(sem, (
            "xT_ps", "xT_ready", "xT_lo_ready", "logits", "q_done", "k_done", "q_ready", "k_ready"))
        s_done, att_masked, max_ready, prob_ready = map(sem, ("s_done", "att_masked", "max_ready", "prob_ready"))
        gate_step, onehot_ready, eneg_ready, gate_ready = map(sem, ("gate_step", "onehot_ready", "eneg_ready", "gate_ready"))
        y_done, y_taken, v_ready = map(sem, ("y_done", "y_taken", "v_ready"))
        ohT_ps, ohT_ready, pT_ps, pT_ready = map(sem, ("ohT_ps", "ohT_ready", "pT_ps", "pT_ready"))
        o_done, scale_step, og_ready, ogT_ps, ogT_hi_ready, ogT_lo_ready = map(sem, (
            "o_done", "scale_step", "og_ready", "ogT_ps", "ogT_hi_ready", "ogT_lo_ready"))
        mask_done, oe_ready, out_done, xo_ready = map(sem, ("mask_done", "oe_ready", "out_done", "xo_ready"))

        with nc.Block() as block:

            @block.sync
            def _(sp):
                def load(b, u):
                    sp.dma_start(x[u][:, :], x_in[b]).then_inc(x_loaded[u], 16)

                def store(b, u):
                    sp.wait_ge(xo_ready, after(b + 1))
                    sp.dma_start(x_out[b], xo[u][:, :]).then_inc(x_stored[u], 16)

                load(0, 0)
                load(1, 1)
                with sp.Fori(0, B // 2 - 1) as i:
                    for u in range(2):
                        b = i * 2 + u
                        store(b, u)
                        load(b + 2, u)
                for u in range(2):
                    store(B - 2 + u, u)
                for u in range(2):
                    sp.wait_ge(x_stored[u], after(16 * B // 2))

            @block.gpsimd
            def _(pool):
                k.prime(pool)
                pool.wait_ge(weights.loaded, weights.LOADED)
                pool.tensor_copy(identb[:, :], k.ident[:, :]).then_inc(consts_cast, 1)
                pool.memset(onehot_b[:, E:2 * E, :], 0.0).then_inc(consts_cast, 1)
                with pool.Fori(0, B) as b:
                    ln.inverse_root(pool, b)
                    pool.wait_ge(xT_ready, after(b + 1))
                    pool.wait_ge(y_done, after(b * 8))
                    pool.tensor_tensor(xnT_lo[:, :, :], xnT[:, :, :], xnT_hi[:, :, :].bitcast(F32), ALU.subtract).then_inc(xT_lo_ready, 1)

            @block.vector
            def _(dve):
                def statistics(n, v):
                    dve.wait_ge(x_loaded[v], loads(n, v))
                    ln.statistics(dve, n, x[v][:, :])

                def normalize(n, v):
                    dve.wait_ge(xT_ps, after(n))
                    ln.normalize(dve, n, x[v][:, :])

                def choose_experts(n):
                    dve.wait_ge(logits, after(n + 1))
                    dve.tensor_scalar(z[:, :, :], t_ps[:, 256:320].rearrange("p (h e) -> p h e", e=E), TOP, None,
                                      ALU.min).then_inc(gate_step, 1)
                    dve.wait_ge(gate_step, after(n * 5 + 1))
                    dve.wait_ge(eneg_ready, after(n))
                    dve.tensor_reduce(z_top[:, :], z[:, :, :], AX.X, ALU.max).then_inc(gate_step, 1)
                    dve.wait_ge(gate_step, after(n * 5 + 2))
                    dve.tensor_tensor(tied[:, :, :], z[:, :, :], z_top[:, :].unsqueeze(2).to_broadcast([128, MH, E]),
                                      ALU.is_equal).then_inc(gate_step, 1)
                    dve.wait_ge(gate_step, after(n * 5 + 3))
                    dve.tensor_tensor(key[:, :, :], tied[:, :, :], rank[:, :, :], ALU.mult).then_inc(gate_step, 1)
                    dve.wait_ge(gate_step, after(n * 5 + 4))
                    dve.tensor_reduce(key_top[:, :], key[:, :, :], AX.X, ALU.max).then_inc(gate_step, 1)
                    dve.wait_ge(gate_step, after(n * 5 + 5))
                    dve.wait_ge(ohT_ps, after(n))
                    dve.wait_ge(y_taken, after(n * 8))
                    dve.tensor_tensor(onehot[:, :, :].rearrange("p e h -> p h e"), key[:, :, :],
                                      key_top[:, :].unsqueeze(2).to_broadcast([128, MH, E]), ALU.is_equal)
                    dve.tensor_tensor(onehot_b[:, 0:E, :].rearrange("p e h -> p h e"), key[:, :, :],
                                      key_top[:, :].unsqueeze(2).to_broadcast([128, MH, E]),
                                      ALU.is_equal).then_inc(onehot_ready, 1)

                def step(b, u, front=True, main=True):
                    nu = 1 - u
                    if not main:
                        statistics(b + 1, nu)
                        normalize(b + 1, nu)
                        choose_experts(b + 1)
                        return
                    for j in range(2):
                        dve.wait_ge(s_done, after(b * 2 + (j + 1)))
                        dve.wait_ge(prob_ready, after(b * 8))
                        dve.tensor_tensor(att[:, j], s_ps[j][:, :, :], causal[:, :].unsqueeze(1).to_broadcast([128, 4, S]),
                                          ALU.add).then_inc(att_masked, 1)
                        dve.wait_ge(att_masked, after(b * 2 + (j + 1)))
                        dve.tensor_reduce(nmax[:, j], att[:, j], AX.X, ALU.max, negate=True).then_inc(max_ready, 1)
                    dve.wait_ge(eneg_ready, after(b + 1))
                    dve.tensor_scalar(gden[:, :], eneg[:, :], 1.0, None, ALU.add).then_inc(gate_ready, 1)
                    dve.wait_ge(gate_ready, after(b * 2 + 1))
                    dve.reciprocal(gate[:, :], gden[:, :]).then_inc(gate_ready, 1)
                    dve.wait_ge(onehot_ready, after(b + 1))
                    for e in range(1, E):
                        dve.wait_ge(y_taken, after(b * 8 + e))
                        dve.wait_ge(y_done, after(b * 8 + (e + 1)))
                        dve.memset(pace[:, :], 0.0)
                        dve.copy_predicated(v_sel[:, :, :], onehot[:, e, :].bitcast(I32).unsqueeze(2).to_broadcast([128, MH, MD]),
                                            y_ps[e % 2][:, :, :].rearrange("p m (h k) -> p (m h) k", k=MD)).then_inc(y_taken, 1)
                        if e == 3 and front:
                            statistics(b + 1, nu)
                        if e == 4 and front:
                            normalize(b + 1, nu)
                    dve.wait_ge(y_taken, after(b * 8 + 8))
                    dve.wait_ge(gate_ready, after(b * 2 + 2))
                    dve.wait_ge(o_done, after(b))
                    dve.tensor_tensor(v[:, :, :], v_sel[:, :, :], gate[:, :].unsqueeze(2).to_broadcast([128, MH, MD]),
                                      ALU.mult).then_inc(v_ready, 1)
                    dve.wait_ge(pT_ps, after(b * 2 + 2))
                    dve.tensor_copy(probT[:, 1], s_ps[1][:, :, :]).then_inc(pT_ready, 1)
                    if front:
                        choose_experts(b + 1)
                    dve.wait_ge(prob_ready, after(b * 8 + 8))
                    dve.reciprocal(rtotal[:, :, :], total[:, :, :]).then_inc(scale_step, 1)
                    dve.wait_ge(scale_step, after(b * 2 + 1))
                    dve.tensor_tensor(scale_o[:, :].rearrange("p (m j) -> p j m", j=2), rtotal[:, :, :],
                                      gate[:, :].rearrange("p (m j) -> p j m", j=2), ALU.mult).then_inc(scale_step, 1)
                    dve.wait_ge(scale_step, after(b * 2 + 2))
                    dve.wait_ge(o_done, after(b + 1))
                    dve.wait_ge(ogT_ps, after(b))
                    dve.tensor_tensor(og[:, :, :], o_ps[:, :].rearrange("p (h k) -> p h k", k=MD),
                                      scale_o[:, :].unsqueeze(2).to_broadcast([128, MH, MD]), ALU.mult).then_inc(og_ready, 1)
                    dve.wait_ge(ogT_hi_ready, after(b + 1))
                    dve.tensor_tensor(ogT[:, 1], o_ps[:, :].rearrange("p (m s) -> p m s", s=S), ogT[:, 0].bitcast(F32),
                                      ALU.subtract).then_inc(ogT_lo_ready, 1)
                    dve.wait_ge(ogT_lo_ready, after(b + 1))
                    for e in range(E):
                        dve.wait_ge(mask_done, after(b * 8 + (e + 1)))
                        dve.wait_ge(out_done, after(b * 8 + (e - 1)))
                        dve.tensor_tensor(oe[e % 2][:, :, :, :].rearrange("p a m s -> p a (m s)"),
                                          y_ps[e % 2][:, :, :].rearrange("p m s -> p (m s)").unsqueeze(1).to_broadcast([128, 2, 4 * S]),
                                          ogT[:, :, :, :].bitcast(F32).rearrange("p a m s -> p a (m s)"), ALU.mult).then_inc(oe_ready, 1)
                    dve.wait_ge(out_done, after(b * 8 + 8))
                    dve.wait_ge(x_stored[u], stores(b, u))
                    dve.scalar_tensor_tensor(xo[u][:, :], k_ps[:, 0:D], k.gates[:, 4:5], x[u][:, :],
                                             ALU.mult, ALU.add).then_inc(xo_ready, 1)

                dve.wait_ge(weights.loaded, weights.LOADED)
                in_two_phases(dve, step)

            @block.scalar
            def _(act):
                def step(b, u, front=True, main=True):
                    if main:
                        act.wait_ge(v_ready, after(b))
                        act.wait_ge(y_done, after(b * 8 + 1))
                        act.activation(v_sel[:, :, :], y_ps[0][:, :, :].rearrange("p m (h k) -> p (m h) k", k=MD),
                                       ACT.Copy).then_inc(y_taken, 1)
                        act.wait_ge(pT_ps, after(b * 2))
                        act.wait_ge(scale_step, after(b * 2))
                        for j in range(2):
                            act.wait_ge(max_ready, after(b * 2 + (j + 1)))
                            for m in range(4):
                                act.activation(prob[:, j, m], att[:, j, m], ACT.Exp, bias=nmax[:, j, m:m + 1],
                                               accum_out=total[:, j, m:m + 1]).then_inc(prob_ready, 1)
                        act.wait_ge(ohT_ps, after(b + 1))
                        act.wait_ge(mask_done, after(b * 8))
                        act.activation(ohT[:, :], oh_view[0:E * MH, :], ACT.Copy).then_inc(ohT_ready, 1)
                        act.wait_ge(pT_ps, after(b * 2 + 1))
                        act.wait_ge(o_done, after(b))
                        act.activation(probT[:, 0], s_ps[0][:, :, :], ACT.Copy).then_inc(pT_ready, 1)
                    if front:
                        act.wait_ge(xT_ps, after(b + 2))
                        act.wait_ge(y_done, after(b * 8 + 8))
                        act.activation(xnT_hi[:, :, :], t_ps[:, 0:D].rearrange("p (t s) -> p t s", t=DT), ACT.Copy)
                        act.activation(xnT[:, :, :], t_ps[:, 0:D].rearrange("p (t s) -> p t s", t=DT), ACT.Copy).then_inc(xT_ready, 1)
                    if main:
                        act.wait_ge(ogT_ps, after(b + 1))
                        act.wait_ge(oe_ready, after(b * 8))
                        act.activation(ogT[:, 0], o_ps[:, :].rearrange("p (m s) -> p m s", s=S), ACT.Copy).then_inc(ogT_hi_ready, 1)
                    if front:
                        act.wait_ge(s_done, after(b * 2 + 2))
                        act.wait_ge(k_done, after(b + 2))
                        act.activation(kT[:, :, :], k_ps[:, :].rearrange("p (m s) -> p m s", s=S), ACT.Copy).then_inc(k_ready, 1)
                        act.wait_ge(gate_step, after(b * 5 + 7))
                        act.wait_ge(gate_ready, after(b * 2 + 2))
                        act.activation(eneg[:, :], z_top[:, :], ACT.Exp, scale=-1.0).then_inc(eneg_ready, 1)
                        act.wait_ge(q_done, after(b + 2))
                        act.activation(qT[:, :, :], q_ps[:, :].rearrange("p (m s) -> p m s", s=S), ACT.Copy, scale=MD ** -0.5).then_inc(q_ready, 1)

                in_two_phases(act, step)

            @block.tensor
            def _(pe):
                def project(out, wt, ms=range(4)):
                    for m in ms:
                        for t in range(DT):
                            last = pe.matmul(out[:, m * S:m * S + S], wt[:, t, 128 * m:128 * m + 128], xnT[:, t, :],
                                             start=(t == 0), stop=(t == DT - 1))
                    return last

                def step(b, u, front=True, main=True):
                    def mask(e):
                        if e >= 2:
                            pe.wait_ge(oe_ready, after(b * 8 + (e - 1)))
                        for m in range(4):
                            last = pe.matmul(y_ps[e % 2][:, m, :], spread[:, (4 * e + m) * 128:(4 * e + m) * 128 + 128],
                                             ohT[:, :], start=True, stop=True)
                        last.then_inc(mask_done, 1)

                    if main:
                        pe.wait_ge(xT_lo_ready, after(b + 1))
                        pe.wait_ge(oe_ready, after(b * 8))
                        for e in range(E):
                            if e >= 2:
                                pe.wait_ge(y_taken, after(b * 8 + (e - 1)))
                            for t in range(DT):
                                last = split_product(pe, y_ps[e % 2][:, :, :], (xnT_hi[:, t, :], xnT_lo[:, t, :]),
                                                     [w[:, e, t, :] for w in value_parts], t == 0, t == DT - 1)
                            last.then_inc(y_done, 1)
                        pe.wait_ge(onehot_ready, after(b + 1))
                        pe.transpose(oh_view, onehot_b[:, :, :].rearrange("p e h -> p (e h)"), identb[:, :]).then_inc(ohT_ps, 1)
                        for j in range(2):
                            pe.wait_ge(prob_ready, after(b * 8 + (4 * j + 4)))
                            for m in range(4):
                                last = pe.transpose(s_ps[j][:, m, :], prob[:, j, m], k.ident[:, :])
                            last.then_inc(pT_ps, 1)
                    if front:
                        pe.wait_ge(ln.xn_ready, after(b + 2))
                        pe.wait_ge(ohT_ready, after(b + 1))
                        for t in range(DT):
                            last = pe.transpose(t_ps[:, 128 * t:128 * t + 128], ln.xn[:, 128 * t:128 * t + 128], k.ident[:, :])
                        last.then_inc(xT_ps, 1)
                    if main:
                        pe.wait_ge(ohT_ready, after(b + 1))
                        pe.wait_ge(y_taken, after(b * 8 + 7))
                        mask(0)
                    if front:
                        pe.wait_ge(xT_ready, after(b + 2))
                        for t in range(DT):
                            last = pe.matmul(t_ps[:, 256:320], xnT[:, t, :], wg[:, t, :], start=(t == 0), stop=(t == DT - 1))
                        last.then_inc(logits, 1)
                    if main:
                        pe.wait_ge(y_taken, after(b * 8 + 8))
                        mask(1)
                    if front:
                        pe.wait_ge(xo_ready, after(b))
                        project(k_ps, wk, range(0, 1))
                    if main:
                        pe.wait_ge(pT_ready, after(b * 2 + 2))
                        pe.wait_ge(v_ready, after(b + 1))
                        pe.wait_ge(ogT_lo_ready, after(b))
                        for h in range(MH):
                            last = pe.matmul(o_ps[:, h * MD:h * MD + MD], probT[:, h % 2, h // 2], v[:, h, :], start=True, stop=True)
                        last.then_inc(o_done, 1)
                    if front:
                        project(k_ps, wk, range(1, 3))
                    if main:
                        pe.wait_ge(og_ready, after(b + 1))
                        for m in range(4):
                            last = pe.transpose(o_ps[:, m * S:m * S + S], og[:, 2 * m:2 * m + 2, :].rearrange("p h k -> p (h k)"), k.ident[:, :])
                        last.then_inc(ogT_ps, 1)
                    if front:
                        project(k_ps, wk, range(3, 4)).then_inc(k_done, 1)
                        pe.wait_ge(q_ready, after(b + 1))
                        project(q_ps, wq).then_inc(q_done, 1)
                        pe.wait_ge(k_ready, after(b + 2))
                    elif main:
                        pe.wait_ge(xo_ready, after(b))
                    if main:
                        for e in range(E):
                            pe.wait_ge(oe_ready, after(b * 8 + (e + 1)))
                            for m in range(4):
                                last = split_product(pe, k_ps[:, 0:D], [oe[e % 2][:, a, m, :] for a in range(2)],
                                                     [w[:, e, m, :] for w in out_parts], e == 0 and m == 0, e == E - 1 and m == 3)
                            last.then_inc(out_done, 1)
                            if e + 2 < E:
                                mask(e + 2)
                    if front:
                        pe.wait_ge(q_ready, after(b + 2))
                        pe.wait_ge(k_ready, after(b + 2))
                        pe.wait_ge(pT_ready, after(b * 2 + 2))
                        for m in range(4):
                            for j in range(2):
                                rows = slice(64 * j, 64 * j + 64)
                                last = pe.matmul(s_ps[j][:, m, :], qT[rows, m, :], kT[rows, m, :], start=True, stop=True)
                                if m == 3:
                                    last.then_inc(s_done, 1)

                pe.wait_ge(weights.loaded, weights.LOADED)
                pe.wait_ge(consts_cast, after(2))
                in_two_phases(pe, step)


BIG = 1.0e30


def stage_distances(k, x_in, dist, later_weights):
    nc = k.nc
    TINY = 1.0e-30
    with ExitStack() as ctx:
        sb = lambda n, s, t=F32: ctx.enter_context(nc.sbuf_tensor("dist_" + n, s, t))
        ps = lambda n, s, t=F32: ctx.enter_context(nc.psum_tensor("dist_" + n, s, t))
        sem = lambda n: k.semaphore(ctx, "dist_" + n)
        x = [sb(f"x{u}", [128, D]) for u in range(2)]
        c = [sb(f"c{u}", [128, D]) for u in range(2)]
        cT = [sb(f"cT{u}", [128, DT, S]) for u in range(2)]
        ln = LayerNorm(k, ctx, "dist_ln")
        ones = sb("ones", [128, 128])
        yT, y2T = sb("yT", [128, DT, S]), sb("y2T", [128, DT, S])
        csq, aa = sb("csq", [128, D]), sb("aa", [128, 2])
        norms, raw, d2, root, floor, safe, quot = (sb(n, [128, S]) for n in ("norms", "raw", "d2", "root", "floor", "safe", "quot"))
        d = [sb(f"d{u}", [128, S]) for u in range(2)]
        t_ps = ps("t_ps", [128, 512])
        ab_ps, bb_ps = ps("ab_ps", [128, 512]), ps("bb_ps", [128, 512])
        x_loaded, c_loaded, d_stored = ([sem(f"{n}{u}") for u in range(2)] for n in ("x_loaded", "c_loaded", "d_stored"))
        ones_set, xT_ps, yT_ready, aa_ready, products, square, root_ready, newton, d_ready = map(sem, (
            "ones_set", "xT_ps", "yT_ready", "aa_ready", "products", "square", "root_ready", "newton", "d_ready"))

        with nc.Block() as block:

            @block.sync
            def _(sp):
                def load_x(n, v):
                    sp.dma_start(x[v][:, :], x_in[n]).then_inc(x_loaded[v], 16)

                def load_context(n, v):
                    sp.dma_start(c[v][:, :], k.ins["ctx_1024"][n]).then_inc(c_loaded[v], 16)
                    sp.dma_start(cT[v][:, :, :], k.ins["ctxT_pairs"][n, 0].rearrange("(t p) s -> p t s", p=128)).then_inc(c_loaded[v], 16)

                def step(b, u, ahead=True, front=True, middle=True, tail=True):
                    nu = 1 - u
                    if ahead and (not isinstance(b, int) or b + 3 < B):
                        sp.wait_ge(ln.xn_ready, after(b + 2))
                        load_x(b + 3, nu)
                        sp.wait_ge(products, after(b + 2))
                        load_context(b + 3, nu)
                    if tail:
                        sp.wait_ge(d_ready, after(b))
                        sp.dma_start(dist[b - 1], d[nu][:, :]).then_inc(d_stored[nu], 16)

                for n in range(2):
                    load_x(n, n)
                    load_context(n, n)
                in_three_phases(sp, step)
                for u in range(2):
                    sp.wait_ge(d_stored[u], after(16 * B // 2))

            @block.gpsimd
            def _(pool):
                k.prime(pool)
                pool.memset(ones[:, :], 1.0).then_inc(ones_set, 1)
                with pool.Fori(0, B) as b:
                    ln.inverse_root(pool, b)

            @block.vector
            def _(dve):
                def statistics(n, v):
                    dve.wait_ge(x_loaded[v], loads(n, v))
                    ln.statistics(dve, n, x[v][:, :])

                def normalize(n, v):
                    dve.wait_ge(xT_ps, after(n))
                    ln.normalize(dve, n, x[v][:, :])

                def step(b, u, ahead=True, front=True, middle=True, tail=True):
                    nu = 1 - u
                    if ahead:
                        statistics(b + 2, u)
                    if middle:
                        dve.wait_ge(products, after(b + 1))
                        dve.wait_ge(aa_ready, after(b + 1))
                        dve.tensor_scalar(norms[:, :], bb_ps[:, 0:S], aa[:, u:u + 1], None, ALU.add).then_inc(square, 1)
                    if tail:
                        dve.wait_ge(root_ready, after(b))
                        dve.tensor_scalar(floor[:, :], root[:, :], TINY, None, ALU.max).then_inc(newton, 1)
                    if middle:
                        dve.wait_ge(square, after(b * 3 + 1))
                        dve.scalar_tensor_tensor(raw[:, :], ab_ps[:, 0:S], -2.0, norms[:, :], ALU.mult, ALU.add).then_inc(square, 1)
                    if tail:
                        dve.wait_ge(newton, after(b * 3 - 2))
                        dve.reciprocal(safe[:, :], floor[:, :]).then_inc(newton, 1)
                    if ahead:
                        normalize(b + 2, u)
                    if tail:
                        dve.wait_ge(newton, after(b * 3 - 1))
                        dve.tensor_tensor(quot[:, :], d2[:, :], safe[:, :], ALU.mult).then_inc(newton, 1)
                        dve.wait_ge(newton, after(b * 3))
                        dve.wait_ge(d_stored[nu], stores(b - 1, nu))
                        dve.tensor_tensor(d[nu][:, :], quot[:, :], root[:, :], ALU.add).then_inc(d_ready, 1)
                    if middle:
                        dve.wait_ge(square, after(b * 3 + 2))
                        dve.wait_ge(d_ready, after(b))
                        dve.tensor_scalar(d2[:, :], raw[:, :], 0.0, None, ALU.max).then_inc(square, 1)

                statistics(0, 0)
                normalize(0, 0)
                in_three_phases(dve, step)

            @block.scalar
            def _(act):
                later_weights.load(act)

                def step(b, u, ahead=True, front=True, middle=True, tail=True):
                    nu = 1 - u
                    if front:
                        act.wait_ge(c_loaded[nu], loads(b + 1, nu, 2))
                        act.wait_ge(square, after(b * 3))
                        act.wait_ge(aa_ready, after(b + 1))
                        act.activation(csq[:, :], c[nu][:, :], ACT.Square, accum_out=aa[:, nu:nu + 1]).then_inc(aa_ready, 1)
                        act.wait_ge(products, after(b + 1))
                        act.wait_ge(xT_ps, after(b + 2))
                        act.activation(yT[:, :, :], t_ps[:, 0:D].rearrange("p (t s) -> p t s", s=S), ACT.Copy)
                        act.activation(y2T[:, :, :], t_ps[:, 0:D].rearrange("p (t s) -> p t s", s=S), ACT.Square).then_inc(yT_ready, 1)
                    if middle:
                        act.wait_ge(square, after(b * 3 + 3))
                        act.wait_ge(d_ready, after(b))
                        act.activation(root[:, :], d2[:, :], ACT.Sqrt).then_inc(root_ready, 1)

                in_three_phases(act, step)

            @block.tensor
            def _(pe):
                def step(b, u, ahead=True, front=True, middle=True, tail=True):
                    nu = 1 - u
                    if front:
                        pe.wait_ge(ln.xn_ready, after(b + 2))
                        pe.wait_ge(yT_ready, after(b + 1))
                        for t in range(DT):
                            last = pe.transpose(t_ps[:, 128 * t:128 * t + 128], ln.xn[:, 128 * t:128 * t + 128], k.ident[:, :])
                        last.then_inc(xT_ps, 1)
                        pe.wait_ge(c_loaded[nu], loads(b + 1, nu, 2))
                        pe.wait_ge(yT_ready, after(b + 2))
                        pe.wait_ge(square, after(b * 3 + 2))
                        for t in range(DT):
                            pe.matmul(ab_ps[:, 0:S], cT[nu][:, t, :], yT[:, t, :], start=(t == 0), stop=(t == DT - 1))
                        for t in range(DT):
                            last = pe.matmul(bb_ps[:, 0:S], ones[:, :], y2T[:, t, :], start=(t == 0), stop=(t == DT - 1))
                        last.then_inc(products, 1)

                pe.wait_ge(ones_set, after(1))
                in_three_phases(pe, step)


def stage_warp(k, dist, costs, steps, path):
    nc = k.nc
    with ExitStack() as ctx:
        sb = lambda n, s, t=F32: ctx.enter_context(nc.sbuf_tensor("warp_" + n, s, t))
        ps = lambda n, s, t=F32: ctx.enter_context(nc.psum_tensor("warp_" + n, s, t))
        sem = lambda n: k.semaphore(ctx, "warp_" + n)
        W = S + 1
        entry = sb("entry", [128, S])
        iota_j = sb("iota_j", [128, S])
        t_ps = ps("t_ps", [128, 512])
        dist_in, big_set, zero_set, row_min, row_ready, costs_out = map(sem, ("dist_in", "big_set", "zero_set", "row_min", "row_ready", "costs_out"))
        tables_in, bulk, steps_out, steps_in, entry_ready, entry_T, onehot_ready = map(sem, (
            "tables_in", "bulk", "steps_out", "steps_in", "entry_ready", "entry_T", "onehot_ready"))
        with ExitStack() as forward:
            sbf = lambda n, s, t=F32: forward.enter_context(nc.sbuf_tensor("warpf_" + n, s, t))
            dd = sbf("dd", [B, S, S])
            rr = sbf("rr", [B, S, W])
            low = [sbf(f"low{j}", [B, S]) for j in range(2)]
            zeros = sbf("zeros", [B, S])
            big = sbf("big", [B, W])
            with nc.Block() as block:
                @block.sync
                def _(sp):
                    sp.dma_start(dd[:, :, :].rearrange("b i j -> b (i j)"), dist.rearrange("b i j -> b (i j)")).then_inc(dist_in, 16)
                    sp.dma_start(iota_j[:, :], k.ins["c_iota"]).then_inc(dist_in, 16)
                    sp.wait_ge(big_set, after(2))
                    sp.dma_start(costs[:, 0, :], big[:, :]).then_inc(costs_out, 16)
                    sp.wait_ge(row_ready, after(S))
                    sp.dma_start(costs[:, 1:S + 1, :].rearrange("b i j -> b (i j)"), rr[:, :, :].rearrange("b i j -> b (i j)")).then_inc(costs_out, 16)
                    sp.wait_ge(costs_out, after(32))

                @block.gpsimd
                def _(pool):
                    k.prime(pool)
                    pool.memset(big[:, :], BIG).then_inc(big_set, 1)
                    pool.memset(rr[:, :, 0:1], BIG).then_inc(big_set, 1)
                    pool.memset(zeros[:, :], 0.0).then_inc(zero_set, 1)
                    pool.memset(entry[:, :], 0.0).then_inc(zero_set, 1)

                @block.vector
                def _(dve):
                    dve.wait_ge(dist_in, after(32))
                    dve.wait_ge(big_set, after(2))
                    dve.wait_ge(zero_set, after(2))
                    dve.tensor_tensor_scan(rr[:, 0, 1:W], dd[:, 0, :], zeros[:, :], 0.0, ALU.add, ALU.add).then_inc(row_ready, 1)

                    def row(i, j):
                        dve.wait_ge(row_ready, after(i))
                        dve.tensor_tensor(low[j][:, :], rr[:, i - 1, 1:W],
                                          rr[:, i - 1, 0:S], ALU.min).then_inc(row_min, 1)
                        dve.wait_ge(row_min, after(i))
                        dve.tensor_tensor_scan(rr[:, i, 1:W], low[j][:, :],
                                               dd[:, i, :], BIG, ALU.min, ALU.add).then_inc(row_ready, 1)

                    for i in range(1, S):
                        row(i, i % 2)

        with ExitStack() as bulk_ctx:
            sbb = lambda n, s, t=F32: bulk_ctx.enter_context(nc.sbuf_tensor("warpb_" + n, s, t))
            cost, above = sbb("cost", [128, B, W]), sbb("above", [128, B, W])
            low = sbb("lowb", [128, B, S])
            go_left = sbb("go_left", [128, B * S + 8])
            stay, diag = sbb("stay", [128, B, S]), sbb("diag", [128, B, S])
            nxt = sbb("nxt", [128, B * S])
            leftv = go_left[:, 0:B * S].rearrange("p (b j) -> p b j", j=S)
            chase = sbb("chase", [B, S, S])
            hit = sbb("hit", [B, S])
            with nc.Block() as block:
                @block.sync
                def _(sp):
                    sp.dma_start(cost[:, :, :], costs[:, 1:S + 1, :].rearrange("b i j -> i b j")).then_inc(tables_in, 16)
                    sp.dma_start(above[:, :, :], costs[:, 0:S, :].rearrange("b i j -> i b j")).then_inc(tables_in, 16)
                    sp.wait_ge(bulk, after(7))
                    sp.dma_start(steps.rearrange("b i j -> i b j"), nxt[:, :].rearrange("p (b j) -> p b j", j=S)).then_inc(steps_out, 16)
                    sp.wait_ge(steps_out, after(16))
                    sp.dma_start(chase[:, :, :].rearrange("b i j -> b (i j)"), steps.rearrange("b i j -> b (i j)")).then_inc(steps_in, 16)
                    sp.wait_ge(bulk, after(9))
                    sp.dma_start(path.rearrange("i b j -> i (b j)"), nxt[:, :]).then_inc(steps_out, 16)
                    sp.wait_ge(steps_out, after(32))

                @block.vector
                def _(dve):
                    iota_b = iota_j[:, :].unsqueeze(1).to_broadcast([128, B, S])
                    dve.memset(go_left[:, B * S:B * S + 8], 0.0)
                    dve.wait_ge(tables_in, after(32))
                    dve.tensor_tensor(low[:, :, :], above[:, :, 1:W], above[:, :, 0:S], ALU.min).then_inc(bulk, 1)
                    dve.tensor_tensor(diag[:, :, :], above[:, :, 0:S], above[:, :, 1:W], ALU.is_le).then_inc(bulk, 1)
                    dve.wait_ge(bulk, after(2))
                    dve.tensor_tensor(leftv, cost[:, :, 0:S], low[:, :, :], ALU.is_lt).then_inc(bulk, 1)
                    dve.tensor_tensor(stay[:, :, :], cost[:, :, 0:S], low[:, :, :], ALU.is_ge).then_inc(bulk, 1)
                    dve.wait_ge(bulk, after(4))
                    dve.tensor_tensor(low[:, :, :], iota_b, diag[:, :, :], ALU.subtract).then_inc(bulk, 1)
                    dve.wait_ge(bulk, after(5))
                    dve.tensor_tensor(diag[:, :, :], low[:, :, :], stay[:, :, :], ALU.mult).then_inc(bulk, 1)
                    dve.wait_ge(bulk, after(6))
                    dve.tensor_tensor_scan(nxt[:, :], go_left[:, 0:B * S], diag[:, :, :].rearrange("p b j -> p (b j)"), 0.0,
                                           ALU.mult, ALU.add).then_inc(bulk, 1)
                    dve.memset(entry[0:B, S - 1:S], float(S - 1)).then_inc(entry_ready, 1)
                    dve.wait_ge(steps_in, after(16))
                    iota_row = iota_j[0:B, :]

                    def lookup(n):
                        dve.wait_ge(entry_ready, after(n))
                        dve.scalar_tensor_tensor(hit[:, :], iota_row, entry[0:B, S - n:S - n + 1], chase[:, S - n, :],
                                                 ALU.is_equal, ALU.mult,
                                                 accum_out=entry[0:B, S - n - 1:S - n]).then_inc(entry_ready, 1)

                    for n in range(1, S):
                        lookup(n)
                    dve.wait_ge(entry_T, after(1))
                    dve.wait_ge(steps_out, after(16))
                    dve.tensor_tensor(low[:, :, :], iota_b, t_ps[:, 0:B].unsqueeze(2).to_broadcast([128, B, S]), ALU.is_equal).then_inc(bulk, 1)
                    dve.wait_ge(bulk, after(8))
                    dve.tensor_tensor_scan(nxt[:, ::-1], go_left[:, 1:B * S + 1][:, ::-1],
                                           low[:, :, :].rearrange("p b j -> p (b j)")[:, ::-1], 0.0, ALU.mult, ALU.add).then_inc(bulk, 1)

                @block.tensor
                def _(pe):
                    pe.wait_ge(entry_ready, after(S))
                    pe.transpose(t_ps[:, 0:128], entry[:, :], k.ident[:, :]).then_inc(entry_T, 1)


def stage_align_int8(k, x_in, path, x_out, later_weights):
    nc = k.nc
    ROUND = 1.5 * 2.0 ** 23
    QMAX, QMIN, QEPS = 127.0, -128.0, 1e-6
    with ExitStack() as ctx:
        sb = lambda n, s, t=F32: ctx.enter_context(nc.sbuf_tensor("int8_" + n, s, t))
        ps = lambda n, s, t=F32: ctx.enter_context(nc.psum_tensor("int8_" + n, s, t))
        sem = lambda n: k.semaphore(ctx, "int8_" + n)
        x = [sb(f"x{u}", [128, D]) for u in range(2)]
        c = [sb(f"c{u}", [128, D]) for u in range(2)]
        p = [sb(f"p{u}", [128, S]) for u in range(2)]
        xo = [sb(f"xo{u}", [128, D]) for u in range(2)]
        w8, w = sb("w8", [128, DT, D // 4], I32), sb("w", [128, DT, D], BF16)
        w_scale, bias = sb("w_scale", [128, D]), sb("bias", [128, D])
        identb = sb("identb", [128, 128], BF16)
        ln = LayerNorm(k, ctx, "int8_ln")
        xa = sb("xa", [128, 2, D])
        amax, scale, inv = sb("amax", [128, 1]), sb("scale", [128, 1]), sb("inv", [128, 1])
        shifted, q = sb("shifted", [128, D]), sb("q", [128, D], BF16)
        qT = sb("qT", [128, DT, S], BF16)
        scaled, biased = sb("scaled", [128, D]), sb("biased", [128, D])
        e_ps, t_ps, a_ps = ps("e_ps", [128, 512]), ps("t_ps", [128, 1024], BF16), ps("a_ps", [128, 512])
        in_loaded = [sem(f"in_loaded{u}") for u in range(2)]
        x_stored = [sem(f"x_stored{u}") for u in range(2)]
        weights_in, weights_cast, expanded, xa_ready, step_done, qT_ps, qT_ready, acc_done, out_step, xo_ready = map(sem, (
            "weights_in", "weights_cast", "expanded", "xa_ready", "step_done", "qT_ps", "qT_ready", "acc_done", "out_step", "xo_ready"))
        with nc.Block() as block:

            @block.sync
            def _(sp):
                def load(n, v):
                    sp.dma_start(x[v][:, :], x_in[n]).then_inc(in_loaded[v], 16)
                    sp.dma_start(c[v][:, :], k.ins["ctx_1024"][n]).then_inc(in_loaded[v], 16)
                    sp.dma_start(p[v][:, :], path[:, bass.ds(n, 1), :].rearrange("i a j -> i (a j)")).then_inc(in_loaded[v], 16)

                def step(b, u, front=True, main=True):
                    if main:
                        if not isinstance(b, int) or b + 2 < B:
                            sp.wait_ge(xa_ready, after(b + 1))
                            load(b + 2, u)
                        sp.wait_ge(xo_ready, after(b + 1))
                        sp.dma_start(x_out[b], xo[u][:, :]).then_inc(x_stored[u], 16)

                load(0, 0)
                sp.dma_start(w8[:, :, :], k.ins["w_int8T"].rearrange("(t p) n -> p t n", p=128)).then_inc(weights_in, 16)
                sp.dma_start(w_scale[:, :], k.ins["L1_ffn_weight_scale"].rearrange("(a n) -> a n", a=1).to_broadcast([128, D])).then_inc(weights_in, 16)
                sp.dma_start(bias[:, :], k.ins["L1_ffn_bias"].rearrange("(a n) -> a n", a=1).to_broadcast([128, D])).then_inc(weights_in, 16)
                load(1, 1)
                in_two_phases(sp, step)
                for u in range(2):
                    sp.wait_ge(x_stored[u], after(16 * B // 2))

            @block.gpsimd
            def _(pool):
                k.prime(pool)
                pool.tensor_copy(identb[:, :], k.ident[:, :]).then_inc(weights_cast, 1)
                pool.wait_ge(weights_in, after(48))
                pool.tensor_copy(w[:, :, :], w8[:, :, :].bitcast(I8)).then_inc(weights_cast, 1)
                with pool.Fori(0, B) as b:
                    ln.inverse_root(pool, b)

            @block.scalar
            def _(act):
                for w_later in later_weights:
                    w_later.load(act)

            @block.vector
            def _(dve):
                def step(b, u, front=True, main=True):
                    nu = 1 - u
                    n = b + 1
                    if front:
                        dve.wait_ge(in_loaded[nu], loads(n, nu, 3))
                        dve.wait_ge(expanded, after(n + 1))
                        dve.wait_ge(xo_ready, after(n - 1))
                        dve.scalar_tensor_tensor(xa[:, nu, :], e_ps[:, 0:D], k.gates[:, 1:2], x[nu][:, :],
                                                 ALU.mult, ALU.add).then_inc(xa_ready, 1)
                        dve.wait_ge(xa_ready, after(n + 1))
                        ln.statistics(dve, n, xa[:, nu, :])
                    if main:
                        dve.wait_ge(qT_ps, after(b + 1))
                        dve.wait_ge(acc_done, after(b))
                        dve.tensor_scalar(qT[:, :, :], t_ps[:, 0:D].rearrange("p (t s) -> p t s", s=S), QMIN, None, ALU.max).then_inc(qT_ready, 1)
                        dve.wait_ge(acc_done, after(b + 1))
                        dve.scalar_tensor_tensor(scaled[:, :], a_ps[:, 0:D], scale[:, :], w_scale[:, :], ALU.mult, ALU.mult).then_inc(out_step, 1)
                        dve.wait_ge(out_step, after(b * 2 + 1))
                        dve.tensor_tensor(biased[:, :], scaled[:, :], bias[:, :], ALU.add).then_inc(out_step, 1)
                        dve.wait_ge(out_step, after(b * 2 + 2))
                        dve.wait_ge(x_stored[u], stores(b, u))
                        dve.scalar_tensor_tensor(xo[u][:, :], biased[:, :], k.gates[:, 5:6], xa[:, u, :], ALU.mult, ALU.add).then_inc(xo_ready, 1)
                    if front:
                        ln.normalize(dve, n, xa[:, nu, :])
                        dve.wait_ge(ln.xn_ready, after(n + 1))
                        dve.tensor_reduce(amax[:, :], ln.xn[:, :], AX.X, ALU.max, apply_absolute_value=True).then_inc(step_done, 1)
                        dve.wait_ge(step_done, after(n * 5 + 1))
                        dve.wait_ge(out_step, after(n * 2))
                        dve.tensor_scalar(scale[:, :], amax[:, :], QEPS, 1.0 / QMAX, ALU.max, ALU.mult).then_inc(step_done, 1)
                        dve.wait_ge(step_done, after(n * 5 + 2))
                        dve.reciprocal(inv[:, :], scale[:, :]).then_inc(step_done, 1)
                        dve.wait_ge(step_done, after(n * 5 + 3))
                        dve.tensor_scalar(shifted[:, :], ln.xn[:, :], inv[:, :], ROUND, ALU.mult, ALU.add).then_inc(step_done, 1)
                        dve.wait_ge(step_done, after(n * 5 + 4))
                        dve.wait_ge(qT_ps, after(n))
                        dve.tensor_scalar(q[:, :], shifted[:, :], -ROUND, QMAX, ALU.add, ALU.min).then_inc(step_done, 1)
                        if not main:
                            dve.wait_ge(weights_in, after(48))

                in_two_phases(dve, step)

            @block.tensor
            def _(pe):
                def step(b, u, front=True, main=True):
                    nu = 1 - u
                    if front:
                        pe.wait_ge(in_loaded[nu], loads(b + 1, nu, 3))
                        pe.wait_ge(xa_ready, after(b + 1))
                        pe.matmul(e_ps[:, 0:D], p[nu][:, :], c[nu][:, :], start=True, stop=True).then_inc(expanded, 1)
                        if not main:
                            pe.wait_ge(weights_cast, after(2))
                    if main:
                        pe.wait_ge(step_done, after(b * 5 + 5))
                        pe.wait_ge(qT_ready, after(b))
                        for t in range(DT):
                            last = pe.transpose(t_ps[:, 128 * t:128 * t + 128], q[:, 128 * t:128 * t + 128], identb[:, :])
                        last.then_inc(qT_ps, 1)
                    if main:
                        pe.wait_ge(qT_ready, after(b + 1))
                        pe.wait_ge(out_step, after(b * 2))
                        for t in range(DT):
                            last = pe.matmul(a_ps[:, 0:D], qT[:, t, :], w[:, t, :], start=(t == 0), stop=(t == DT - 1))
                        last.then_inc(acc_done, 1)

                in_two_phases(pe, step)


def sinusoid_reversed_T():
    f = np.float32
    pos = np.arange(S - 1, -1, -1, dtype=f)
    n = D // 2
    inv = np.exp(np.arange(n, dtype=f) * f(-math.log(10000.0) / (n - 1))).astype(f)
    st = (pos[:, None] * inv[None, :]).astype(f)
    return np.ascontiguousarray(np.concatenate([np.sin(st), np.cos(st)], axis=-1).astype(f).T)


class AttentionWeights:

    def __init__(self, k, ctx, layer, relative):
        sb = lambda n, s: ctx.enter_context(k.nc.sbuf_tensor(f"{layer}_{n}", s, F32))
        self.ins, self.layer, self.relative = k.ins, layer, relative
        self.nc = k.nc
        self.loaded = k.nc.alloc_semaphore(f"{layer}_weights_loaded")
        self.LOADED = 16 * (13 if relative else 8)
        self.wq, self.wk, self.wv, self.wo = (sb(n, [128, DT, D]) for n in ("wq", "wk", "wv", "wo"))
        self.bq, self.bk = sb("bq", [128, DT]), sb("bk", [128, DT])
        self.bv, self.bo = sb("bv", [128, D]), sb("bo", [128, D])
        if relative:
            self.wp, self.sinT, self.bp = sb("wp", [128, DT, D]), sb("sinT", [128, DT, S]), sb("bp", [128, DT])
            self.rw, self.rr = sb("rw", [128, DT]), sb("rr", [128, DT])

    def load(self, engine):
        w = lambda n: self.ins[f"{self.layer}_xattn_{n}"]
        column = lambda a: a.rearrange("(t p) -> p t", p=128)
        row = lambda a: a.rearrange("(a n) -> a n", a=1).to_broadcast([128, D])
        for tile, name in ((self.wq, "Wq"), (self.wk, "Wk"), (self.wv, "Wv"), (self.wo, "Wo")):
            engine.dma_start(tile[:, :, :], w(name).rearrange("(t p) n -> p t n", p=128)).then_inc(self.loaded, 16)
        with self.nc.allow_non_contiguous_dma(reason="small bias columns"):
            engine.dma_start(self.bq[:, :], column(w("bq"))).then_inc(self.loaded, 16)
            engine.dma_start(self.bk[:, :], column(w("bk"))).then_inc(self.loaded, 16)
            if self.relative:
                engine.dma_start(self.bp[:, :], column(w("bp"))).then_inc(self.loaded, 16)
                engine.dma_start(self.rw[:, :], column(w("r_w_bias").rearrange("a b h d -> (a b h d)"))).then_inc(self.loaded, 16)
                engine.dma_start(self.rr[:, :], column(w("r_r_bias").rearrange("a b h d -> (a b h d)"))).then_inc(self.loaded, 16)
        engine.dma_start(self.bv[:, :], row(w("bv"))).then_inc(self.loaded, 16)
        engine.dma_start(self.bo[:, :], row(w("bo"))).then_inc(self.loaded, 16)
        if self.relative:
            engine.dma_start(self.wp[:, :, :], w("Wp").rearrange("(t p) n -> p t n", p=128)).then_inc(self.loaded, 16)
            engine.dma_start(self.sinT[:, :, :], self.ins["c_sinT"].rearrange("(t p) s -> p t s", p=128)).then_inc(self.loaded, 16)


def stage_attention(k, x_in, x_out, layer, gate, relative, weights, bounce=None):
    nc = k.nc
    SCALE = 1.0 / math.sqrt(HD)
    with ExitStack() as ctx:
        sb = lambda n, s, t=F32: ctx.enter_context(nc.sbuf_tensor(f"{layer}_{n}", s, t))
        ps = lambda n, s, t=F32: ctx.enter_context(nc.psum_tensor(f"{layer}_{n}", s, t))
        sem = lambda n: k.semaphore(ctx, f"{layer}_{n}")
        x = [sb(f"x{u}", [128, D]) for u in range(2)]
        res = [sb(f"res{u}", [128, D]) for u in range(2)]
        cT = [sb(f"cT{u}", [128, DT, S]) for u in range(2)]
        xo = [sb(f"xo{u}", [128, D]) for u in range(2)]
        wq, wk, wv, wo = weights.wq, weights.wk, weights.wv, weights.wo
        bq, bk, bv, bo = weights.bq, weights.bk, weights.bv, weights.bo
        ones = sb("ones", [1, 128])
        ln = LayerNorm(k, ctx, f"{layer}_ln")
        xnT = sb("xnT", [128, DT, S])
        qT = sb("qT", [128, DT, S])
        kz = sb("kz", [128, DT, 2, S])
        v = sb("v", [128, 2, D])
        prob = sb("prob", [128, H, S])
        nmax, total, rtotal = sb("nmax", [128, H]), sb("total", [128, H]), sb("rtotal", [128, H])
        smax = nmax if relative else sb("smax", [128, H])
        pT = sb("pT", [128, H, S])
        o_even, oT = sb("o_even", [128, DT, S]), sb("oT", [128, DT, S])
        gbo = sb("gbo", [128, D])
        if relative:
            mask = [sb(f"mask{u}", [128, S]) for u in range(2)]
            wp, sinT, bp, rw, rr = weights.wp, weights.sinT, weights.bp, weights.rw, weights.rr
            pz = sb("pz", [128, DT, 2, S])
            qrT = sb("qrT", [128, DT, S])
            rel = sb("rel", [128, S + 1, H])
            shifted = sb("shifted", [128, S, H])
            mask_s, mask_add = sb("mask_s", [128, S]), sb("mask_add", [128, S])
            att, masked = sb("att", [128, H, S]), sb("masked", [128, H, S])

        a_ps = ps("a_ps", [128, 512])
        b_ps = ps("b_ps", [128, 512])
        r_ps = [ps(f"r_ps{j}", [128, 4, S]) for j in range(2)]
        s_ps = [ps(f"s_ps{j}", [128, 4, S]) for j in range(4)]
        pair_out = b_ps[:, :].rearrange("p (t two s) -> p t two s", two=2, s=S)

        parity = lambda n: [sem(f"{n}{u}") for u in range(2)]
        x_loaded, res_loaded, cT_loaded, x_stored = map(parity, ("x_loaded", "res_loaded", "cT_loaded", "x_stored"))
        setup, pe_ps = sem("setup"), sem("pe_ps")
        xT_ps, xT_ready, qk_done, v_done, q_ready, k_ready, v_ready, res_ready = map(sem, (
            "xT_ps", "xT_ready", "qk_done", "v_done", "q_ready", "k_ready", "v_ready", "res_ready"))
        s_done, max_ready, prob_ready, rt_ready, norm_ready, pT_ps, pT_ready, pT_ready_act = map(sem, (
            "s_done", "max_ready", "prob_ready", "rt_ready", "norm_ready", "pT_ps", "pT_ready", "pT_ready_act"))
        o_done, even_ready, oT_ready, out_done, xo_ready = map(sem, (
            "o_done", "even_ready", "oT_ready", "out_done", "xo_ready"))
        if relative:
            mask_loaded = parity("mask_loaded")
            rel_done, rel_out, rel_written, rel_read, mask_ready, att_ready, masked_ready, added = map(sem, (
                "rel_done", "rel_out", "rel_written", "rel_read", "mask_ready", "att_ready", "masked_ready", "added"))
        else:
            scaled_max = sem("scaled_max")
        n_setup = 1 + (7 if relative else 0)

        with nc.Block() as block:

            @block.sync
            def _(sp):
                def load_x(n, v):
                    sp.dma_start(x[v][:, :], x_in[n]).then_inc(x_loaded[v], 16)

                def load_residual(n, v):
                    sp.dma_start(res[v][:, :], x_in[n]).then_inc(res_loaded[v], 16)

                def load_context(n, v):
                    sp.dma_start(cT[v][:, :, :], k.ins["ctxT_pairs"][n, 0].rearrange("(t p) s -> p t s", p=128)).then_inc(cT_loaded[v], 16)

                def load_mask(n, v):
                    sp.dma_start(mask[v][:, :], k.ins["mask_Bx1xSxS2_ff1"][n, 0]).then_inc(mask_loaded[v], 16)

                load_x(0, 0)
                load_x(1, 1)
                for v_ in range(2):
                    load_context(v_, v_)
                    load_residual(v_, v_)
                    if relative:
                        load_mask(v_, v_)

                def step(b, u, ahead=True, front=True, middle=True, tail=True):
                    nu = 1 - u
                    more = not isinstance(b, int) or b + 3 < B
                    b_less = not isinstance(b, int) or b + 2 < B
                    if ahead:
                        if more:
                            sp.wait_ge(ln.xn_ready, after(b + 2))
                            load_x(b + 3, nu)
                            sp.wait_ge(v_done, after(b + 2))
                            load_context(b + 3, nu)
                    if tail:
                        sp.wait_ge(xo_ready, after(b))
                        sp.dma_start(x_out[b - 1], xo[nu][:, :]).then_inc(x_stored[nu], 16)
                        if not isinstance(b, int) or b + 1 < B:
                            load_residual(b + 1, nu)
                    if front and relative:
                        sp.wait_ge(rel_out, after(b * 4 + 8))
                        sp.dma_start(bounce[nu][0:S * (S + 1) * H].rearrange("(s n) -> s n", s=S),
                                     rel[:, :, :].rearrange("p j h -> p (j h)")).then_inc(rel_written, 16)
                        sp.wait_ge(rel_written, after(b * 16 + 32))
                        sp.dma_start(shifted[:, :, :].rearrange("p j h -> p (j h)"),
                                     bounce[nu][S * H:S * H + S * S * H].rearrange("(s n) -> s n", s=S)).then_inc(rel_read, 16)
                        if middle and b_less:
                            sp.wait_ge(mask_ready, after(b + 1))
                            load_mask(b + 2, u)

                in_three_phases(sp, step)
                for u in range(2):
                    sp.wait_ge(x_stored[u], after(16 * B // 2))

            @block.gpsimd
            def _(pool):
                def step(b, u, ahead=True, front=True, middle=True, tail=True):
                    nu = 1 - u
                    if middle and relative:
                        for g in range(4):
                            heads = slice(4 * g, 4 * g + 4)
                            pool.wait_ge(masked_ready, after(b * 4 + (g + 1)))
                            pool.tensor_tensor(att[:, heads, :], masked[:, heads, :], mask_add[:, :].unsqueeze(1).to_broadcast([128, 4, S]),
                                               ALU.add).then_inc(added, 1)
                    if ahead:
                        ln.inverse_root(pool, b + 2)
                    if front:
                        pool.wait_ge(res_loaded[nu], loads(b + 1, nu))
                        pool.tensor_tensor(res[nu][:, :], res[nu][:, :], gbo[:, :], ALU.add).then_inc(res_ready, 1)

                k.prime(pool)
                if relative:
                    pool.memset(rel[:, :, :], 0.0).then_inc(setup, 1)
                ln.inverse_root(pool, 0)
                pool.wait_ge(setup, after(n_setup))
                in_three_phases(pool, step)

            @block.vector
            def _(dve):
                def layer_norm(n, v):
                    dve.wait_ge(x_loaded[v], loads(n, v))
                    ln.statistics(dve, n, x[v][:, :])
                    dve.wait_ge(xT_ps, after(n))
                    ln.normalize(dve, n, x[v][:, :])

                def keys(n):
                    dve.wait_ge(q_ready, after(n + 1))
                    dve.wait_ge(s_done, after(n * 4))
                    for t in range(DT):
                        for par in range(2):
                            last = dve.tensor_scalar(kz[:, t, par, :], a_ps[:, D + t * S:D + t * S + S], bk[:, t:t + 1],
                                                     k.pair_mask[:, par:par + 1], ALU.add, ALU.mult)
                    last.then_inc(k_ready, 1)

                def outputs_transposed(n):
                    dve.wait_ge(even_ready, after(n + 1))
                    dve.wait_ge(out_done, after(n))
                    dve.scalar_tensor_tensor(oT[:, :, :], pair_out[:, :, 1, :], k.pair_mask[:, 1:2], o_even[:, :, :],
                                             ALU.mult, ALU.add).then_inc(oT_ready, 1)

                def values(n, v_):
                    dve.wait_ge(v_done, after(n + 1))
                    dve.wait_ge(out_done, after(n - 1))
                    dve.tensor_tensor(v[:, v_, :], b_ps[:, 0:D], bv[:, :], ALU.add).then_inc(v_ready, 1)

                def result(n, v_):
                    dve.wait_ge(out_done, after(n + 1))
                    dve.wait_ge(res_ready, after(n + 1))
                    dve.wait_ge(x_stored[v_], stores(n, v_))
                    dve.scalar_tensor_tensor(xo[v_][:, :], b_ps[:, D:2 * D], k.gates[:, gate:gate + 1], res[v_][:, :],
                                             ALU.mult, ALU.add).then_inc(xo_ready, 1)

                def over_sums(b, g):
                    heads = slice(4 * g, 4 * g + 4)
                    dve.wait_ge(prob_ready, after(b * 4 + (g + 1)))
                    dve.wait_ge(norm_ready, after(b * 4 + g))
                    dve.reciprocal(rtotal[:, heads], total[:, heads]).then_inc(rt_ready, 1)
                    dve.wait_ge(rt_ready, after(b * 4 + (g + 1)))
                    dve.tensor_tensor(prob[:, heads, :], prob[:, heads, :], rtotal[:, heads].unsqueeze(2).to_broadcast([128, 4, S]),
                                      ALU.mult).then_inc(norm_ready, 1)

                def copy_transposed(b, g):
                    dve.wait_ge(pT_ps, after(b * 4 + (g + 1)))
                    dve.wait_ge(o_done, after(b))
                    dve.tensor_copy(pT[:, 4 * g:4 * g + 4, :], r_ps[1][:, :, :]).then_inc(pT_ready, 1)

                layer_norm(0, 0)
                dve.wait_ge(weights.loaded, weights.LOADED)
                dve.tensor_scalar(gbo[:, :], bo[:, :], k.gates[:, gate:gate + 1], None, ALU.mult).then_inc(setup, 1)
                if relative:
                    dve.tensor_tensor(rw[:, :], rw[:, :], bq[:, :], ALU.add).then_inc(setup, 1)
                    dve.tensor_tensor(rr[:, :], rr[:, :], bq[:, :], ALU.add).then_inc(setup, 1)
                    dve.wait_ge(pe_ps, after(1))
                    for t in range(DT):
                        for par in range(2):
                            dve.tensor_scalar(pz[:, t, par, :], a_ps[:, t * S:t * S + S], bp[:, t:t + 1],
                                              k.pair_mask[:, par:par + 1], ALU.add, ALU.mult).then_inc(setup, 1)

                def step_relative(b, u, ahead=True, front=True, middle=True, tail=True):
                    nu = 1 - u
                    if tail:
                        outputs_transposed(b - 1)
                    if middle:
                        dve.wait_ge(rel_read, after(b * 16 + 16))
                        dve.wait_ge(added, after(b * 4))
                        for r in range(4):
                            dve.wait_ge(s_done, after(b * 4 + (r + 1)))
                            dve.wait_ge(prob_ready, after(b * 4))
                            dve.tensor_tensor(att[:, 4 * r:4 * r + 4, :], s_ps[r][:, :, :],
                                              shifted[:, :, 4 * r:4 * r + 4].rearrange("p j h -> p h j"), ALU.add).then_inc(att_ready, 1)
                    def times_mask(g):
                        heads = slice(4 * g, 4 * g + 4)
                        dve.wait_ge(att_ready, after(b * 4 + (g + 1)))
                        dve.tensor_tensor(masked[:, heads, :], att[:, heads, :], mask_s[:, :].unsqueeze(1).to_broadcast([128, 4, S]),
                                          ALU.mult).then_inc(masked_ready, 1)

                    def maxima(g):
                        heads = slice(4 * g, 4 * g + 4)
                        dve.wait_ge(added, after(b * 4 + (g + 1)))
                        dve.tensor_reduce(nmax[:, heads], att[:, heads, :], AX.X, ALU.max, negate=True).then_inc(max_ready, 1)

                    if middle:
                        dve.wait_ge(mask_loaded[u], loads(b, u))
                        dve.tensor_scalar(mask_s[:, :], mask[u][:, :], SCALE, None, ALU.mult)
                        dve.tensor_scalar(mask_add[:, :], mask[u][:, :], -1.0, 1.0e10, ALU.add, ALU.mult).then_inc(mask_ready, 1)
                        dve.wait_ge(mask_ready, after(b + 1))
                        times_mask(0)
                        times_mask(1)
                    if front:
                        keys(b + 1)
                        values(b + 1, nu)
                    if tail:
                        result(b - 1, nu)
                    if middle:
                        maxima(0)
                        times_mask(2)
                        maxima(1)
                        times_mask(3)
                        maxima(2)
                        over_sums(b, 0)
                        maxima(3)
                        over_sums(b, 1)
                    if ahead:
                        layer_norm(b + 2, u)
                    if middle:
                        over_sums(b, 2)
                        copy_transposed(b, 1)
                        over_sums(b, 3)
                        copy_transposed(b, 3)

                def step_plain(b, u, ahead=True, front=True, middle=True, tail=True):
                    nu = 1 - u
                    if tail:
                        outputs_transposed(b - 1)
                    if middle:
                        over_sums(b, 0)
                    if front:
                        keys(b + 1)
                        values(b + 1, nu)
                    if tail:
                        result(b - 1, nu)
                    if middle:
                        over_sums(b, 1)
                        over_sums(b, 2)
                        over_sums(b, 3)
                    if ahead:
                        layer_norm(b + 2, u)

                    def maxima(r):
                        heads = slice(4 * r, 4 * r + 4)
                        dve.wait_ge(s_done, after(b * 4 + (r + 5)))
                        dve.tensor_reduce(nmax[:, heads], s_ps[r][:, :, :], AX.X, ALU.max, negate=True).then_inc(max_ready, 1)
                        dve.wait_ge(max_ready, after(b * 4 + (r + 5)))
                        dve.wait_ge(prob_ready, after(b * 4 + (r + 1)))
                        dve.tensor_scalar(smax[:, heads], nmax[:, heads], SCALE, None, ALU.mult).then_inc(scaled_max, 1)

                    if front:
                        maxima(0)
                    if middle:
                        copy_transposed(b, 1)
                    if front:
                        maxima(1)
                    if middle:
                        copy_transposed(b, 3)
                    if front:
                        maxima(2)
                        maxima(3)

                in_three_phases(dve, step_relative if relative else step_plain)

            @block.scalar
            def _(act):
                def exponentials(b, g, source, bias, bias_ready, scale):
                    act.wait_ge(bias_ready, after(b * 4 + (g + 1)))
                    act.wait_ge(rt_ready, after(b * 4))
                    act.wait_ge(pT_ps, after(b * 4))
                    for j in range(4):
                        h = 4 * g + j
                        last = act.activation(prob[:, h, :], source(h), ACT.Exp, bias=bias[:, h:h + 1], scale=scale,
                                              accum_out=total[:, h:h + 1])
                    last.then_inc(prob_ready, 1)

                def even_outputs(n):
                    act.wait_ge(o_done, after(n + 1))
                    act.wait_ge(oT_ready, after(n))
                    act.activation(o_even[:, :, :], pair_out[:, :, 0, :], ACT.Copy, scale=k.pair_mask[:, 0:1]).then_inc(even_ready, 1)

                def copy_x(n):
                    act.wait_ge(xT_ps, after(n + 1))
                    act.wait_ge(qk_done, after(n))
                    act.activation(xnT[:, :, :], a_ps[:, 0:D].rearrange("p (t s) -> p t s", s=S), ACT.Copy).then_inc(xT_ready, 1)

                def step(b, u, ahead=True, front=True, middle=True, tail=True):
                    nu = 1 - u
                    if tail and relative:
                        even_outputs(b - 1)
                    if front:
                        act.wait_ge(qk_done, after(b + 2))
                        act.wait_ge(s_done, after(b * 4 + 4))
                        for t in range(DT):
                            if relative:
                                act.activation(qrT[:, t, :], a_ps[:, t * S:t * S + S], ACT.Identity, bias=rr[:, t:t + 1])
                            last = act.activation(qT[:, t, :], a_ps[:, t * S:t * S + S], ACT.Identity,
                                                  bias=(rw if relative else bq)[:, t:t + 1])
                        last.then_inc(q_ready, 1)
                    if middle and not relative:
                        for g in (2, 3):
                            exponentials(b, g, lambda h: s_ps[h // 4][:, h % 4, :], smax, scaled_max, SCALE)

                    def relative_out(r):
                        act.wait_ge(rel_done, after(b * 4 + (r + 5)))
                        act.activation(rel[:, 1:S + 1, 4 * r:4 * r + 4].rearrange("p j h -> p h j"), r_ps[r % 2][:, :, :],
                                       ACT.Copy).then_inc(rel_out, 1)

                    if front and relative:
                        act.wait_ge(rel_written, after(b * 16 + 16))
                        act.wait_ge(att_ready, after(b * 4 + 4))
                        relative_out(0)
                        relative_out(1)
                    for g in range(4):
                        if middle and relative:
                            exponentials(b, g, lambda h: att[:, h, :], nmax, max_ready, 1.0)
                        if front and relative and g < 2:
                            relative_out(g + 2)
                    for g in (0, 2):
                        if middle:
                            act.wait_ge(pT_ps, after(b * 4 + (g + 1)))
                            act.wait_ge(o_done, after(b))
                            act.activation(pT[:, 4 * g:4 * g + 4, :], r_ps[0][:, :, :], ACT.Copy).then_inc(pT_ready_act, 1)
                    if ahead:
                        copy_x(b + 2)
                    if front and not relative:
                        exponentials(b + 1, 0, lambda h: s_ps[h // 4][:, h % 4, :], smax, scaled_max, SCALE)
                    if middle and not relative:
                        even_outputs(b)
                    if front and not relative:
                        exponentials(b + 1, 1, lambda h: s_ps[h // 4][:, h % 4, :], smax, scaled_max, SCALE)

                act.wait_ge(weights.loaded, weights.LOADED)
                act.wait_ge(setup, after(n_setup))
                copy_x(0)
                in_three_phases(act, step)

            @block.tensor
            def _(pe):
                pe.wait_ge(weights.loaded, weights.LOADED)
                if relative:
                    for m in range(DT):
                        for t in range(DT):
                            last = pe.matmul(a_ps[:, m * S:m * S + S], wp[:, t, 128 * m:128 * m + 128], sinT[:, t, :],
                                             start=(t == 0), stop=(t == DT - 1))
                    last.then_inc(pe_ps, 1)
                pe.wait_ge(setup, after(n_setup))

                def transpose_x(n):
                    pe.wait_ge(ln.xn_ready, after(n + 1))
                    pe.wait_ge(k_ready, after(n))
                    for t in range(DT):
                        last = pe.transpose(a_ps[:, 128 * t:128 * t + 128], ln.xn[:, 128 * t:128 * t + 128], k.ident[:, :])
                    last.then_inc(xT_ps, 1)

                def step(b, u, ahead=True, front=True, middle=True, tail=True):
                    nu = 1 - u
                    if front:
                        pe.wait_ge(cT_loaded[nu], loads(b + 1, nu))
                        pe.wait_ge(xT_ready, after(b + 2))
                        for off, wt, src in ((0, wq, xnT), (D, wk, cT[nu])):
                            for m in range(DT):
                                for t in range(DT):
                                    last = pe.matmul(a_ps[:, off + m * S:off + m * S + S], wt[:, t, 128 * m:128 * m + 128],
                                                     src[:, t, :], start=(t == 0), stop=(t == DT - 1))
                        last.then_inc(qk_done, 1)
                        if tail:
                            pe.wait_ge(oT_ready, after(b))
                        elif middle:
                            pe.wait_ge(v_ready, after(b + 1))
                        for t in range(DT):
                            last = pe.matmul(b_ps[:, 0:D], cT[nu][:, t, :], wv[:, t, :], start=(t == 0), stop=(t == DT - 1))
                        last.then_inc(v_done, 1)
                    if tail:
                        pe.wait_ge(oT_ready, after(b))
                        for t in range(DT):
                            last = pe.matmul(b_ps[:, D:2 * D], oT[:, t, :], wo[:, t, :], start=(t == 0), stop=(t == DT - 1))
                        last.then_inc(out_done, 1)
                    if front:
                        pe.wait_ge(q_ready, after(b + 2))
                        if relative:
                            for r in range(4):
                                if r < 2:
                                    pe.wait_ge(pT_ready if r else pT_ready_act, after(b * 2))
                                else:
                                    pe.wait_ge(rel_out, after(b * 4 + (r + 3)))
                                rows = slice(32 * r, 32 * r + 32)
                                for half in range(2):
                                    last = pe.matmul(r_ps[r % 2][:, 2 * half:2 * half + 2, :], qrT[rows, half, :],
                                                     pz[rows, half, :, :], start=True, stop=True, tile_position=(32 * r, 0))
                                last.then_inc(rel_done, 1)
                        pe.wait_ge(k_ready, after(b + 2))
                        for r in range(4):
                            pe.wait_ge(att_ready if relative else prob_ready, after(b * 4 + (r + 1)))
                            rows = slice(32 * r, 32 * r + 32)
                            for half in range(2):
                                last = pe.matmul(s_ps[r][:, 2 * half:2 * half + 2, :], qT[rows, half, :], kz[rows, half, :, :],
                                                 start=True, stop=True, tile_position=(32 * r, 0))
                            last.then_inc(s_done, 1)
                    if middle:
                        for g in range(4):
                            if g >= 2:
                                pe.wait_ge(pT_ready if g % 2 else pT_ready_act, after(b * 2 + 1))
                            elif relative:
                                pe.wait_ge(rel_out, after(b * 4 + 8) if front else after(B * 4))
                            else:
                                pe.wait_ge(pT_ready if g % 2 else pT_ready_act, after(b * 2))
                            pe.wait_ge(norm_ready, after(b * 4 + (g + 1)))
                            for j in range(4):
                                last = pe.transpose(r_ps[g % 2][:, j, :], prob[:, 4 * g + j, :], k.ident[:, :])
                            last.then_inc(pT_ps, 1)
                    if ahead:
                        transpose_x(b + 2)
                    if middle:
                        if front:
                            pe.wait_ge(v_ready, after(b + 2))
                        if tail:
                            pe.wait_ge(xo_ready, after(b))
                        pe.wait_ge(pT_ready, after(b * 2 + 2))
                        pe.wait_ge(pT_ready_act, after(b * 2 + 2))
                        for half in range(2):
                            for g in range(4):
                                pair = 4 * half + g
                                last = pe.matmul(pair_out[32 * g:32 * g + 32, half, :, :], v[:, u, 32 * pair:32 * pair + 32],
                                                 pT[:, 4 * g + 2 * half:4 * g + 2 * half + 2, :], start=True, stop=True,
                                                 tile_position=(0, 32 * g))
                        last.then_inc(o_done, 1)

                transpose_x(0)
                in_three_phases(pe, step)


FF, RANK = 1024, 64


class LowRankWeights:
    LOADED = 16 * 6

    def __init__(self, k, ctx):
        sb = lambda n, s: ctx.enter_context(k.nc.sbuf_tensor("lr_" + n, s, F32))
        self.ins = k.ins
        self.loaded = k.nc.alloc_semaphore("lr_weights_loaded")
        self.u1, self.v1 = sb("u1", [128, DT, RANK]), sb("v1", [RANK + 1, FF])
        self.u2, self.v2 = sb("u2", [128, FF // 128, RANK]), sb("v2", [RANK + 1, D])

    def load(self, engine):
        row = lambda a: a.rearrange("(a n) -> a n", a=1)
        engine.dma_start(self.u1[:, :, :], self.ins["L2_ffn_U1"].rearrange("(t p) n -> p t n", p=128)).then_inc(self.loaded, 16)
        engine.dma_start(self.u2[:, :, :], self.ins["L2_ffn_U2"].rearrange("(t p) n -> p t n", p=128)).then_inc(self.loaded, 16)
        engine.dma_start(self.v1[0:RANK, :], self.ins["L2_ffn_V1"]).then_inc(self.loaded, 16)
        engine.dma_start(self.v1[RANK:RANK + 1, :], row(self.ins["L2_ffn_b1"])).then_inc(self.loaded, 16)
        engine.dma_start(self.v2[0:RANK, :], self.ins["L2_ffn_V2"]).then_inc(self.loaded, 16)
        engine.dma_start(self.v2[RANK:RANK + 1, :], row(self.ins["L2_ffn_b2"])).then_inc(self.loaded, 16)


def stage_low_rank_ffn(k, x_in, x_out, weights):
    nc = k.nc
    FT = FF // 128
    with ExitStack() as ctx:
        sb = lambda n, s, t=F32: ctx.enter_context(nc.sbuf_tensor("lr_" + n, s, t))
        ps = lambda n, s, t=F32: ctx.enter_context(nc.psum_tensor("lr_" + n, s, t))
        sem = lambda n: k.semaphore(ctx, "lr_" + n)
        x = [sb(f"x{u}", [128, D]) for u in range(2)]
        xo = [sb(f"xo{u}", [128, D]) for u in range(2)]
        res = [sb(f"res{u}", [128, D]) for u in range(2)]
        u1, v1, u2, v2 = weights.u1, weights.v1, weights.u2, weights.v2
        ln = LayerNorm(k, ctx, "lr_ln")
        xnT = sb("xnT", [128, DT, S])
        p, q = sb("p", [RANK + 1, S]), sb("q", [RANK + 1, S])
        h = sb("h", [128, FT, S])
        t_ps, p_ps, q_ps, o_ps = (ps(n, [128, 512]) for n in ("t_ps", "p_ps", "q_ps", "o_ps"))
        h_ps = [ps(f"h_ps{j}", [128, 4, S]) for j in range(2)]
        x_loaded, res_loaded, x_stored = ([sem(f"{n}{u}") for u in range(2)] for n in ("x_loaded", "res_loaded", "x_stored"))
        ones_set, xT_ps, xT_ready, p_done, p_ready, h_done, h_ready, q_done, q_ready, out_done, xo_ready = map(sem, (
            "ones_set", "xT_ps", "xT_ready", "p_done", "p_ready", "h_done", "h_ready", "q_done", "q_ready", "out_done", "xo_ready"))
        table_pull, table_in = sb("table_pull", [128, 1]), sem("table_in")
        with nc.Block() as block:

            @block.sync
            def _(sp):
                def load_x(n, v):
                    sp.dma_start(x[v][:, :], x_in[n]).then_inc(x_loaded[v], 16)

                def load_residual(n, v):
                    sp.dma_start(res[v][:, :], x_in[n]).then_inc(res_loaded[v], 16)

                load_x(0, 0)
                load_x(1, 1)
                load_residual(0, 0)
                load_residual(1, 1)

                def step(b, u, ahead=True, front=True, middle=True, tail=True):
                    nu = 1 - u
                    more = not isinstance(b, int) or b + 3 < B
                    if ahead and more:
                        sp.wait_ge(ln.xn_ready, after(b + 2))
                        load_x(b + 3, nu)
                    if tail:
                        sp.wait_ge(xo_ready, after(b))
                        sp.dma_start(x_out[b - 1], xo[nu][:, :]).then_inc(x_stored[nu], 16)
                        if not isinstance(b, int) or b + 1 < B:
                            load_residual(b + 1, nu)

                in_three_phases(sp, step)
                for u in range(2):
                    sp.wait_ge(x_stored[u], after(16 * B // 2))

            @block.gpsimd
            def _(pool):
                k.prime(pool)
                pool.memset(p[RANK:RANK + 1, :], 1.0).then_inc(ones_set, 1)
                pool.memset(q[RANK:RANK + 1, :], 1.0).then_inc(ones_set, 1)
                pool.wait_ge(ones_set, after(2))
                with pool.Fori(0, B) as b:
                    ln.inverse_root(pool, b)

            @block.vector
            def _(dve):
                def layer_norm(n, v):
                    dve.wait_ge(x_loaded[v], loads(n, v))
                    ln.statistics(dve, n, x[v][:, :])
                    dve.wait_ge(xT_ps, after(n))
                    ln.normalize(dve, n, x[v][:, :])

                def step(b, u, ahead=True, front=True, middle=True, tail=True):
                    nu = 1 - u
                    if front:
                        dve.wait_ge(xT_ps, after(b + 2))
                        dve.wait_ge(p_done, after(b + 1))
                        dve.tensor_copy(xnT[:, :, :], t_ps[:, 0:D].rearrange("p (t s) -> p t s", s=S)).then_inc(xT_ready, 1)
                    if ahead:
                        layer_norm(b + 2, u)
                    if front:
                        dve.wait_ge(p_done, after(b + 2))
                        dve.wait_ge(h_done, after(b * 2 + 2))
                        dve.tensor_copy(p[0:RANK, :], p_ps[0:RANK, 0:S]).then_inc(p_ready, 1)
                    if tail:
                        dve.wait_ge(out_done, after(b))
                        dve.wait_ge(res_loaded[nu], loads(b - 1, nu))
                        dve.wait_ge(x_stored[nu], stores(b - 1, nu))
                        dve.scalar_tensor_tensor(xo[nu][:, :], o_ps[:, 0:D], k.gates[:, 6:7], res[nu][:, :],
                                                 ALU.mult, ALU.add).then_inc(xo_ready, 1)
                    if middle:
                        dve.wait_ge(q_done, after(b + 1))
                        dve.wait_ge(out_done, after(b))
                        dve.tensor_copy(q[0:RANK, :], q_ps[0:RANK, 0:S]).then_inc(q_ready, 1)

                layer_norm(0, 0)
                in_three_phases(dve, step)

            @block.scalar
            def _(act):
                with act.Fori(0, B) as b:
                    act.wait_ge(table_in, after(b))
                    act.activation(table_pull[:, :], k.eps[:, :], ACT.Gelu_apprx_tanh).then_inc(table_in, 1)
                    for j in range(2):
                        act.wait_ge(h_done, after(b * 2 + (j + 1)))
                        act.wait_ge(q_done, after(b))
                        act.activation(h[:, 4 * j:4 * j + 4, :], h_ps[j][:, :, :], ACT.Gelu_apprx_tanh).then_inc(h_ready, 1)

            @block.tensor
            def _(pe):
                def step(b, u, ahead=True, front=True, middle=True, tail=True):
                    if front:
                        pe.wait_ge(ln.xn_ready, after(b + 2))
                        pe.wait_ge(xT_ready, after(b + 1))
                        for t in range(DT):
                            last = pe.transpose(t_ps[:, 128 * t:128 * t + 128], ln.xn[:, 128 * t:128 * t + 128], k.ident[:, :])
                        last.then_inc(xT_ps, 1)
                    if middle:
                        pe.wait_ge(p_ready, after(b + 1))
                        pe.wait_ge(h_ready, after(b * 2))
                        for j in range(2):
                            for m in range(4):
                                f = 4 * j + m
                                last = pe.matmul(h_ps[j][:, m, :], v1[:, 128 * f:128 * f + 128], p[:, :], start=True, stop=True)
                            last.then_inc(h_done, 1)
                    if front:
                        pe.wait_ge(xT_ready, after(b + 2))
                        pe.wait_ge(p_ready, after(b + 1))
                        for t in range(DT):
                            last = pe.matmul(p_ps[0:RANK, 0:S], u1[:, t, :], xnT[:, t, :], start=(t == 0), stop=(t == DT - 1))
                        last.then_inc(p_done, 1)
                    if tail:
                        pe.wait_ge(q_ready, after(b))
                        pe.wait_ge(xo_ready, after(b - 1))
                        pe.matmul(o_ps[:, 0:D], q[:, :], v2[:, :], start=True, stop=True).then_inc(out_done, 1)
                    if middle:
                        pe.wait_ge(q_ready, after(b))
                        for f in range(FT):
                            if f % 4 == 0:
                                pe.wait_ge(h_ready, after(b * 2 + (f // 4 + 1)))
                            last = pe.matmul(q_ps[0:RANK, 0:S], u2[:, f, :], h[:, f, :], start=(f == 0), stop=(f == FT - 1))
                        last.then_inc(q_done, 1)

                pe.wait_ge(weights.loaded, weights.LOADED)
                pe.wait_ge(ones_set, after(2))
                in_three_phases(pe, step)


HE = 128


NT = E + 2


class MixtureWeights:
    LOADED = 16 * 9

    def __init__(self, k, ctx):
        sb = lambda n, s: ctx.enter_context(k.nc.sbuf_tensor("mix_" + n, s, F32))
        self.ins = k.ins
        self.loaded = k.nc.alloc_semaphore("mix_weights_loaded")
        self.router = sb("w_router", [128, DT, E])
        self.gate, self.up = sb("w_gate", [128, DT, E, HE]), sb("w_up", [128, DT, E, HE])
        self.sgate, self.sup = sb("w_sgate", [128, DT, D]), sb("w_sup", [128, DT, D])
        self.down = sb("w_down", [128, NT, D])

    def load(self, engine):
        w = lambda n: self.ins["L3_ffn_" + n]
        engine.dma_start(self.router[:, :, :], w("router").rearrange("(t p) n -> p t n", p=128)).then_inc(self.loaded, 16)
        for t in range(DT):
            rows = slice(128 * t, 128 * t + 128)
            engine.dma_start(self.gate[:, t, :, :], w("experts_gate")[:, rows, :].rearrange("e p n -> p e n")).then_inc(self.loaded, 16)
            engine.dma_start(self.up[:, t, :, :], w("experts_up")[:, rows, :].rearrange("e p n -> p e n")).then_inc(self.loaded, 16)
        engine.dma_start(self.sgate[:, :, :], w("shared_gate").rearrange("(t p) n -> p t n", p=128)).then_inc(self.loaded, 16)
        engine.dma_start(self.sup[:, :, :], w("shared_up").rearrange("(t p) n -> p t n", p=128)).then_inc(self.loaded, 16)
        engine.dma_start(self.down[:, 0:E, :], w("experts_down").rearrange("e p n -> p e n")).then_inc(self.loaded, 16)
        engine.dma_start(self.down[:, E:NT, :], w("shared_down").rearrange("(t p) n -> p t n", p=128)).then_inc(self.loaded, 16)


def stage_mixture_ffn(k, x_in, x_out, weights):
    nc = k.nc
    with ExitStack() as ctx:
        sb = lambda n, s, t=F32: ctx.enter_context(nc.sbuf_tensor("mix_" + n, s, t))
        ps = lambda n, s, t=F32: ctx.enter_context(nc.psum_tensor("mix_" + n, s, t))
        sem = lambda n: k.semaphore(ctx, "mix_" + n)
        x = [sb(f"x{u}", [128, D]) for u in range(2)]
        xo = [sb(f"xo{u}", [128, D]) for u in range(2)]
        w_router, w_gate, w_up, w_down = weights.router, weights.gate, weights.up, weights.down
        w_sgate, w_sup = weights.sgate, weights.sup
        iota_j, base_e = sb("iota_j", [128, S]), sb("base_e", [128, E])
        ln = LayerNorm(k, ctx, "mix_ln")
        xnT = sb("xnT", [128, DT, S])
        xnT_hi, xnT_lo = sb("xnT_hi", [128, DT, S], F32R), sb("xnT_lo", [128, DT, S], F32R)
        parts = lambda n, s: (sb(f"w_{n}_hi", s, F32R), sb(f"w_{n}_lo", s, F32R))
        gate_parts, up_parts = parts("gate", [128, DT, E, HE]), parts("up", [128, DT, E, HE])
        sgate_parts, sup_parts = parts("sgate", [128, DT, D]), parts("sup", [128, DT, D])
        down_parts = parts("down", [128, NT, D])
        z, top, top_i, top_f = sb("z", [128, E]), sb("top", [128, 8]), sb("top_i", [128, 8], mybir.dt.uint32), sb("top_f", [128, 8])
        zs, ez, total, rtotal = sb("zs", [128, E]), sb("ez", [128, E]), sb("total", [128, 1]), sb("rtotal", [128, 1])
        first, both, coef = sb("first", [128, E]), sb("both", [128, E]), sb("coef", [128, E])
        act_g = sb("act_g", [128, NT * HE])
        hid = sb("hid", [128, NT * HE])
        hT_hi, hT_lo = sb("hT_hi", [128, NT, S], F32R), sb("hT_lo", [128, NT, S], F32R)
        t_ps, o_ps = ps("t_ps", [128, 512]), ps("o_ps", [128, 512])
        g_ps = [ps(f"g_ps{j}", [128, 512]) for j in range(3)]
        u_ps = [ps(f"u_ps{j}", [128, 512]) for j in range(3)]
        table_pull = sb("table_pull", [128, 1])
        iota_in, table_in = sem("iota_in"), sem("table_in")
        in_loaded = [sem(f"in_loaded{u}") for u in range(2)]
        x_stored = [sem(f"x_stored{u}") for u in range(2)]
        consts, xT_ps, xT_ready, xT_lo_ready, logits, rstep, zs_ready, ez_ready, gu_done, act_ready, hid_ready = map(sem, (
            "consts", "xT_ps", "xT_ready", "xT_lo_ready", "logits", "rstep", "zs_ready", "ez_ready", "gu_done", "act_ready", "hid_ready"))
        hT_ps, hT_hi_ready, hT_lo_ready, out_done, xo_ready = map(sem, ("hT_ps", "hT_hi_ready", "hT_lo_ready", "out_done", "xo_ready"))
        w_hi, w_lo, down_hi, down_lo = map(sem, ("w_hi", "w_lo", "down_hi", "down_lo"))
        four = lambda w, j: w[:, :, 4 * j:4 * j + 4, :]
        split = [(four(w, j), (four(p[0], j), four(p[1], j))) for j in range(2) for w, p in ((w_gate, gate_parts), (w_up, up_parts))]
        split += [(w[:, :, :], (p[0][:, :, :], p[1][:, :, :])) for w, p in ((w_sgate, sgate_parts), (w_sup, sup_parts))]
        with nc.Block() as block:

            @block.sync
            def _(sp):
                def load(b, u):
                    sp.dma_start(x[u][:, :], x_in[b]).then_inc(in_loaded[u], 16)

                def store(b, u):
                    sp.wait_ge(xo_ready, after(b + 1))
                    sp.dma_start(x_out[b], xo[u][:, :]).then_inc(x_stored[u], 16)

                load(0, 0)
                load(1, 1)
                sp.dma_start(iota_j[:, :], k.ins["c_iota"]).then_inc(iota_in, 16)
                with sp.Fori(0, B // 2 - 1) as i:
                    for u in range(2):
                        b = i * 2 + u
                        store(b, u)
                        load(b + 2, u)
                for u in range(2):
                    store(B - 2 + u, u)
                for u in range(2):
                    sp.wait_ge(x_stored[u], after(16 * B // 2))

            @block.gpsimd
            def _(pool):
                k.prime(pool)
                pool.memset(base_e[:, :], math.e).then_inc(consts, 1)
                pool.wait_ge(consts, after(1))
                for c in range(0, NT, 2):
                    pool.wait_ge(down_hi, after(c // 2 + 1))
                    pool.tensor_tensor(down_parts[1][:, c:c + 2, :], w_down[:, c:c + 2, :], down_parts[0][:, c:c + 2, :].bitcast(F32),
                                       ALU.subtract).then_inc(down_lo, 1)
                with pool.Fori(0, B) as b:
                    ln.inverse_root(pool, b)
                    pool.wait_ge(xT_ready, after(b + 1))
                    pool.wait_ge(gu_done, after(b * 3))
                    pool.tensor_tensor(xnT_lo[:, :, :], xnT[:, :, :], xnT_hi[:, :, :].bitcast(F32), ALU.subtract).then_inc(xT_lo_ready, 1)
                    pool.wait_ge(zs_ready, after(b + 1))
                    pool.wait_ge(rstep, after(b * RSTEPS))
                    pool.tensor_tensor(ez[:, :], base_e[:, :], zs[:, :], ALU.pow).then_inc(ez_ready, 1)

            @block.vector
            def _(dve):
                def statistics(n, v):
                    dve.wait_ge(in_loaded[v], loads(n, v))
                    ln.statistics(dve, n, x[v][:, :])

                def normalize(n, v):
                    dve.wait_ge(xT_ps, after(n))
                    ln.normalize(dve, n, x[v][:, :])

                def router(n):
                    dve.wait_ge(logits, after(n + 1))
                    step = lambda m: dve.wait_ge(rstep, after(n * RSTEPS + m))
                    dve.tensor_copy(z[:, :], t_ps[:, 256:256 + E]).then_inc(rstep, 1)
                    step(1)
                    dve.memset(ln.pace[:, :], 0.0)
                    dve.max(top[:, :], z[:, :]).then_inc(rstep, 1)
                    step(2)
                    dve.memset(ln.pace[:, :], 0.0)
                    dve.max_index(top_i[:, :], top[:, :], z[:, :]).then_inc(rstep, 1)
                    dve.wait_ge(ez_ready, after(n))
                    dve.tensor_scalar(zs[:, :], z[:, :], top[:, 0:1], None, ALU.subtract).then_inc(zs_ready, 1)
                    step(3)
                    dve.tensor_copy(top_f[:, :], top_i[:, :]).then_inc(rstep, 1)
                    step(4)
                    dve.tensor_scalar(first[:, :], iota_j[:, 0:E], top_f[:, 0:1], None, ALU.is_equal).then_inc(rstep, 1)
                    step(5)
                    dve.scalar_tensor_tensor(both[:, :], iota_j[:, 0:E], top_f[:, 1:2], first[:, :], ALU.is_equal, ALU.add).then_inc(rstep, 1)
                    dve.wait_ge(ez_ready, after(n + 1))
                    dve.tensor_reduce(total[:, :], ez[:, :], AX.X, ALU.add).then_inc(rstep, 1)
                    step(7)
                    dve.reciprocal(rtotal[:, :], total[:, :]).then_inc(rstep, 1)
                    step(8)
                    dve.wait_ge(hid_ready, after(n * 3))
                    dve.scalar_tensor_tensor(coef[:, :], ez[:, :], rtotal[:, :], both[:, :], ALU.mult, ALU.mult).then_inc(rstep, 1)

                def step(b, u, front=True, main=True):
                    nu = 1 - u
                    if not main:
                        statistics(b + 1, nu)
                        normalize(b + 1, nu)
                        router(b + 1)
                        return
                    dve.wait_ge(rstep, after(b * RSTEPS + 9))
                    for j in range(3):
                        dve.wait_ge(act_ready, after(b * 3 + (j + 1)))
                        dve.wait_ge(hT_ps, after(b * 3 + (j - 2)))
                        if j < 2:
                            for e in range(4):
                                cols = slice((4 * j + e) * HE, (4 * j + e) * HE + HE)
                                last = dve.scalar_tensor_tensor(hid[:, cols], act_g[:, cols], coef[:, 4 * j + e:4 * j + e + 1],
                                                                u_ps[j][:, e * HE:e * HE + HE], ALU.mult, ALU.mult)
                        else:
                            last = dve.tensor_tensor(hid[:, E * HE:], act_g[:, E * HE:], u_ps[2][:, 0:D], ALU.mult)
                        last.then_inc(hid_ready, 1)
                        if j == 0 and front:
                            statistics(b + 1, nu)
                        if j == 1 and front:
                            normalize(b + 1, nu)
                    for j in range(3):
                        n = 4 if j < 2 else 2
                        dve.wait_ge(hT_hi_ready, after(b * 3 + (j + 1)))
                        dve.tensor_tensor(hT_lo[:, 4 * j:4 * j + n, :], g_ps[j][:, 0:n * S].rearrange("p (m s) -> p m s", s=S),
                                          hT_hi[:, 4 * j:4 * j + n, :].bitcast(F32), ALU.subtract).then_inc(hT_lo_ready, 1)
                    if front:
                        router(b + 1)
                    dve.wait_ge(out_done, after(b + 1))
                    dve.wait_ge(x_stored[u], stores(b, u))
                    dve.scalar_tensor_tensor(xo[u][:, :], o_ps[:, 0:D], k.gates[:, 7:8], x[u][:, :],
                                             ALU.mult, ALU.add).then_inc(xo_ready, 1)

                for j in range(5):
                    dve.wait_ge(weights.loaded, weights.LOADED)
                    dve.tensor_copy(down_parts[0][:, 2 * j:2 * j + 2, :], w_down[:, 2 * j:2 * j + 2, :]).then_inc(down_hi, 1)
                for n, (w, (hi, lo)) in enumerate(split):
                    dve.wait_ge(w_hi, after(n + 1))
                    dve.tensor_tensor(lo, w, hi.bitcast(F32), ALU.subtract).then_inc(w_lo, 1)
                dve.wait_ge(iota_in, after(16))
                in_two_phases(dve, step)

            @block.scalar
            def _(act):
                def step(b, u, front=True, main=True):
                    if main:
                        act.wait_ge(table_in, after(b))
                        act.activation(table_pull[:, :], k.eps[:, :], ACT.Silu).then_inc(table_in, 1)
                        for j in range(3):
                            act.wait_ge(gu_done, after(b * 3 + (j + 1)))
                            act.wait_ge(hid_ready, after(b * 3))
                            n = 512 if j < 2 else D
                            act.activation(act_g[:, 512 * j:512 * j + n], g_ps[j][:, 0:n], ACT.Silu).then_inc(act_ready, 1)
                    def copy_hidden(j):
                        n = 4 if j < 2 else 2
                        act.wait_ge(hT_ps, after(b * 3 + (j + 1)))
                        act.wait_ge(out_done, after(b))
                        act.activation(hT_hi[:, 4 * j:4 * j + n, :], g_ps[j][:, 0:n * S].rearrange("p (m s) -> p m s", s=S),
                                       ACT.Copy).then_inc(hT_hi_ready, 1)

                    if main:
                        copy_hidden(0)
                        copy_hidden(1)
                    if front:
                        act.wait_ge(xT_ps, after(b + 2))
                        act.wait_ge(gu_done, after(b * 3 + 3))
                        act.activation(xnT_hi[:, :, :], t_ps[:, 0:D].rearrange("p (t s) -> p t s", s=S), ACT.Copy)
                        act.activation(xnT[:, :, :], t_ps[:, 0:D].rearrange("p (t s) -> p t s", s=S), ACT.Copy).then_inc(xT_ready, 1)
                    if main:
                        copy_hidden(2)

                act.wait_ge(weights.loaded, weights.LOADED)
                for w, (hi, lo) in split:
                    act.activation(hi, w, ACT.Copy).then_inc(w_hi, 1)
                in_two_phases(act, step)

            @block.tensor
            def _(pe):
                def step(b, u, front=True, main=True):
                    if main:
                        pe.wait_ge(xT_lo_ready, after(b + 1))
                        pe.wait_ge(hT_lo_ready, after(b * 3))
                        for j in range(3):
                            for out, wp, sp in ((g_ps[j], gate_parts, sgate_parts), (u_ps[j], up_parts, sup_parts)):
                                for t in range(DT):
                                    rhs = [w[:, t, 4 * j:4 * j + 4, :] for w in wp] if j < 2 else [w[:, t, :] for w in sp]
                                    last = split_product(pe, out[:, 0:512] if j < 2 else out[:, 0:D], (xnT_hi[:, t, :], xnT_lo[:, t, :]), rhs,
                                                         t == 0, t == DT - 1)
                            last.then_inc(gu_done, 1)
                    def transpose_hidden(j):
                        pe.wait_ge(hid_ready, after(b * 3 + (j + 1)))
                        for m in range(4 if j < 2 else 2):
                            c = 4 * j + m
                            last = pe.transpose(g_ps[j][:, m * S:m * S + S], hid[:, c * HE:c * HE + HE], k.ident[:, :])
                        last.then_inc(hT_ps, 1)

                    if main:
                        transpose_hidden(0)
                        transpose_hidden(1)
                    if front:
                        pe.wait_ge(ln.xn_ready, after(b + 2))
                        pe.wait_ge(rstep, after(b * RSTEPS + RSTEPS))
                        for t in range(DT):
                            last = pe.transpose(t_ps[:, 128 * t:128 * t + 128], ln.xn[:, 128 * t:128 * t + 128], k.ident[:, :])
                        last.then_inc(xT_ps, 1)
                    if main:
                        transpose_hidden(2)
                    if front:
                        pe.wait_ge(xT_ready, after(b + 2))
                        for t in range(DT):
                            last = pe.matmul(t_ps[:, 256:256 + E], xnT[:, t, :], w_router[:, t, :], start=(t == 0), stop=(t == DT - 1))
                        last.then_inc(logits, 1)
                    if main:
                        pe.wait_ge(xo_ready, after(b))
                        for c in range(NT):
                            if c % 4 == 0:
                                pe.wait_ge(hT_lo_ready, after(b * 3 + (c // 4 + 1)))
                            last = split_product(pe, o_ps[:, 0:D], (hT_hi[:, c, :], hT_lo[:, c, :]), [w[:, c, :] for w in down_parts],
                                                 c == 0, c == NT - 1)
                        last.then_inc(out_done, 1)

                pe.wait_ge(weights.loaded, weights.LOADED)
                pe.wait_ge(w_lo, after(len(split)))
                pe.wait_ge(down_lo, after(NT // 2))
                in_two_phases(pe, step)


RSTEPS = 9


def build(nc, ins, out):
    k = Kernel(nc, ins, out)
    with ExitStack() as ctx:
        sb = lambda n, s, t=F32: ctx.enter_context(nc.sbuf_tensor(n, s, t))
        sem = lambda n: ctx.enter_context(nc.semaphore(n))
        k.ident = sb("ident", [128, 128])
        k.minus_half = sb("minus_half", [128, 1])
        k.eps = sb("eps", [128, 1])
        k.pair_mask = sb("pair_mask", [128, 2])
        k.gates = sb("gates", [128, 8])
        raw_gates = sb("raw_gates", [128, 8])
        setup_in, mh = sem("setup_in"), sem("minus_half_set")
        k.setup_in = setup_in
        with nc.Block() as block:
            @block.sync
            def _(sp):
                sp.dma_start(k.ident[:, :], ins["c_ident"]).then_inc(setup_in, 16)
                sp.dma_start(k.pair_mask[:, :], ins["c_pair_mask"]).then_inc(setup_in, 16)
                sp.dma_start(raw_gates[:, 0:4], ins["g_xattn"].rearrange("(a n) -> a n", a=1).to_broadcast([128, 4])).then_inc(setup_in, 16)
                sp.dma_start(raw_gates[:, 4:8], ins["g_ffn"].rearrange("(a n) -> a n", a=1).to_broadcast([128, 4])).then_inc(setup_in, 16)

            @block.gpsimd
            def _(pool):
                pool.memset(k.minus_half[:, :], -0.5).then_inc(mh, 1)
                pool.memset(k.eps[:, :], LN_EPS).then_inc(mh, 1)

            @block.scalar
            def _(act):
                act.wait_ge(setup_in, 64)
                act.activation(k.gates[:, :], raw_gates[:, :], ACT.Tanh).then_inc(mh, 1)
                act.wait_ge(mh, 3)
        def scratch(name, shape):
            return nc.dram_tensor(name, shape, F32).ap()

        def x_after(n):
            return out if n == LAYERS - 1 else scratch(f"x_after_{n}", (B, S, D))

        x = x_after(0)
        with ExitStack() as switch_ctx:
            switch_weights = SwitchWeights(k, switch_ctx)
            stage_retention(k, ins["x"], x, switch_weights)
            k.clear_semaphores()
            x, x_in = x_after(1), x
            stage_switch_attention(k, x_in, x, switch_weights)
            k.clear_semaphores()
        L2_weights = AttentionWeights(k, ctx, "L2", True)
        x, x_in = x_after(3), x
        dist, costs = scratch("dist", (B, S, S)), scratch("costs", (B, S + 1, S + 1))
        steps, path = scratch("steps", (B, S, S)), scratch("path", (S, B, S))
        stage_distances(k, x_in, dist, L2_weights)
        k.clear_semaphores()
        stage_warp(k, dist, costs, steps, path)
        k.clear_semaphores()
        L3_weights = AttentionWeights(k, ctx, "L3", False)
        low_rank_weights, mixture_weights = LowRankWeights(k, ctx), MixtureWeights(k, ctx)
        stage_align_int8(k, x_in, path, x, (low_rank_weights, L3_weights, mixture_weights))
        k.clear_semaphores()
        x, x_in = x_after(4), x
        bounce = [scratch(f"bounce{u}", ((S * (S + 1)) * H,)) for u in range(2)]
        stage_attention(k, x_in, x, "L2", 2, True, L2_weights, bounce)
        k.clear_semaphores()
        x, x_in = x_after(5), x
        stage_low_rank_ffn(k, x_in, x, low_rank_weights)
        k.clear_semaphores()
        x, x_in = x_after(6), x
        stage_attention(k, x_in, x, "L3", 3, False, L3_weights)
        k.clear_semaphores()
        stage_mixture_ffn(k, x, out, mixture_weights)
        k.clear_semaphores()


def kernel(**inputs):
    import numpy as _np
    import concourse.bacc as _bacc
    from concourse import mybir as _mybir
    from concourse.bass_utils import run_bass_kernel_spmd as _run

    nc = _bacc.Bacc("TRN2", target_bir_lowering=False, num_devices=1)
    arrays = {n: _np.ascontiguousarray(a) for n, a in inputs.items()}
    cT = _np.ascontiguousarray(_np.swapaxes(arrays["ctx_1024"], 1, 2))
    swapped = cT.reshape(B, D // 2, 2, S)[:, :, ::-1, :].reshape(B, D, S)
    arrays["ctxT_pairs"] = _np.ascontiguousarray(_np.stack([cT, swapped], axis=1))
    q_rot, k_rot, decay = retention_tables()
    arrays.update(c_q_rot=q_rot, c_k_rot=k_rot, c_decay=decay, c_ident=_np.eye(128, dtype=_np.float32),
                  c_pair_mask=pair_masks())
    arrays["w_value"] = _np.ascontiguousarray(arrays.pop("L0_ffn_value_experts").transpose(2, 0, 1, 3).reshape(D, E, HK))
    arrays["w_out"] = _np.ascontiguousarray(
        arrays.pop("L0_ffn_output_experts").reshape(E, HK // 128, 128, D).transpose(2, 0, 1, 3))
    arrays["c_causal"] = _np.where(_np.arange(S)[None, :] > _np.arange(S)[:, None], MASKED, 0.0).astype(_np.float32)
    arrays["c_rank"] = _np.broadcast_to(_np.arange(E, 0, -1).astype(_np.float32), (128, MH, E)).copy()
    arrays["c_spread"] = expert_spread()
    arrays["w_int8T"] = _np.ascontiguousarray(arrays.pop("L1_ffn_weight_q").T).view(_np.int32)
    arrays["c_iota"] = _np.broadcast_to(_np.arange(S, dtype=_np.float32), (128, S)).copy()
    arrays["c_sinT"] = sinusoid_reversed_T()
    feed = {f"in_{n}_dram": a for n, a in arrays.items()}
    ins = {n: nc.dram_tensor(f"in_{n}_dram", a.shape, _mybir.dt.from_np(a.dtype), kind="ExternalInput").ap()
           for n, a in arrays.items()}
    out = nc.dram_tensor("out_0_dram", (B, S, D), F32, kind="ExternalOutput").ap()
    build(nc, ins, out)
    r = _run(nc, [feed], core_ids=[0])
    return r.results[0]["out_0_dram"]
```
